# Optimizing a Trainium2 kernel written in Bass

```python
import numpy as np
import jax
import jax.numpy as jnp

def _softmax(x, axis=-1):
    return jax.nn.softmax(x, axis=axis)

def _gelu(x):
    return jax.nn.gelu(x, approximate=True)

def _silu(x):
    return jax.nn.silu(x)

def _sigmoid(x):
    return jax.nn.sigmoid(x)

def _layernorm(x, axis=-1, eps=1e-05):
    m = jnp.mean(x, axis=axis, keepdims=True)
    v = jnp.var(x, axis=axis, keepdims=True)
    return (x - m) / jnp.sqrt(v + eps)

def _scatter_add(tgt, idx, src, axis=0):
    return tgt.at[idx].add(src)

def _segment_sum(src, seg, n):
    return jax.ops.segment_sum(src, seg, n)
kernel_name = 'mk_gnn_preln_d2_gnn_r64_0c8cec'

def setup_inputs(seed: int=0):
    np.random.seed(seed)
    _w = jnp.asarray

    def _rec_inputs():
        import jax
        import jax.numpy as jnp
        _gk = jax.random.key(seed)
        x = -0.0003713 + 1 * jax.random.normal(jax.random.fold_in(_gk, 1), (100000, 128), jnp.float32)
        src = jax.random.randint(jax.random.fold_in(_gk, 2), (25000,), 0, 100000, jnp.int32)
        dst = jnp.minimum((100000 * jax.random.uniform(jax.random.fold_in(_gk, 3), (25000,)) ** 2.0).astype(jnp.int32), 99999)
        _o = jnp.argsort(dst, stable=True)
        src = src[_o]
        dst = dst[_o]
        edge_type_8 = jax.random.randint(jax.random.fold_in(_gk, 12), (25000,), 0, 8, jnp.int32)
        return (x, src, dst, edge_type_8)
    x, src, dst, edge_type_8 = _rec_inputs()

    def _L0_gnn_setup():
        import jax, jax.numpy as jnp
        import numpy as np
        N = 100000
        E = 25000
        IN_DIM = 128
        HEADS = 4
        C = 32
        SLOPE = 0.2
        key = jax.random.key(seed)
        k1, k2, k3, k4, k5 = jax.random.split(key, 5)
        x = jax.random.normal(k1, (N, IN_DIM), dtype=jnp.float32)
        edge_index = jax.random.randint(k2, (2, E), 0, N, dtype=jnp.int32)
        W = jax.random.normal(k3, (IN_DIM, HEADS * C), dtype=jnp.float32) / np.sqrt(IN_DIM)
        att_src = jax.random.normal(k4, (HEADS, C), dtype=jnp.float32) * 0.1
        att_dst = jax.random.normal(k5, (HEADS, C), dtype=jnp.float32) * 0.1
        bias = jnp.zeros((HEADS * C,), dtype=jnp.float32)
        return {'x': x, 'edge_index': edge_index, 'W': W, 'att_src': att_src, 'att_dst': att_dst, 'bias': bias}
    _L0_gnn_all = _L0_gnn_setup()
    _L0_gnn_in = {k: v for k, v in _L0_gnn_all.items() if k in ('W', 'att_src', 'att_dst', 'bias')}
    del _L0_gnn_all

    def _L1_gnn_setup():
        import jax, jax.numpy as jnp
        import numpy as np
        N_NODES = 100000
        N_EDGES = 9375
        HID = 128
        N_ETYPES = 8
        key = jax.random.key(seed)
        ks = jax.random.split(key, 10)
        s = 1.0 / np.sqrt(HID)
        return {'h': jax.random.normal(ks[0], (N_NODES, HID), dtype=jnp.float32), 'edge_index': jax.random.randint(ks[1], (2, N_EDGES), 0, N_NODES, dtype=jnp.int64), 'edge_type': jax.random.randint(ks[2], (N_EDGES,), 0, N_ETYPES, dtype=jnp.int64), 'message_W': jax.random.uniform(ks[3], (N_ETYPES, HID, HID), jnp.float32, -s, s), 'message_b': jax.random.uniform(ks[4], (N_ETYPES, HID), jnp.float32, -s, s), 'gru_w_ih': jax.random.uniform(ks[5], (3 * HID, HID), jnp.float32, -s, s), 'gru_w_hh': jax.random.uniform(ks[6], (3 * HID, HID), jnp.float32, -s, s), 'gru_b_ih': jax.random.uniform(ks[7], (3 * HID,), jnp.float32, -s, s), 'gru_b_hh': jax.random.uniform(ks[8], (3 * HID,), jnp.float32, -s, s)}
    _L1_gnn_all = _L1_gnn_setup()
    _L1_gnn_in = {k: v for k, v in _L1_gnn_all.items() if k in ('message_W', 'message_b', 'gru_w_ih', 'gru_w_hh', 'gru_b_ih', 'gru_b_hh')}
    del _L1_gnn_all
    return {'x': x, 'src': src, 'dst': dst, 'edge_type_8': edge_type_8, 'L0_gnn_W': _L0_gnn_in['W'], 'L0_gnn_att_src': _L0_gnn_in['att_src'], 'L0_gnn_att_dst': _L0_gnn_in['att_dst'], 'L0_gnn_bias': _L0_gnn_in['bias'], 'L1_gnn_message_W': _L1_gnn_in['message_W'], 'L1_gnn_message_b': _L1_gnn_in['message_b'], 'L1_gnn_gru_w_ih': _L1_gnn_in['gru_w_ih'], 'L1_gnn_gru_w_hh': _L1_gnn_in['gru_w_hh'], 'L1_gnn_gru_b_ih': _L1_gnn_in['gru_b_ih'], 'L1_gnn_gru_b_hh': _L1_gnn_in['gru_b_hh']}

def reference(x, src, dst, edge_type_8, L0_gnn_W, L0_gnn_att_src, L0_gnn_att_dst, L0_gnn_bias, L1_gnn_message_W, L1_gnn_message_b, L1_gnn_gru_w_ih, L1_gnn_gru_w_hh, L1_gnn_gru_b_ih, L1_gnn_gru_b_hh):
    import jax
    import jax.numpy as jnp

    def _L0_gnn_ref(x, edge_index, W, att_src, att_dst, bias):
        import jax, jax.numpy as jnp
        import numpy as np
        N = 100000
        E = 25000
        IN_DIM = 128
        HEADS = 4
        C = 32
        SLOPE = 0.2
        loops = jnp.arange(N, dtype=edge_index.dtype)
        ei = jnp.concatenate([edge_index, jnp.stack([loops, loops])], axis=1)
        src, dst = (ei[0], ei[1])
        h = (x @ W).reshape(N, HEADS, C)
        a_src = jnp.einsum('nhc,hc->nh', h, att_src)
        a_dst = jnp.einsum('nhc,hc->nh', h, att_dst)
        e = a_src[src] + a_dst[dst]
        e = jax.nn.leaky_relu(e, SLOPE)
        m = jax.ops.segment_max(e, dst, num_segments=N)
        e = jnp.exp(e - m[dst])
        s = jax.ops.segment_sum(e, dst, num_segments=N)
        alpha = e / (s[dst] + 1e-16)
        msg = h[src] * alpha[:, :, None]
        out = jax.ops.segment_sum(msg, dst, num_segments=N)
        return out.reshape(N, HEADS * C) + bias

    def _L1_gnn_ref(h, edge_index, edge_type, message_W, message_b, gru_w_ih, gru_w_hh, gru_b_ih, gru_b_hh):
        import jax, jax.numpy as jnp
        import numpy as np
        N_NODES = 100000
        N_EDGES = 9375
        HID = 128
        N_ETYPES = 8
        num_nodes = h.shape[0]
        src, dst = (edge_index[0], edge_index[1])
        all_msgs = jnp.einsum('nh,thd->ntd', h, message_W) + message_b
        msg = all_msgs[src, edge_type]
        messages = jax.ops.segment_sum(msg, dst, num_segments=num_nodes)
        gi = messages @ gru_w_ih.T + gru_b_ih
        gh = h @ gru_w_hh.T + gru_b_hh
        i_r, i_z, i_n = jnp.split(gi, 3, axis=-1)
        h_r, h_z, h_n = jnp.split(gh, 3, axis=-1)
        r = jax.nn.sigmoid(i_r + h_r)
        z = jax.nn.sigmoid(i_z + h_z)
        n = jnp.tanh(i_n + r * h_n)
        return (1.0 - z) * n + z * h
    edge_index = jnp.stack([src, dst])
    h = jnp.maximum(_layernorm(x, axis=-1), 0.0)
    x = x + _L0_gnn_ref(h, edge_index, L0_gnn_W, L0_gnn_att_src, L0_gnn_att_dst, L0_gnn_bias)
    h = jnp.maximum(_layernorm(x, axis=-1), 0.0)
    x = x + _L1_gnn_ref(h, edge_index, edge_type_8, L1_gnn_message_W, L1_gnn_message_b, L1_gnn_gru_w_ih, L1_gnn_gru_w_hh, L1_gnn_gru_b_ih, L1_gnn_gru_b_hh)
    return x

_drawn_inputs = setup_inputs


def setup_inputs(seed=0):
    import zlib

    import numpy as np

    out = dict(_drawn_inputs(seed))
    spreads = {'L0_gnn_bias': (0.0, 0.1)}
    factors = {'L0_gnn_att_dst': 7.798,
     'L1_gnn_message_b': 8.0,
     'L1_gnn_gru_b_ih': 3.33,
     'L1_gnn_gru_b_hh': 5.117}
    for name, (base, spread) in spreads.items():
        noise = np.random.default_rng([zlib.crc32(name.encode()), seed]).standard_normal(out[name].shape)
        drawn = base * np.exp(spread * noise) if base else spread * noise
        out[name] = jnp.asarray(drawn.astype(out[name].dtype))
    for name, factor in factors.items():
        out[name] = (out[name] * factor).astype(out[name].dtype)
    return out
```

```python
from contextlib import ExitStack

import concourse.bass as bass
from concourse import mybir

ALU = mybir.AluOpType
ACT = mybir.ActivationFunctionType
F32 = mybir.dt.float32
I32 = mybir.dt.int32
U32 = mybir.dt.uint32

F = 128
ROWS = 125
TILES = 4
CHUNK = ROWS * TILES
HEADS = 4
ETYPES = 8
EPS = 1e-5
SLOPE = 0.2
FAR = 1.0e30
SKIP = 1 << 20


class Step:

    def __init__(self, unroll, turn, lane):
        self.unroll, self.turn, self.lane = unroll, turn, lane
        self.n = turn * unroll + lane

    def known(self):
        return isinstance(self.n, int)

    def has_before(self, depth):
        return not self.known() or self.n >= depth

    def uses(self, depth):
        return self.turn * (self.unroll // depth) + self.lane // depth + 1

    def slot(self, depth):
        return self.lane % depth


def pass_on(eng, passed):
    eng.sem_inc(passed, 1)


def skewed(eng, chunks, unroll, stages, margin=4):
    last_lag = max(lag for lag, _ in stages)
    first = -(-(last_lag + margin) // unroll) * unroll

    def step(turn, lane, known):
        for lag, body in stages:
            if known and not 0 <= turn * unroll + lane - lag < chunks:
                continue
            body(Step(unroll, turn + (lane - lag) // unroll, (lane - lag) % unroll))

    for s in range(first):
        step(s // unroll, s % unroll, True)
    with eng.Fori(first // unroll, chunks // unroll) as turn:
        for lane in range(unroll):
            step(turn, lane, False)
    for s in range(chunks, chunks + last_lag):
        step(s // unroll, s % unroll, True)


def build(nc, x, src, dst, etype, W, att_src, att_dst, bias, msg_W, msg_b, w_ih, w_hh, b_ih, b_hh, out):
    N, E = x.shape[0], src.shape[0]
    NODE_CHUNKS, EDGE_CHUNKS, EDGE_TILES = N // CHUNK, E // CHUNK, E // ROWS
    HALF = EDGE_TILES // 2
    assert N % (4 * CHUNK) == 0 and E % (2 * CHUNK) == 0 and HALF <= 128 and W.shape[0] == F

    x1_table = nc.dram_tensor("x1_table", (N, F), F32).ap()

    with ExitStack() as ctx:
        def sb(name, shape, dt=F32):
            return ctx.enter_context(nc.sbuf_tensor(name, shape, dt))

        def sems(names):
            return [ctx.enter_context(nc.semaphore(n)) for n in names.split()]

        def sem_ring(name, depth):
            return [ctx.enter_context(nc.semaphore(f"{name}{i}")) for i in range(depth)]

        bank = [ctx.enter_context(nc.psum_tensor(f"bank{i}", [128, 512], F32)) for i in range(8)]

        ident = sb("ident", [128, 128])
        W_sb = sb("W_sb", [F, F])
        Wlog_src = sb("Wlog_src", [F, F])
        Wlog_dst = sb("Wlog_dst", [F, F])
        Wlog_self = sb("Wlog_self", [F, F])
        whh_T = sb("whh_T", [F, 3, F])
        wih_T = sb("wih_T", [F, 3, F])
        bih = sb("bih", [F, 3])
        bhh = sb("bhh", [F, 3])
        bsum = sb("bsum", [F, 3])
        bias_row = sb("bias_row", [128, TILES, F])
        bias_col = sb("bias_col", [F, 1])
        msgW_sb = sb("msgW_sb", [F, ETYPES, F])
        msgb_sb = sb("msgb_sb", [ETYPES, F])
        minus_half = sb("minus_half", [128, 2 * TILES])
        type_id = sb("type_id", [ETYPES, 1])
        src_idx = sb("src_idx", [ROWS, EDGE_TILES], U32)
        dst_idx = sb("dst_idx", [ROWS, EDGE_TILES], U32)
        end_idx = sb("end_idx", [ROWS, EDGE_TILES], U32)

        with ExitStack() as sctx:
            def tmp(name, shape, dt=F32):
                return sctx.enter_context(nc.sbuf_tensor(name, shape, dt))
            wt_rows = tmp("wt_rows", [F, 6, F])
            att_col = tmp("att_col", [F, 2])
            head_of = tmp("head_of", [F, F])
            att_blk = tmp("att_blk", [F, 2, F])
            W_T = tmp("W_T", [F, F])
            rows_i = tmp("rows_i", [HALF, 6, ROWS], I32)
            rows_f = tmp("rows_f", [HALF, 6, ROWS])
            not_end = tmp("not_end", [HALF, 2, ROWS])
            (w_landed, e_landed, consts, ident_ready, blk_ready, rowsf_ready, notend_ready, endf_ready, wt_ps,
             wt_sb, log_ps, idx_ps, idx_sb, log_sb, minus1, headmask, attblk) = [sctx.enter_context(nc.semaphore(n)) for n in
             "w_landed e_landed consts ident_ready blk_ready rowsf_ready notend_ready endf_ready wt_ps wt_sb log_ps idx_ps idx_sb log_sb minus1 headmask attblk".split()]
            n_w = 0
            with nc.Block() as block:
                @block.sync
                def _(sp):
                    loads = [(W_sb[:, :], W), (wt_rows[:, 0:3, :], w_ih.rearrange("(g o) k -> o g k", g=3)),
                             (wt_rows[:, 3:6, :], w_hh.rearrange("(g o) k -> o g k", g=3)),
                             (msgW_sb[:, :, :], msg_W.rearrange("t k o -> k t o")), (msgb_sb[:, :], msg_b),
                             (att_col[:, 0:1], att_src.rearrange("h (c a) -> (h c) a", a=1)),
                             (att_col[:, 1:2], att_dst.rearrange("h (c a) -> (h c) a", a=1)),
                             (bih[:, :], b_ih.rearrange("(g p) -> p g", g=3)), (bhh[:, :], b_hh.rearrange("(g p) -> p g", g=3)),
                             (bias_col[:, :], bias.rearrange("(p a) -> p a", a=1))]
                    loads += [(bias_row[:, j, :], bias.partition_broadcast(128)) for j in range(TILES)]
                    nonlocal n_w
                    n_w = 16 * len(loads)
                    for o, i in loads:
                        with nc.allow_non_contiguous_dma(reason="small"):
                            sp.dma_start(o, i).then_inc(w_landed, 16)
                    for k, a in enumerate((src, dst)):
                        for h in range(2):
                            sp.dma_start(rows_i[:, 2 * k + h, :], a[h * HALF * ROWS:(h + 1) * HALF * ROWS]
                                         .rearrange("(t p) -> t p", p=ROWS)).then_inc(e_landed, 16)
                    sp.dma_start(rows_i[:, 4, :], dst[1:HALF * ROWS + 1].rearrange("(t p) -> t p", p=ROWS)).then_inc(e_landed, 16)
                    sp.wait_ge(minus1, 1)
                    sp.dma_start(rows_i[0:HALF - 1, 5, :], dst[HALF * ROWS + 1:E - ROWS + 1]
                                 .rearrange("(t p) -> t p", p=ROWS)).then_inc(e_landed, 16)
                    sp.dma_start(rows_i[HALF - 1:HALF, 5, 0:ROWS - 1], dst[E - ROWS + 1:E]
                                 .rearrange("(a p) -> a p", a=1)).then_inc(e_landed, 16)
                    sp.wait_ge(w_landed, n_w)
                    sp.wait_ge(e_landed, 16 * 7)
                n_w = 16 * 14

                @block.gpsimd
                def _(pool):
                    pool.memset(ident[:, :], 0.0).then_inc(consts, 1)
                    pool.memset(minus_half[:, :], -0.5).then_inc(consts, 1)
                    pool.memset(head_of[:, :], 1.0).then_inc(consts, 1)
                    pool.iota(type_id[:, :], [[0, 1]], base=0, channel_multiplier=1, allow_small_or_imprecise_dtypes=True).then_inc(consts, 1)
                    pool.wait_ge(consts, 4)
                    pool.affine_select(out=ident[:, :], in_=ident[:, :], compare_op=ALU.not_equal, fill=1.0, base=0,
                                       pattern=[[-1, 128]], channel_multiplier=1).then_inc(ident_ready, 1)
                    C = F // HEADS
                    v = head_of[:, :].rearrange("p (h c) -> p h c", h=HEADS)
                    pool.affine_select(out=v, in_=v, compare_op=ALU.is_ge, fill=0.0, base=0,
                                       pattern=[[-C, HEADS], [0, C]], channel_multiplier=1).then_inc(headmask, 1)
                    pool.wait_ge(headmask, 1)
                    pool.affine_select(out=v, in_=v, compare_op=ALU.is_ge, fill=0.0, base=C - 1,
                                       pattern=[[C, HEADS], [0, C]], channel_multiplier=-1).then_inc(headmask, 1)

                @block.vector
                def _(dve):
                    dve.memset(rows_i[:, 5, :], -1).then_inc(minus1, 1)
                    dve.wait_ge(w_landed, n_w)
                    dve.wait_ge(headmask, 2)
                    for k in range(2):
                        dve.tensor_scalar(att_blk[:, k, :], head_of[:, :], att_col[:, k:k + 1], None, ALU.mult).then_inc(attblk, 1)
                    dve.tensor_tensor(bsum[:, :], bih[:, :], bhh[:, :], ALU.add)
                    dve.wait_ge(e_landed, 16 * 7)
                    dve.tensor_copy(rows_f[:, :, :], rows_i[:, :, :]).then_inc(rowsf_ready, 1)
                    dve.wait_ge(rowsf_ready, 1)
                    dve.tensor_tensor(not_end[:, :, :], rows_f[:, 2:4, :], rows_f[:, 4:6, :], ALU.is_equal).then_inc(notend_ready, 1)
                    dve.wait_ge(notend_ready, 1)
                    dve.scalar_tensor_tensor(rows_f[:, 4:6, :], not_end[:, :, :], float(SKIP), rows_f[:, 2:4, :],
                                             ALU.mult, ALU.add).then_inc(endf_ready, 1)
                    dve.wait_ge(wt_ps, 1)
                    dve.tensor_copy(wih_T[:, :, :], bank[0][:, 0:384].rearrange("p (g k) -> p g k", g=3)).then_inc(wt_sb, 1)
                    dve.tensor_copy(whh_T[:, :, :], bank[1][:, 0:384].rearrange("p (g k) -> p g k", g=3)).then_inc(wt_sb, 1)
                    dve.tensor_copy(W_T[:, :], bank[2][:, 0:F]).then_inc(wt_sb, 1)
                    dve.wait_ge(log_ps, 1)
                    dve.tensor_copy(Wlog_src[:, :], bank[3][:, 0:F]).then_inc(log_sb, 1)
                    dve.tensor_copy(Wlog_dst[:, :], bank[3][:, F:2 * F]).then_inc(log_sb, 1)
                    dve.wait_ge(log_sb, 2)
                    dve.tensor_tensor(Wlog_self[:, :], Wlog_src[:, :], Wlog_dst[:, :], ALU.add)
                    dve.wait_ge(idx_ps, 1)
                    for k, o in enumerate((src_idx, dst_idx, end_idx)):
                        for h in range(2):
                            dve.tensor_copy(o[:, h * HALF:(h + 1) * HALF], bank[4 + k][0:ROWS, h * HALF:(h + 1) * HALF])

                @block.tensor
                def _(pe):
                    pe.wait_ge(ident_ready, 1)
                    pe.wait_ge(w_landed, n_w)
                    for g in range(3):
                        pe.transpose(bank[0][:, g * F:(g + 1) * F], wt_rows[:, g, :], ident[:, :])
                        pe.transpose(bank[1][:, g * F:(g + 1) * F], wt_rows[:, 3 + g, :], ident[:, :])
                    pe.transpose(bank[2][:, 0:F], W_sb[:, :], ident[:, :]).then_inc(wt_ps, 1)
                    pe.wait_ge(wt_sb, 3)
                    pe.wait_ge(attblk, 2)
                    for k in range(2):
                        mm = pe.matmul(bank[3][:, k * F:(k + 1) * F], W_T[:, :], att_blk[:, k, :], start=True, stop=True)
                    mm.then_inc(log_ps, 1)
                    pe.wait_ge(rowsf_ready, 1)
                    pe.wait_ge(endf_ready, 1)
                    for k in range(3):
                        for h in range(2):
                            mm = pe.transpose(bank[4 + k][0:ROWS, h * HALF:(h + 1) * HALF], rows_f[:, 2 * k + h, :],
                                              ident[0:HALF, 0:HALF])
                    mm.then_inc(idx_ps, 1)

        with ExitStack() as dctx:
            def ring(name, depth, shape, dt=F32):
                return [dctx.enter_context(nc.sbuf_tensor(f"{name}{i}", shape, dt)) for i in range(depth)]

            def sem(name):
                return dctx.enter_context(nc.semaphore("n_" + name))
            U = 4
            node_major = [ROWS, TILES, F]
            X = ring("nX", 4, node_major)
            XB = ring("nXB", 2, node_major)
            HN = ring("nHN", 2, node_major)
            HT = ring("nHT", 2, [F, CHUNK])
            X1 = ring("nX1", 4, node_major)
            H1N = ring("nH1N", 2, node_major)
            H1T = ring("nH1T", 4, [F, CHUNK])
            ST = ring("nST", 2, [ROWS, 2, TILES, 6])
            MV = ring("nMV", 2, [ROWS, 2, TILES, 2])
            VE = ring("nVE", 2, [ROWS, 2, TILES])
            RS = ring("nRS", 2, [ROWS, 2, TILES])
            R = ring("nR", 2, [F, CHUNK])
            Z = ring("nZ", 2, [F, CHUNK])
            NT = ring("nNT", 2, [F, CHUNK])
            NN = ring("nNN", 2, [F, CHUNK])
            D = ring("nD", 2, [F, CHUNK])
            D2 = ring("nD2", 2, [F, CHUNK])
            D3 = ring("nD3", 2, [F, CHUNK])
            OUT = ring("nOUT", 2, node_major)
            x_landed = [sem(f"x_landed{i}") for i in range(4)]
            x1_stored = [sem(f"x1_stored{i}") for i in range(4)]
            out_stored = [sem(f"out_stored{i}") for i in range(2)]
            bn0, stat0, ve0, rstd0, norm0, tr0, relu0, xb = map(sem, "bn0 stat0 ve0 rstd0 norm0 tr0 relu0 xb".split())
            wmm, x1, bn1, stat1, ve1, rstd1, norm1, tr1, relu1 = map(sem, "wmm x1 bn1 stat1 ve1 rstd1 norm1 tr1 relu1".split())
            gates, r_ready, z_ready, nt, nn, diff, zdiff, summed, trd, outsum = map(
                sem, "gates r_ready z_ready nt nn diff zdiff summed trd outsum".split())
            sp_passed, pool_passed, dve_passed = map(sem, "sp_passed pool_passed dve_passed".split())
            P_T0, P_W, P_T1, P_R, P_Z, P_N, P_O = bank[0:7]

            def rows_of(table, c):
                return table[bass.ds(c.n * CHUNK, CHUNK), :].rearrange("(p j) f -> p j f", j=TILES)

            with nc.Block() as block:
                @block.sync
                def _(sp):
                    def load(c):
                        if c.has_before(4):
                            sp.wait_ge(norm0, c.n - 3)
                            sp.wait_ge(xb, c.n - 3)
                            pass_on(sp, sp_passed)
                        sp.dma_start(X[c.slot(4)][:, :, :], rows_of(x, c)).then_inc(x_landed[c.slot(4)], 16)

                    def store_x1(c):
                        sp.wait_ge(x1, c.n + 1)
                        pass_on(sp, sp_passed)
                        sp.dma_start(rows_of(x1_table, c), X1[c.slot(4)][:, :, :]).then_inc(x1_stored[c.slot(4)], 16)

                    def store_out(c):
                        sp.wait_ge(outsum, c.n + 1)
                        pass_on(sp, sp_passed)
                        sp.dma_start(rows_of(out, c), OUT[c.slot(2)][:, :, :]).then_inc(out_stored[c.slot(2)], 16)

                    skewed(sp, NODE_CHUNKS, U, [(0, load), (3, store_x1), (6, store_out)])
                    for s in x1_stored:
                        sp.wait_ge(s, 16 * (NODE_CHUNKS // 4))
                    for s in out_stored:
                        sp.wait_ge(s, 16 * (NODE_CHUNKS // 2))

                @block.gpsimd
                def _(pool):
                    def rstd(c, k, stat, ve, done, norm):
                        b = c.slot(2)
                        pool.wait_ge(stat, c.n + 1)
                        if c.has_before(2):
                            pool.wait_ge(norm, c.n - 1)
                        pass_on(pool, pool_passed)
                        pool.tensor_scalar(VE[b][:, k, :], MV[b][:, k, :, 1], EPS, None, ALU.add).then_inc(ve, 1)
                        pool.wait_ge(ve, c.n + 1)
                        pool.tensor_tensor(RS[b][:, k, :], VE[b][:, k, :], minus_half[0:ROWS, 0:TILES], ALU.pow).then_inc(done, 1)

                    def rstd_0(c):
                        rstd(c, 0, stat0, ve0, rstd0, norm0)

                    def rstd_1(c):
                        rstd(c, 1, stat1, ve1, rstd1, norm1)

                    def add_bias(c):
                        pool.wait_ge(x_landed[c.slot(4)], 16 * c.uses(4))
                        if c.has_before(2):
                            pool.wait_ge(x1, c.n - 1)
                        pool.tensor_tensor(XB[c.slot(2)][:, :, :], X[c.slot(4)][:, :, :], bias_row[0:ROWS, :, :], ALU.add).then_inc(xb, 1)

                    def h_minus_n(c):
                        pool.wait_ge(nn, c.n + 1)
                        if c.has_before(2):
                            pool.wait_ge(zdiff, c.n - 1)
                        pool.tensor_tensor(D[c.slot(2)][:, :], H1T[c.slot(4)][:, :], NN[c.slot(2)][:, :], ALU.subtract).then_inc(diff, 1)

                    skewed(pool, NODE_CHUNKS, U, [(0, rstd_0), (1, rstd_1), (0, add_bias), (2, h_minus_n)])

                @block.vector
                def _(dve):
                    def stats(c, k, S, bn, stat):
                        b = c.slot(2)
                        for j in range(TILES):
                            i = dve.bn_stats(ST[b][:, k, j, :], S[:, j, :])
                        i.then_inc(bn, 1)
                        dve.wait_ge(bn, c.n + 1)
                        pass_on(dve, dve_passed)
                        for j in range(TILES):
                            i = dve.bn_aggr(MV[b][:, k, j, :], ST[b][:, k, j, :])
                        i.then_inc(stat, 1)

                    def normalise(c, k, S, O, rstd, done):
                        b = c.slot(2)
                        dve.wait_ge(rstd, c.n + 1)
                        for j in range(TILES):
                            i = dve.tensor_scalar(O[:, j, :], S[:, j, :], MV[b][:, k, j, 0:1], RS[b][:, k, j:j + 1],
                                                  ALU.subtract, ALU.mult)
                        i.then_inc(done, 1)

                    def stats_0(c):
                        dve.wait_ge(x_landed[c.slot(4)], 16 * c.uses(4))
                        if c.has_before(2):
                            dve.wait_ge(rstd0, c.n - 1)
                        stats(c, 0, X[c.slot(4)], bn0, stat0)

                    def norm_0(c):
                        if c.has_before(2):
                            dve.wait_ge(tr0, c.n - 1)
                        normalise(c, 0, X[c.slot(4)], HN[c.slot(2)], rstd0, norm0)

                    def add_x1(c):
                        dve.wait_ge(wmm, c.n + 1)
                        dve.wait_ge(xb, c.n + 1)
                        if c.has_before(4):
                            dve.wait_ge(x1_stored[c.slot(4)], 16 * (c.uses(4) - 1))
                            dve.wait_ge(outsum, c.n - 3)
                        dve.tensor_tensor(X1[c.slot(4)][:, :, :], P_W[0:ROWS, :].rearrange("p (j f) -> p j f", j=TILES),
                                          XB[c.slot(2)][:, :, :], ALU.add).then_inc(x1, 1)
                        dve.wait_ge(x1, c.n + 1)
                        if c.has_before(2):
                            dve.wait_ge(rstd1, c.n - 1)
                        stats(c, 1, X1[c.slot(4)], bn1, stat1)

                    def norm_1(c):
                        if c.has_before(2):
                            dve.wait_ge(tr1, c.n - 1)
                        normalise(c, 1, X1[c.slot(4)], H1N[c.slot(2)], rstd1, norm1)

                    def reset_gate(c):
                        dve.wait_ge(gates, c.n + 1)
                        dve.wait_ge(r_ready, c.n + 1)
                        if c.has_before(2):
                            dve.wait_ge(nn, c.n - 1)
                        dve.scalar_tensor_tensor(NT[c.slot(2)][:, :], P_N[:, 0:CHUNK], bhh[:, 2:3], R[c.slot(2)][:, :],
                                                 ALU.add, ALU.mult).then_inc(nt, 1)

                    def mix(c):
                        b = c.slot(2)
                        dve.wait_ge(diff, c.n + 1)
                        dve.wait_ge(z_ready, c.n + 1)
                        dve.tensor_tensor(D2[b][:, :], Z[b][:, :], D[b][:, :], ALU.mult).then_inc(zdiff, 1)
                        dve.wait_ge(zdiff, c.n + 1)
                        if c.has_before(2):
                            dve.wait_ge(trd, c.n - 1)
                        dve.tensor_tensor(D3[b][:, :], D2[b][:, :], NN[b][:, :], ALU.add).then_inc(summed, 1)

                    def add_out(c):
                        b = c.slot(2)
                        dve.wait_ge(trd, c.n + 1)
                        if c.has_before(2):
                            dve.wait_ge(out_stored[b], 16 * (c.uses(2) - 1))
                        dve.tensor_tensor(OUT[b][:, :, :], P_O[0:ROWS, :].rearrange("p (j f) -> p j f", j=TILES),
                                          X1[c.slot(4)][:, :, :], ALU.add).then_inc(outsum, 1)

                    skewed(dve, NODE_CHUNKS, U, [(0, stats_0), (1, add_x1), (0, norm_0), (2, reset_gate), (1, norm_1),
                                                 (4, add_out), (3, mix)])

                @block.scalar
                def _(act):
                    def relu_0(c):
                        act.wait_ge(tr0, c.n + 1)
                        if c.has_before(2):
                            act.wait_ge(wmm, c.n - 1)
                        act.activation(HT[c.slot(2)][:, :], P_T0[:, 0:CHUNK], ACT.Relu).then_inc(relu0, 1)

                    def relu_1(c):
                        act.wait_ge(tr1, c.n + 1)
                        if c.has_before(4):
                            act.wait_ge(gates, c.n - 3)
                            act.wait_ge(diff, c.n - 3)
                        act.activation(H1T[c.slot(4)][:, :], P_T1[:, 0:CHUNK], ACT.Relu).then_inc(relu1, 1)

                    def sigmoids(c):
                        b = c.slot(2)
                        act.wait_ge(gates, c.n + 1)
                        if c.has_before(2):
                            act.wait_ge(nt, c.n - 1)
                            act.wait_ge(zdiff, c.n - 1)
                        act.activation(R[b][:, :], P_R[:, 0:CHUNK], ACT.Sigmoid, bias=bsum[:, 0:1]).then_inc(r_ready, 1)
                        act.activation(Z[b][:, :], P_Z[:, 0:CHUNK], ACT.Sigmoid, bias=bsum[:, 1:2]).then_inc(z_ready, 1)

                    def tanh(c):
                        b = c.slot(2)
                        act.wait_ge(nt, c.n + 1)
                        if c.has_before(2):
                            act.wait_ge(summed, c.n - 1)
                            act.wait_ge(diff, c.n - 1)
                        act.activation(NN[b][:, :], NT[b][:, :], ACT.Tanh, bias=bih[:, 2:3]).then_inc(nn, 1)

                    skewed(act, NODE_CHUNKS, U, [(2, sigmoids), (0, relu_0), (2, tanh), (1, relu_1)])

                @block.tensor
                def _(pe):
                    def transposes(c, bank_, S, done):
                        for j in range(TILES):
                            i = pe.transpose(bank_[:, j * ROWS:(j + 1) * ROWS], S[:, j, :], ident[0:ROWS, 0:ROWS])
                        i.then_inc(done, 1)

                    def tr_0(c):
                        pe.wait_ge(norm0, c.n + 1)
                        if c.has_before(1):
                            pe.wait_ge(relu0, c.n)
                        transposes(c, P_T0, HN[c.slot(2)], tr0)

                    def w_mm(c):
                        pe.wait_ge(relu0, c.n + 1)
                        if c.has_before(1):
                            pe.wait_ge(x1, c.n)
                        for j in range(TILES):
                            i = pe.matmul(P_W[0:ROWS, j * F:(j + 1) * F], HT[c.slot(2)][:, j * ROWS:(j + 1) * ROWS], W_sb[:, :],
                                          start=True, stop=True)
                        i.then_inc(wmm, 1)

                    def tr_1(c):
                        pe.wait_ge(norm1, c.n + 1)
                        if c.has_before(1):
                            pe.wait_ge(relu1, c.n)
                        transposes(c, P_T1, H1N[c.slot(2)], tr1)

                    def gate_mm(c):
                        pe.wait_ge(relu1, c.n + 1)
                        if c.has_before(1):
                            pe.wait_ge(r_ready, c.n)
                            pe.wait_ge(z_ready, c.n)
                            pe.wait_ge(nt, c.n)
                        for g, P in enumerate((P_R, P_Z, P_N)):
                            i = pe.matmul(P[:, 0:CHUNK], whh_T[:, g, :], H1T[c.slot(4)][:, :], start=True, stop=True)
                        i.then_inc(gates, 1)

                    def tr_out(c):
                        pe.wait_ge(summed, c.n + 1)
                        if c.has_before(1):
                            pe.wait_ge(outsum, c.n)
                        for j in range(TILES):
                            i = pe.transpose(P_O[0:ROWS, j * F:(j + 1) * F], D3[c.slot(2)][:, j * ROWS:(j + 1) * ROWS], ident[:, :])
                        i.then_inc(trd, 1)

                    skewed(pe, NODE_CHUNKS, U, [(1, w_mm), (2, gate_mm), (0, tr_0), (3, tr_out), (1, tr_1)])

        def edge_front(nc, ctx, pre, table):
            class S:
                pass
            s = S()

            def ring(name, depth, shape, dt=F32):
                return [ctx.enter_context(nc.sbuf_tensor(f"{pre}{name}{i}", shape, dt)) for i in range(depth)]

            def sem(name):
                return ctx.enter_context(nc.semaphore(f"{pre}_{name}"))
            s.ring, s.sem, s.table = ring, sem, table
            s.XG = ring("XG", 2, [ROWS, 2 * TILES, F])
            s.HN = ring("HN", 2, [ROWS, 2 * TILES, F])
            s.H = ring("H", 2, [F, 2, CHUNK])
            s.ST = ring("ST", 2, [ROWS, 2 * TILES, 6])
            s.MV = ring("MV", 2, [ROWS, 2 * TILES, 2])
            s.VE = ring("VE", 2, [ROWS, 2 * TILES])
            s.RS = ring("RS", 2, [ROWS, 2 * TILES])
            s.IX = ring("IX", 2, [ROWS, 3 * TILES], U32)
            s.NODE = ring("NODE", 2, [128, CHUNK + 1], I32)
            s.gathered = [sem(f"gathered{i}") for i in range(2)]
            s.node_landed = [sem(f"node_landed{i}") for i in range(2)]
            s.scattered = [sem(f"scattered{i}") for i in range(2)]
            s.sp_passed, s.pool_passed, s.dve_passed = sem("sp_passed"), sem("pool_passed"), sem("dve_passed")
            s.idx = sem("idx")
            s.bn, s.stat = sem("bn"), sem("stat")
            s.ve, s.rstd = sem("ve"), sem("rstd")
            s.norm, s.tr, s.relu = sem("norm"), sem("tr"), sem("relu")
            s.first = sem("first")
            s.keep = sem("keep")
            s.x_out = sem("x_out")
            return s

        def load_nodes(sp, s, c):
            b = c.slot(2)
            if c.has_before(2):
                sp.wait_ge(s.keep, c.n - 1)
                pass_on(sp, s.sp_passed)
            if c.known() and c.n == 0:
                sp.dma_start(s.NODE[b][:, 1:CHUNK + 1], dst[0:CHUNK].partition_broadcast(128)).then_inc(s.node_landed[b], 16)
            else:
                sp.dma_start(s.NODE[b][:, :], dst[bass.ds(c.n * CHUNK - 1, CHUNK + 1)].partition_broadcast(128)).then_inc(s.node_landed[b], 16)

        def gather(pool, s, c):
            b = c.slot(2)
            pool.wait_ge(s.idx, c.n + 1)
            if c.has_before(2):
                pool.wait_ge(s.norm, c.n - 1)
                pool.wait_ge(s.x_out, c.n - 1)
            pass_on(pool, s.pool_passed)
            for j in range(2 * TILES):
                pool.indirect_dma_start(out=s.XG[b][:, j, :], out_offset=None, in_=s.table,
                                        in_offset=bass.IndirectOffsetOnAxis(ap=s.IX[b][:, j:j + 1], axis=0),
                                        bounds_check=N - 1, oob_is_err=False).then_inc(s.gathered[b], 16)

        def edge_rstd(pool, s, c):
            b = c.slot(2)
            pool.wait_ge(s.stat, c.n + 1)
            if c.has_before(2):
                pool.wait_ge(s.norm, c.n - 1)
            pass_on(pool, s.pool_passed)
            pool.tensor_scalar(s.VE[b][:, :], s.MV[b][:, :, 1], EPS, None, ALU.add).then_inc(s.ve, 1)
            pool.wait_ge(s.ve, c.n + 1)
            pool.tensor_tensor(s.RS[b][:, :], s.VE[b][:, :], minus_half[0:ROWS, :], ALU.pow).then_inc(s.rstd, 1)

        def scatter(pool, s, c, OUT, to):
            b = c.slot(2)
            pool.wait_ge(s.x_out, c.n + 1)
            pass_on(pool, s.pool_passed)
            for j in range(TILES):
                pool.indirect_dma_start(out=to, out_offset=bass.IndirectOffsetOnAxis(ap=s.IX[b][:, 2 * TILES + j:2 * TILES + j + 1], axis=0),
                                        in_=OUT[b][:, j, :], in_offset=None,
                                        bounds_check=N - 1, oob_is_err=False).then_inc(s.scattered[b], 16)

        def edge_index(dve, s, c):
            b = c.slot(2)
            if c.has_before(2):
                dve.wait_ge(s.scattered[b], 16 * TILES * (c.uses(2) - 1))
            for k, t in enumerate((src_idx, dst_idx, end_idx)):
                i = dve.tensor_copy(s.IX[b][:, k * TILES:(k + 1) * TILES], t[:, bass.ds(c.n * TILES, TILES)])
            i.then_inc(s.idx, 1)

        def edge_stats(dve, s, c):
            b = c.slot(2)
            dve.wait_ge(s.gathered[b], 16 * 2 * TILES * c.uses(2))
            if c.has_before(2):
                dve.wait_ge(s.rstd, c.n - 1)
            for j in range(2 * TILES):
                i = dve.bn_stats(s.ST[b][:, j, :], s.XG[b][:, j, :])
            i.then_inc(s.bn, 1)
            dve.wait_ge(s.bn, c.n + 1)
            pass_on(dve, s.dve_passed)
            for j in range(2 * TILES):
                i = dve.bn_aggr(s.MV[b][:, j, :], s.ST[b][:, j, :])
            i.then_inc(s.stat, 1)

        def edge_norm(dve, s, c):
            b = c.slot(2)
            dve.wait_ge(s.rstd, c.n + 1)
            if c.has_before(2):
                dve.wait_ge(s.tr, c.n - 1)
            for j in range(2 * TILES):
                i = dve.tensor_scalar(s.HN[b][:, j, :], s.XG[b][:, j, :], s.MV[b][:, j, 0:1], s.RS[b][:, j:j + 1],
                                      ALU.subtract, ALU.mult)
            i.then_inc(s.norm, 1)

        def edge_transposes(pe, s, c, banks):
            b = c.slot(2)
            pe.wait_ge(s.norm, c.n + 1)
            if c.has_before(1):
                pe.wait_ge(s.relu, c.n)
            for j in range(2 * TILES):
                i = pe.transpose(banks[j // TILES][:, j % TILES * ROWS:(j % TILES + 1) * ROWS], s.HN[b][:, j, :], ident[0:ROWS, 0:ROWS])
            i.then_inc(s.tr, 1)

        def edge_relu(act, s, c, banks, used):
            b = c.slot(2)
            act.wait_ge(s.tr, c.n + 1)
            if c.has_before(2):
                act.wait_ge(used, c.n - 1)
            for k in range(2):
                i = act.activation(s.H[b][:, k, :], banks[k][:, 0:CHUNK], ACT.Relu)
            i.then_inc(s.relu, 1)

        def edge_keep(dve, s, c, KEEP, used):
            b = c.slot(2)
            dve.wait_ge(s.node_landed[b], 16 * c.uses(2))
            if c.known() and c.n == 0:
                dve.memset(s.NODE[b][:, 0:1], -1).then_inc(s.first, 1)
                dve.wait_ge(s.first, 1)
            dve.tensor_tensor(KEEP[:, :], s.NODE[b][:, 1:CHUNK + 1], s.NODE[b][:, 0:CHUNK], ALU.is_equal).then_inc(s.keep, 1)

        def wait_scatters(pool, s):
            for m in s.scattered:
                pool.wait_ge(m, 16 * TILES * (EDGE_CHUNKS // 2))

        with ExitStack() as gctx:
            s = edge_front(nc, gctx, "g", x)
            ring, sem = s.ring, s.sem
            KEEP = ring("KEEP", 1, [F, CHUNK])[0]
            CUT = ring("CUT", 1, [F, CHUNK])[0]
            LR = ring("LR", 2, [F, 2, CHUNK])
            L = ring("L", 2, [F, 2, CHUNK])
            SELF = ring("SELF", 1, [F, CHUNK])[0]
            TOP = ring("TOP", 1, [F, CHUNK])[0]
            MX = ring("MX", 1, [F, CHUNK + 1])[0]
            ARG = ring("ARG", 2, [F, 3, CHUNK])
            EX = ring("EX", 2, [F, 3, CHUNK])
            PV = ring("PV", 1, [F, CHUNK])[0]
            QV = ring("QV", 1, [F, CHUNK])[0]
            UV = ring("UV", 1, [F, CHUNK])[0]
            PQ = ring("PQ", 1, [F, CHUNK])[0]
            ACC = ring("ACC", 2, [F, CHUNK])
            DEN = ring("DEN", 2, [F, CHUNK])
            RD = ring("RD", 1, [F, CHUNK])[0]
            O = ring("O", 1, [F, CHUNK])[0]
            OB = ring("OB", 1, [F, CHUNK])[0]
            OUT = ring("OUT", 2, [ROWS, TILES, F])
            values, logits, cut, selfl, top, mx, arg, ex, carry, pv, uv, acc, den, rd, o, ob, tro, pq, cut_d, sums, leaky = map(
                sem, "values logits cut selfl top mx arg ex carry pv uv acc den rd o ob tro pq cut_d sums leaky".split())
            P_S, P_D, P_VS, P_VD, P_E, P_SELF, P_O = bank[0:7]
            with nc.Block() as block:
                @block.sync
                def _(sp):
                    skewed(sp, EDGE_CHUNKS, 2, [(0, lambda c: load_nodes(sp, s, c))])

                @block.gpsimd
                def _(pool):
                    skewed(pool, EDGE_CHUNKS, 2, [(0, lambda c: gather(pool, s, c)), (0, lambda c: edge_rstd(pool, s, c)),
                                                  (1, lambda c: scatter(pool, s, c, OUT, x1_table))])
                    wait_scatters(pool, s)

                @block.tensor
                def _(pe):
                    def project(c):
                        b = c.slot(2)
                        pe.wait_ge(s.relu, c.n + 1)
                        if c.has_before(1):
                            pe.wait_ge(logits, 2 * c.n)
                        pe.matmul(P_E[:, 0:CHUNK], Wlog_src[:, :], s.H[b][:, 0, :], start=True, stop=False)
                        pe.matmul(P_E[:, 0:CHUNK], Wlog_dst[:, :], s.H[b][:, 1, :], start=False, stop=True)
                        pe.matmul(P_SELF[:, 0:CHUNK], Wlog_self[:, :], s.H[b][:, 1, :], start=True, stop=True)
                        if c.has_before(1):
                            pe.wait_ge(uv, c.n)
                        pe.matmul(P_VS[:, 0:CHUNK], W_sb[:, :], s.H[b][:, 0, :], start=True, stop=True)
                        pe.matmul(P_VD[:, 0:CHUNK], W_sb[:, :], s.H[b][:, 1, :], start=True, stop=True).then_inc(values, 1)

                    def tr_out(c):
                        pe.wait_ge(ob, c.n + 1)
                        if c.has_before(1):
                            pe.wait_ge(s.x_out, c.n)
                        for j in range(TILES):
                            i = pe.transpose(P_O[0:ROWS, j * F:(j + 1) * F], OB[:, j * ROWS:(j + 1) * ROWS], ident[:, :])
                        i.then_inc(tro, 1)

                    skewed(pe, EDGE_CHUNKS, 2, [(0, lambda c: edge_transposes(pe, s, c, (P_S, P_D))), (1, tr_out), (0, project)])

                @block.scalar
                def _(act):
                    def raw_logits(c):
                        b = c.slot(2)
                        act.wait_ge(values, c.n + 1)
                        if c.has_before(2):
                            act.wait_ge(leaky, c.n - 1)
                        act.activation(LR[b][:, 0, :], P_E[:, 0:CHUNK], ACT.Copy).then_inc(logits, 1)
                        act.activation(LR[b][:, 1, :], P_SELF[:, 0:CHUNK], ACT.Copy).then_inc(logits, 1)

                    def exps(c):
                        b = c.slot(2)
                        act.wait_ge(arg, 3 * (c.n + 1))
                        if c.has_before(2):
                            act.wait_ge(sums, c.n - 1)
                        act.activation(EX[b][:, :, :], ARG[b][:, :, :], ACT.Exp).then_inc(ex, 1)

                    def add_bias(c):
                        act.wait_ge(o, c.n + 1)
                        if c.has_before(1):
                            act.wait_ge(tro, c.n)
                        act.activation(OB[:, :], O[:, :], ACT.Identity, bias=bias_col[:, 0:1]).then_inc(ob, 1)

                    skewed(act, EDGE_CHUNKS, 2, [(1, exps), (1, add_bias), (0, lambda c: edge_relu(act, s, c, (P_S, P_D), values)),
                                                 (0, raw_logits)])

                @block.vector
                def _(dve):
                    def softmax(c):
                        b = c.slot(2)
                        edge_keep(dve, s, c, KEEP, None)
                        dve.wait_ge(s.keep, c.n + 1)
                        dve.tensor_scalar(CUT[:, :], KEEP[:, :], 1.0, FAR, ALU.subtract, ALU.mult).then_inc(cut, 1)
                        dve.wait_ge(logits, 2 * (c.n + 1))
                        dve.scalar_tensor_tensor(L[b][:, :, :], LR[b][:, :, :], SLOPE, LR[b][:, :, :], ALU.mult, ALU.max).then_inc(leaky, 1)
                        dve.wait_ge(leaky, c.n + 1)
                        dve.scalar_tensor_tensor(SELF[:, :], KEEP[:, :], -FAR, L[b][:, 1, :], ALU.mult, ALU.add).then_inc(selfl, 1)
                        dve.wait_ge(selfl, c.n + 1)
                        dve.tensor_tensor(TOP[:, :], L[b][:, 0, :], SELF[:, :], ALU.max).then_inc(top, 1)
                        dve.wait_ge(top, c.n + 1)
                        dve.wait_ge(cut, c.n + 1)
                        if c.known() and c.n == 0:
                            dve.memset(MX[:, 0:1], 0.0).then_inc(carry, 1)
                        else:
                            dve.tensor_copy(MX[:, 0:1], MX[:, CHUNK:CHUNK + 1]).then_inc(carry, 1)
                        dve.wait_ge(carry, c.n + 1)
                        dve.tensor_tensor_scan(MX[:, 1:CHUNK + 1], CUT[:, :], TOP[:, :], MX[:, 0:1], ALU.add, ALU.max).then_inc(mx, 1)
                        dve.wait_ge(mx, c.n + 1)
                        if c.has_before(2):
                            dve.wait_ge(ex, c.n - 1)
                        dve.tensor_tensor(ARG[b][:, 0, :], L[b][:, 0, :], MX[:, 1:CHUNK + 1], ALU.subtract).then_inc(arg, 1)
                        dve.tensor_tensor(ARG[b][:, 1, :], SELF[:, :], MX[:, 1:CHUNK + 1], ALU.subtract).then_inc(arg, 1)
                        dve.tensor_tensor(CUT[:, :], CUT[:, :], MX[:, 0:CHUNK], ALU.add).then_inc(cut_d, 1)
                        dve.wait_ge(cut_d, c.n + 1)
                        dve.tensor_tensor(ARG[b][:, 2, :], CUT[:, :], MX[:, 1:CHUNK + 1], ALU.subtract).then_inc(arg, 1)

                    def combine(c):
                        b = c.slot(2)
                        p = 1 - b
                        dve.wait_ge(ex, c.n + 1)
                        dve.tensor_tensor(PQ[:, :], EX[b][:, 0, :], EX[b][:, 1, :], ALU.add).then_inc(pq, 1)
                        dve.wait_ge(values, c.n + 1)
                        dve.tensor_tensor(PV[:, :], P_VS[:, 0:CHUNK], EX[b][:, 0, :], ALU.mult).then_inc(pv, 1)
                        dve.tensor_tensor(QV[:, :], P_VD[:, 0:CHUNK], EX[b][:, 1, :], ALU.mult).then_inc(pv, 1)
                        dve.wait_ge(pq, c.n + 1)
                        if c.has_before(1):
                            dve.wait_ge(den, c.n)
                            dve.wait_ge(acc, c.n)
                        first = c.known() and c.n == 0
                        dve.tensor_tensor_scan(DEN[b][:, :], EX[b][:, 2, :], PQ[:, :], 0.0 if first else DEN[p][:, CHUNK - 1:CHUNK],
                                               ALU.mult, ALU.add).then_inc(den, 1)
                        dve.wait_ge(pv, 2 * (c.n + 1))
                        dve.tensor_tensor(UV[:, :], PV[:, :], QV[:, :], ALU.add).then_inc(uv, 1)
                        dve.wait_ge(uv, c.n + 1)
                        dve.tensor_tensor_scan(ACC[b][:, :], EX[b][:, 2, :], UV[:, :], 0.0 if first else ACC[p][:, CHUNK - 1:CHUNK],
                                               ALU.mult, ALU.add).then_inc(acc, 1)
                        dve.wait_ge(den, c.n + 1)
                        dve.tensor_scalar(PQ[:, :], DEN[b][:, :], 1e-16, None, ALU.add).then_inc(sums, 1)
                        dve.wait_ge(sums, c.n + 1)
                        dve.reciprocal(RD[:, :], PQ[:, :]).then_inc(rd, 1)
                        dve.wait_ge(rd, c.n + 1)
                        dve.wait_ge(acc, c.n + 1)
                        if c.has_before(1):
                            dve.wait_ge(ob, c.n)
                        dve.tensor_tensor(O[:, :], ACC[b][:, :], RD[:, :], ALU.mult).then_inc(o, 1)

                    def add_rows(c):
                        b = c.slot(2)
                        dve.wait_ge(tro, c.n + 1)
                        if c.has_before(2):
                            dve.wait_ge(s.scattered[b], 16 * TILES * (c.uses(2) - 1))
                        dve.tensor_tensor(OUT[b][:, :, :], P_O[0:ROWS, :].rearrange("p (j f) -> p j f", j=TILES),
                                          s.XG[b][:, TILES:2 * TILES, :], ALU.add).then_inc(s.x_out, 1)

                    skewed(dve, EDGE_CHUNKS, 2, [(0, lambda c: edge_index(dve, s, c)), (0, lambda c: edge_stats(dve, s, c)),
                                                 (1, combine), (0, lambda c: edge_norm(dve, s, c)), (1, add_rows), (0, softmax)])

        with ExitStack() as mctx:
            s = edge_front(nc, mctx, "m", x1_table)
            ring, sem = s.ring, s.sem
            KEEP = ring("KEEP", 1, [F, CHUNK])[0]
            TYPE = ring("TYPE", 2, [128, CHUNK], I32)
            HOT = ring("HOT", 1, [ETYPES, CHUNK])[0]
            HM = ring("HM", 4, [F, CHUNK])
            MS = ring("MS", 2, [F, CHUNK])
            R = ring("R", 1, [F, CHUNK])[0]
            Z = ring("Z", 1, [F, CHUNK])[0]
            NT = ring("NT", 1, [F, CHUNK])[0]
            NT2 = ring("NT2", 1, [F, CHUNK])[0]
            NN = ring("NN", 1, [F, CHUNK])[0]
            D = ring("D", 1, [F, CHUNK])[0]
            D2 = ring("D2", 1, [F, CHUNK])[0]
            D3 = ring("D3", 1, [F, CHUNK])[0]
            OUT = ring("OUT", 2, [ROWS, TILES, F])
            type_landed = [sem(f"type_landed{i}") for i in range(2)]
            masked, hot, msg_used, msg, msum, gates, r_ready, z_ready, nt, nt2, nn, diff, zdiff, summed, tro = map(
                sem, "masked hot msg_used msg msum gates r_ready z_ready nt nt2 nn diff zdiff summed tro".split())
            P_S, P_D, P_M, P_R, P_Z, P_NI, P_NH, P_O = bank
            with nc.Block() as block:
                @block.sync
                def _(sp):
                    def load_types(c):
                        b = c.slot(2)
                        if c.has_before(2):
                            sp.wait_ge(masked, ETYPES * (c.n - 1))
                            sp.wait_ge(hot, c.n - 1)
                            pass_on(sp, s.sp_passed)
                        sp.dma_start(TYPE[b][:, :], etype[bass.ds(c.n * CHUNK, CHUNK)].partition_broadcast(128)).then_inc(type_landed[b], 16)
                    skewed(sp, EDGE_CHUNKS, 2, [(0, lambda c: load_nodes(sp, s, c)), (0, load_types)])

                @block.gpsimd
                def _(pool):
                    skewed(pool, EDGE_CHUNKS, 2, [(0, lambda c: gather(pool, s, c)), (0, lambda c: edge_rstd(pool, s, c)),
                                                  (1, lambda c: scatter(pool, s, c, OUT, out))])
                    wait_scatters(pool, s)

                @block.tensor
                def _(pe):
                    def messages(c):
                        if c.has_before(1):
                            pe.wait_ge(msum, c.n)
                        for t in range(ETYPES):
                            pe.wait_ge(masked, ETYPES * c.n + t + 1)
                            pe.matmul(P_M[:, 0:CHUNK], msgW_sb[:, t, :], HM[t % 4][:, :], start=(t == 0), stop=False).then_inc(msg_used, 1)
                        pe.wait_ge(hot, c.n + 1)
                        pe.matmul(P_M[:, 0:CHUNK], msgb_sb[:, :], HOT[:, :], start=False, stop=True).then_inc(msg, 1)

                    def gate_mm(c):
                        b = c.slot(2)
                        if c.has_before(1):
                            pe.wait_ge(r_ready, c.n)
                            pe.wait_ge(z_ready, c.n)
                            pe.wait_ge(nt, c.n)
                            pe.wait_ge(nt2, c.n)
                        pe.wait_ge(s.relu, c.n + 1)
                        for g, P in enumerate((P_R, P_Z)):
                            pe.matmul(P[:, 0:CHUNK], whh_T[:, g, :], s.H[b][:, 1, :], start=True, stop=False)
                        pe.matmul(P_NH[:, 0:CHUNK], whh_T[:, 2, :], s.H[b][:, 1, :], start=True, stop=True)
                        pe.wait_ge(msum, c.n + 1)
                        for g, P in enumerate((P_R, P_Z)):
                            pe.matmul(P[:, 0:CHUNK], wih_T[:, g, :], MS[b][:, :], start=False, stop=True)
                        pe.matmul(P_NI[:, 0:CHUNK], wih_T[:, 2, :], MS[b][:, :], start=True, stop=True).then_inc(gates, 1)

                    def tr_out(c):
                        pe.wait_ge(summed, c.n + 1)
                        if c.has_before(1):
                            pe.wait_ge(s.x_out, c.n)
                        for j in range(TILES):
                            i = pe.transpose(P_O[0:ROWS, j * F:(j + 1) * F], D3[:, j * ROWS:(j + 1) * ROWS], ident[:, :])
                        i.then_inc(tro, 1)

                    skewed(pe, EDGE_CHUNKS, 2, [(0, lambda c: edge_transposes(pe, s, c, (P_S, P_D))), (1, tr_out), (0, messages), (0, gate_mm)])

                @block.scalar
                def _(act):
                    def sigmoids(c):
                        act.wait_ge(gates, c.n + 1)
                        if c.has_before(1):
                            act.wait_ge(nt, c.n)
                            act.wait_ge(zdiff, c.n)
                        act.activation(R[:, :], P_R[:, 0:CHUNK], ACT.Sigmoid, bias=bsum[:, 0:1]).then_inc(r_ready, 1)
                        act.activation(Z[:, :], P_Z[:, 0:CHUNK], ACT.Sigmoid, bias=bsum[:, 1:2]).then_inc(z_ready, 1)

                    def tanh(c):
                        act.wait_ge(nt2, c.n + 1)
                        if c.has_before(1):
                            act.wait_ge(summed, c.n)
                        act.activation(NN[:, :], NT2[:, :], ACT.Tanh, bias=bih[:, 2:3]).then_inc(nn, 1)

                    skewed(act, EDGE_CHUNKS, 2, [(1, sigmoids), (1, tanh), (0, lambda c: edge_relu(act, s, c, (P_S, P_D), diff))])

                @block.vector
                def _(dve):
                    def mask(c):
                        b = c.slot(2)
                        edge_keep(dve, s, c, KEEP, None)
                        dve.wait_ge(type_landed[b], 16 * c.uses(2))
                        if c.has_before(1):
                            dve.wait_ge(msg, c.n)
                        dve.tensor_scalar(HOT[:, :], TYPE[b][0:ETYPES, :], type_id[:, 0:1], None, ALU.is_equal).then_inc(hot, 1)
                        dve.wait_ge(s.relu, c.n + 1)
                        for t in range(ETYPES):
                            if t >= 4 or c.has_before(1):
                                dve.wait_ge(msg_used, ETYPES * c.n + t - 3)
                            dve.scalar_tensor_tensor(HM[t % 4][:, :], TYPE[b][:, :], float(t), s.H[b][:, 0, :],
                                                     ALU.is_equal, ALU.mult).then_inc(masked, 1)

                    def total(c):
                        b = c.slot(2)
                        dve.wait_ge(msg, c.n + 1)
                        dve.wait_ge(s.keep, c.n + 1)
                        if c.has_before(1):
                            dve.wait_ge(msum, c.n)
                        if c.has_before(2):
                            dve.wait_ge(gates, c.n - 1)
                        first = c.known() and c.n == 0
                        dve.tensor_tensor_scan(MS[b][:, :], KEEP[:, :], P_M[:, 0:CHUNK], 0.0 if first else MS[1 - b][:, CHUNK - 1:CHUNK],
                                               ALU.mult, ALU.add).then_inc(msum, 1)

                    def candidate(c):
                        dve.wait_ge(gates, c.n + 1)
                        dve.wait_ge(r_ready, c.n + 1)
                        dve.scalar_tensor_tensor(NT[:, :], P_NH[:, 0:CHUNK], bhh[:, 2:3], R[:, :], ALU.add, ALU.mult).then_inc(nt, 1)
                        dve.wait_ge(nt, c.n + 1)
                        if c.has_before(1):
                            dve.wait_ge(nn, c.n)
                        dve.tensor_tensor(NT2[:, :], P_NI[:, 0:CHUNK], NT[:, :], ALU.add).then_inc(nt2, 1)

                    def mix(c):
                        b = c.slot(2)
                        dve.wait_ge(nn, c.n + 1)
                        dve.tensor_tensor(D[:, :], s.H[b][:, 1, :], NN[:, :], ALU.subtract).then_inc(diff, 1)
                        dve.wait_ge(diff, c.n + 1)
                        dve.wait_ge(z_ready, c.n + 1)
                        dve.tensor_tensor(D2[:, :], Z[:, :], D[:, :], ALU.mult).then_inc(zdiff, 1)
                        dve.wait_ge(zdiff, c.n + 1)
                        if c.has_before(1):
                            dve.wait_ge(tro, c.n)
                        dve.tensor_tensor(D3[:, :], D2[:, :], NN[:, :], ALU.add).then_inc(summed, 1)

                    def add_rows(c):
                        b = c.slot(2)
                        dve.wait_ge(tro, c.n + 1)
                        if c.has_before(2):
                            dve.wait_ge(s.scattered[b], 16 * TILES * (c.uses(2) - 1))
                        dve.tensor_tensor(OUT[b][:, :, :], P_O[0:ROWS, :].rearrange("p (j f) -> p j f", j=TILES),
                                          s.XG[b][:, TILES:2 * TILES, :], ALU.add).then_inc(s.x_out, 1)

                    skewed(dve, EDGE_CHUNKS, 2, [(0, lambda c: edge_index(dve, s, c)), (1, candidate), (0, lambda c: edge_stats(dve, s, c)),
                                                 (1, mix), (0, lambda c: edge_norm(dve, s, c)), (1, add_rows), (0, mask), (0, total)])


_INS = ['x', 'src', 'dst', 'edge_type_8', 'L0_gnn_W', 'L0_gnn_att_src', 'L0_gnn_att_dst', 'L0_gnn_bias',
        'L1_gnn_message_W', 'L1_gnn_message_b', 'L1_gnn_gru_w_ih', 'L1_gnn_gru_w_hh', 'L1_gnn_gru_b_ih', 'L1_gnn_gru_b_hh']


def kernel(**inputs):
    import numpy as _np
    import concourse.bacc as _bacc
    from concourse import mybir as _mybir
    from concourse.bass_utils import run_bass_kernel_spmd as _run

    nc = _bacc.Bacc("TRN2", target_bir_lowering=False, num_devices=1)
    arrays, args = {}, []
    for name in _INS:
        a = _np.ascontiguousarray(inputs[name])
        arrays[f"in_{name}"] = a
        args.append(nc.dram_tensor(f"in_{name}", a.shape, _mybir.dt.from_np(a.dtype), kind="ExternalInput").ap())
    args.append(nc.dram_tensor("out_0", inputs['x'].shape, _mybir.dt.float32, kind="ExternalOutput").ap())
    build(nc, *args)
    r = _run(nc, [arrays], core_ids=[0])
    return r.results[0]["out_0"]
```

```python
from contextlib import ExitStack

import concourse.bass as bass
from concourse import mybir

ALU = mybir.AluOpType
ACT = mybir.ActivationFunctionType
F32 = mybir.dt.float32
I32 = mybir.dt.int32
U32 = mybir.dt.uint32

F = 128
ROWS = 125
TILES = 4
CHUNK = ROWS * TILES
HEADS = 4
ETYPES = 8
EPS = 1e-5
SLOPE = 0.2
FAR = 1.0e30
SKIP = 1 << 20


class Step:

    def __init__(self, unroll, turn, lane):
        self.unroll, self.turn, self.lane = unroll, turn, lane
        self.n = turn * unroll + lane

    def known(self):
        return isinstance(self.n, int)

    def has_before(self, depth):
        return not self.known() or self.n >= depth

    def uses(self, depth):
        return self.turn * (self.unroll // depth) + self.lane // depth + 1

    def slot(self, depth):
        return self.lane % depth


def pass_on(eng, passed):
    eng.sem_inc(passed, 1)


def skewed(eng, chunks, unroll, stages):
    stages = [(st[0], st[1], st[2] if len(st) > 2 else 0) for st in stages]
    last_lag = max(lag + more for lag, _, more in stages)
    first = -(-(last_lag + unroll) // unroll)
    last = chunks // unroll

    def step(turn, lane, known):
        for lag, body, more in stages:
            if known and not 0 <= turn * unroll + lane - lag < chunks + more:
                continue
            body(Step(unroll, turn + (lane - lag) // unroll, (lane - lag) % unroll))

    for s in range(first * unroll):
        step(s // unroll, s % unroll, True)
    with eng.Fori(first, last) as turn:
        for lane in range(unroll):
            step(turn, lane, False)
    for s in range(last * unroll, chunks + last_lag):
        step(s // unroll, s % unroll, True)


def fills(chunks, depth, slot):
    return (chunks - slot + depth - 1) // depth


def build(nc, x, src, dst, etype, W, att_src, att_dst, bias, msg_W, msg_b, w_ih, w_hh, b_ih, b_hh, out):
    N, E = x.shape[0], src.shape[0]
    NODE_CHUNKS, EDGE_CHUNKS, EDGE_TILES = N // CHUNK, E // CHUNK, E // ROWS
    HALF = EDGE_TILES // 2
    assert N % (4 * CHUNK) == 0 and E % (2 * CHUNK) == 0 and HALF <= 128 and W.shape[0] == F

    x1_table = nc.dram_tensor("x1_table", (N, F), F32).ap()
    x1_edges = nc.dram_tensor("x1_edges", (E, F), F32).ap()

    with ExitStack() as ctx:
        def sb(name, shape, dt=F32):
            return ctx.enter_context(nc.sbuf_tensor(name, shape, dt))

        phase_sems = []

        def new_sem(name):
            phase_sems.append(nc.alloc_semaphore(name=name))
            return phase_sems[-1]

        def end_phase():
            nc.clear_and_free_semaphores(phase_sems)
            phase_sems.clear()
            nc.all_engine_barrier()

        bank = [ctx.enter_context(nc.psum_tensor(f"bank{i}", [128, 512], F32)) for i in range(8)]

        ident = sb("ident", [128, 128])
        W_sb = sb("W_sb", [F, F])
        Wlog_src = sb("Wlog_src", [F, F])
        Wlog_dst = sb("Wlog_dst", [F, F])
        Wlog_self = sb("Wlog_self", [F, F])
        whh_T = sb("whh_T", [F, 3, F])
        wih_T = sb("wih_T", [F, 3, F])
        bih = sb("bih", [F, 3])
        bhh = sb("bhh", [F, 3])
        bsum = sb("bsum", [F, 3])
        first_row = sb("first_row", [128, ROWS])
        head_sel = sb("head_sel", [F, HEADS])
        bias_row = sb("bias_row", [128, TILES, F])
        bias_col = sb("bias_col", [F, 1])
        msgW_sb = sb("msgW_sb", [F, ETYPES, F])
        msgb_sb = sb("msgb_sb", [ETYPES, F])
        minus_half = sb("minus_half", [128, 2 * TILES])
        type_id = sb("type_id", [ETYPES, 1])
        src_idx = sb("src_idx", [ROWS, EDGE_TILES], U32)
        dst_idx = sb("dst_idx", [ROWS, EDGE_TILES], U32)
        end_idx = sb("end_idx", [ROWS, EDGE_TILES], U32)

        with ExitStack() as sctx:
            def tmp(name, shape, dt=F32):
                return sctx.enter_context(nc.sbuf_tensor(name, shape, dt))
            wt_rows = tmp("wt_rows", [F, 6, F])
            att_col = tmp("att_col", [F, 2])
            head_of = tmp("head_of", [F, F])
            att_blk = tmp("att_blk", [F, 2, F])
            W_T = tmp("W_T", [F, F])
            rows_i = tmp("rows_i", [HALF, 6, ROWS], I32)
            rows_f = tmp("rows_f", [HALF, 6, ROWS])
            not_end = tmp("not_end", [HALF, 2, ROWS])
            (w_landed, e_landed, consts, ident_ready, blk_ready, rowsf_ready, notend_ready, endf_ready, wt_ps,
             wt_sb, log_ps, idx_ps, idx_sb, log_sb, minus1, headmask, attblk) = [new_sem((n)) for n in
             "w_landed e_landed consts ident_ready blk_ready rowsf_ready notend_ready endf_ready wt_ps wt_sb log_ps idx_ps idx_sb log_sb minus1 headmask attblk".split()]
            n_w = 0
            with nc.Block() as block:
                @block.sync
                def _(sp):
                    loads = [(W_sb[:, :], W), (wt_rows[:, 0:3, :], w_ih.rearrange("(g o) k -> o g k", g=3)),
                             (wt_rows[:, 3:6, :], w_hh.rearrange("(g o) k -> o g k", g=3)),
                             (msgW_sb[:, :, :], msg_W.rearrange("t k o -> k t o")), (msgb_sb[:, :], msg_b),
                             (att_col[:, 0:1], att_src.rearrange("h (c a) -> (h c) a", a=1)),
                             (att_col[:, 1:2], att_dst.rearrange("h (c a) -> (h c) a", a=1)),
                             (bih[:, :], b_ih.rearrange("(g p) -> p g", g=3)), (bhh[:, :], b_hh.rearrange("(g p) -> p g", g=3)),
                             (bias_col[:, :], bias.rearrange("(p a) -> p a", a=1))]
                    loads += [(bias_row[:, j, :], bias.partition_broadcast(128)) for j in range(TILES)]
                    nonlocal n_w
                    n_w = 16 * len(loads)
                    for o, i in loads:
                        with nc.allow_non_contiguous_dma(reason="small"):
                            sp.dma_start(o, i).then_inc(w_landed, 16)
                    for k, a in enumerate((src, dst)):
                        for h in range(2):
                            sp.dma_start(rows_i[:, 2 * k + h, :], a[h * HALF * ROWS:(h + 1) * HALF * ROWS]
                                         .rearrange("(t p) -> t p", p=ROWS)).then_inc(e_landed, 16)
                    sp.dma_start(rows_i[:, 4, :], dst[1:HALF * ROWS + 1].rearrange("(t p) -> t p", p=ROWS)).then_inc(e_landed, 16)
                    sp.wait_ge(minus1, 1)
                    sp.dma_start(rows_i[0:HALF - 1, 5, :], dst[HALF * ROWS + 1:E - ROWS + 1]
                                 .rearrange("(t p) -> t p", p=ROWS)).then_inc(e_landed, 16)
                    sp.dma_start(rows_i[HALF - 1:HALF, 5, 0:ROWS - 1], dst[E - ROWS + 1:E]
                                 .rearrange("(a p) -> a p", a=1)).then_inc(e_landed, 16)
                    sp.wait_ge(w_landed, n_w)
                    sp.wait_ge(e_landed, 16 * 7)
                n_w = 16 * 14

                @block.gpsimd
                def _(pool):
                    pool.memset(ident[:, :], 0.0).then_inc(consts, 1)
                    pool.memset(minus_half[:, :], -0.5).then_inc(consts, 1)
                    pool.memset(head_of[:, :], 1.0).then_inc(consts, 1)
                    pool.memset(first_row[:, :], 0.0).then_inc(consts, 1)
                    pool.memset(head_sel[:, :], 0.0).then_inc(consts, 1)
                    pool.iota(type_id[:, :], [[0, 1]], base=0, channel_multiplier=1, allow_small_or_imprecise_dtypes=True).then_inc(consts, 1)
                    pool.wait_ge(consts, 6)
                    pool.affine_select(out=ident[:, :], in_=ident[:, :], compare_op=ALU.not_equal, fill=1.0, base=0,
                                       pattern=[[-1, 128]], channel_multiplier=1).then_inc(ident_ready, 1)
                    pool.affine_select(out=first_row[:, :], in_=first_row[:, :], compare_op=ALU.not_equal, fill=1.0, base=0,
                                       pattern=[[0, ROWS]], channel_multiplier=1)
                    pool.affine_select(out=head_sel[:, :], in_=head_sel[:, :], compare_op=ALU.not_equal, fill=1.0, base=0,
                                       pattern=[[-(F // HEADS), HEADS]], channel_multiplier=1)
                    C = F // HEADS
                    v = head_of[:, :].rearrange("p (h c) -> p h c", h=HEADS)
                    pool.affine_select(out=v, in_=v, compare_op=ALU.is_ge, fill=0.0, base=0,
                                       pattern=[[-C, HEADS], [0, C]], channel_multiplier=1).then_inc(headmask, 1)
                    pool.wait_ge(headmask, 1)
                    pool.affine_select(out=v, in_=v, compare_op=ALU.is_ge, fill=0.0, base=C - 1,
                                       pattern=[[C, HEADS], [0, C]], channel_multiplier=-1).then_inc(headmask, 1)

                @block.vector
                def _(dve):
                    dve.memset(rows_i[:, 5, :], -1).then_inc(minus1, 1)
                    dve.wait_ge(w_landed, n_w)
                    dve.wait_ge(headmask, 2)
                    for k in range(2):
                        dve.tensor_scalar(att_blk[:, k, :], head_of[:, :], att_col[:, k:k + 1], None, ALU.mult).then_inc(attblk, 1)
                    dve.tensor_tensor(bsum[:, :], bih[:, :], bhh[:, :], ALU.add)
                    dve.wait_ge(e_landed, 16 * 7)
                    dve.tensor_copy(rows_f[:, :, :], rows_i[:, :, :]).then_inc(rowsf_ready, 1)
                    dve.wait_ge(rowsf_ready, 1)
                    dve.tensor_tensor(not_end[:, :, :], rows_f[:, 2:4, :], rows_f[:, 4:6, :], ALU.is_equal).then_inc(notend_ready, 1)
                    dve.wait_ge(notend_ready, 1)
                    dve.scalar_tensor_tensor(rows_f[:, 4:6, :], not_end[:, :, :], float(SKIP), rows_f[:, 2:4, :],
                                             ALU.mult, ALU.add).then_inc(endf_ready, 1)
                    dve.wait_ge(wt_ps, 1)
                    dve.tensor_copy(wih_T[:, :, :], bank[0][:, 0:384].rearrange("p (g k) -> p g k", g=3)).then_inc(wt_sb, 1)
                    dve.tensor_copy(whh_T[:, :, :], bank[1][:, 0:384].rearrange("p (g k) -> p g k", g=3)).then_inc(wt_sb, 1)
                    dve.tensor_copy(W_T[:, :], bank[2][:, 0:F]).then_inc(wt_sb, 1)
                    dve.wait_ge(log_ps, 1)
                    dve.tensor_copy(Wlog_src[:, :], bank[3][:, 0:F]).then_inc(log_sb, 1)
                    dve.tensor_copy(Wlog_dst[:, :], bank[3][:, F:2 * F]).then_inc(log_sb, 1)
                    dve.wait_ge(log_sb, 2)
                    dve.tensor_tensor(Wlog_self[:, :], Wlog_src[:, :], Wlog_dst[:, :], ALU.add)
                    dve.wait_ge(idx_ps, 1)
                    for k, o in enumerate((src_idx, dst_idx, end_idx)):
                        for h in range(2):
                            dve.tensor_copy(o[:, h * HALF:(h + 1) * HALF], bank[4 + k][0:ROWS, h * HALF:(h + 1) * HALF])

                @block.tensor
                def _(pe):
                    pe.wait_ge(ident_ready, 1)
                    pe.wait_ge(w_landed, n_w)
                    for g in range(3):
                        pe.transpose(bank[0][:, g * F:(g + 1) * F], wt_rows[:, g, :], ident[:, :])
                        pe.transpose(bank[1][:, g * F:(g + 1) * F], wt_rows[:, 3 + g, :], ident[:, :])
                    pe.transpose(bank[2][:, 0:F], W_sb[:, :], ident[:, :]).then_inc(wt_ps, 1)
                    pe.wait_ge(wt_sb, 3)
                    pe.wait_ge(attblk, 2)
                    for k in range(2):
                        mm = pe.matmul(bank[3][:, k * F:(k + 1) * F], W_T[:, :], att_blk[:, k, :], start=True, stop=True)
                    mm.then_inc(log_ps, 1)
                    pe.wait_ge(rowsf_ready, 1)
                    pe.wait_ge(endf_ready, 1)
                    for k in range(3):
                        for h in range(2):
                            mm = pe.transpose(bank[4 + k][0:ROWS, h * HALF:(h + 1) * HALF], rows_f[:, 2 * k + h, :],
                                              ident[0:HALF, 0:HALF])
                    mm.then_inc(idx_ps, 1)

        end_phase()

        with ExitStack() as dctx:
            def ring(name, depth, shape, dt=F32):
                return [dctx.enter_context(nc.sbuf_tensor(f"{name}{i}", shape, dt)) for i in range(depth)]

            def sem(name):
                return new_sem(("n_" + name))
            U = 8
            node_major = [ROWS, TILES, F]
            X = ring("nX", 4, node_major)
            HN = ring("nHN", 2, node_major)
            HT = ring("nHT", 2, [F, CHUNK])
            X1 = ring("nX1", 8, node_major)
            H1N = ring("nH1N", 2, node_major)
            H1T = ring("nH1T", 4, [F, CHUNK])
            ST = ring("nST", 2, [ROWS, 2, TILES, 6])
            MV = ring("nMV", 2, [ROWS, 2, TILES, 2])
            VE = ring("nVE", 2, [ROWS, 2, TILES])
            RS = ring("nRS", 2, [ROWS, 2, TILES])
            NB = ring("nNB", 2, [ROWS, TILES])
            R = ring("nR", 2, [F, CHUNK])
            Z = ring("nZ", 2, [F, CHUNK])
            NT = ring("nNT", 2, [F, CHUNK])
            NN = ring("nNN", 2, [F, CHUNK])
            D = ring("nD", 2, [F, CHUNK])
            D2 = ring("nD2", 2, [F, CHUNK])
            D3 = ring("nD3", 2, [F, CHUNK])
            OUT = ring("nOUT", 2, node_major)
            x_landed = [sem(f"x_landed{i}") for i in range(4)]
            x1_stored = [sem(f"x1_stored{i}") for i in range(8)]
            out_stored = [sem(f"out_stored{i}") for i in range(2)]
            bn0, stat0, ve, rstd, nb, norm0, tr0, relu0 = map(sem, "bn0 stat0 ve rstd nb norm0 tr0 relu0".split())
            wmm, x1, bn1, stat1, norm1, tr1, relu1 = map(sem, "wmm x1 bn1 stat1 norm1 tr1 relu1".split())
            gates, r_ready, z_ready, nt, nn, diff, zdiff, summed, trd, outsum = map(
                sem, "gates r_ready z_ready nt nn diff zdiff summed trd outsum".split())
            sp_passed, pool_passed, dve_passed, filled = map(sem, "sp_passed pool_passed dve_passed filled".split())
            P_T0, P_W, P_T1, P_R, P_Z, P_N, P_O = bank[0:7]

            def rows_of(table, c):
                return table[bass.ds(c.n * CHUNK, CHUNK), :].rearrange("(p j) f -> p j f", j=TILES)

            with nc.Block() as block:
                @block.sync
                def _(sp):
                    def load(c):
                        if c.has_before(4):
                            sp.wait_ge(norm0, c.n - 3)
                            sp.wait_ge(wmm, c.n - 3)
                            sp.wait_ge(x1, c.n - 3)
                            pass_on(sp, sp_passed)
                        sp.dma_start(X[c.slot(4)][:, :, :], rows_of(x, c)).then_inc(x_landed[c.slot(4)], 16)

                    def store_x1(c):
                        sp.wait_ge(x1, c.n + 1)
                        pass_on(sp, sp_passed)
                        sp.dma_start(rows_of(x1_table, c), X1[c.slot(8)][:, :, :]).then_inc(x1_stored[c.slot(8)], 16)

                    def store_out(c):
                        sp.wait_ge(outsum, c.n + 1)
                        pass_on(sp, sp_passed)
                        sp.dma_start(rows_of(out, c), OUT[c.slot(2)][:, :, :]).then_inc(out_stored[c.slot(2)], 16)

                    skewed(sp, NODE_CHUNKS, U, [(3, store_x1), (8, store_out), (0, load)])
                    for i, s in enumerate(x1_stored):
                        sp.wait_ge(s, 16 * fills(NODE_CHUNKS, 8, i))
                    for i, s in enumerate(out_stored):
                        sp.wait_ge(s, 16 * fills(NODE_CHUNKS, 2, i))

                @block.gpsimd
                def _(pool):
                    def rstds(c):
                        b = c.slot(2)
                        if not c.known() or c.n < NODE_CHUNKS:
                            pool.wait_ge(stat0, c.n + 1)
                        if c.has_before(2):
                            pool.wait_ge(stat1, c.n - 1)
                            pool.wait_ge(norm0, c.n - 1)
                            pool.wait_ge(nb, c.n - 1)
                        else:
                            pool.wait_ge(filled, 2)
                        if c.has_before(4):
                            pool.wait_ge(norm1, c.n - 3)
                        pass_on(pool, pool_passed)
                        pool.tensor_scalar(VE[b][:, :, :], MV[b][:, :, :, 1], EPS, None, ALU.add).then_inc(ve, 1)
                        pool.wait_ge(ve, c.n + 1)
                        pool.tensor_tensor(RS[b][:, :, :], VE[b][:, :, :], minus_half[0:ROWS, :].rearrange("p (k j) -> p k j", k=2),
                                           ALU.pow).then_inc(rstd, 1)

                    def h_minus_n(c):
                        b = c.slot(2)
                        pool.wait_ge(nn, c.n + 1)
                        pool.tensor_tensor(D[b][:, :], H1T[c.slot(4)][:, :], NN[b][:, :], ALU.subtract).then_inc(diff, 1)
                        pool.wait_ge(diff, c.n + 1)
                        if c.has_before(2):
                            pool.wait_ge(summed, c.n - 1)
                        pool.tensor_tensor(D2[b][:, :], Z[b][:, :], D[b][:, :], ALU.mult).then_inc(zdiff, 1)

                    skewed(pool, NODE_CHUNKS, U, [(0, rstds, 2), (5, h_minus_n)])

                @block.vector
                def _(dve):
                    for b in range(2):
                        dve.memset(MV[b][:, :, :, :], 1.0).then_inc(filled, 1)
                    dve.wait_ge(filled, 2)

                    def stats(c, k, S, bn, stat):
                        b = c.slot(2)
                        for j in range(TILES):
                            i = dve.bn_stats(ST[b][:, k, j, :], S[:, j, :])
                        i.then_inc(bn, 1)
                        dve.wait_ge(bn, c.n + 1)
                        pass_on(dve, dve_passed)
                        for j in range(TILES):
                            i = dve.bn_aggr(MV[b][:, k, j, :], ST[b][:, k, j, :])
                        i.then_inc(stat, 1)

                    def stats_0(c):
                        dve.wait_ge(x_landed[c.slot(4)], 16 * c.uses(4))
                        if c.has_before(2):
                            dve.wait_ge(rstd, c.n - 1)
                        stats(c, 0, X[c.slot(4)], bn0, stat0)

                    def shift_0(c):
                        b = c.slot(2)
                        dve.wait_ge(rstd, c.n + 1)
                        if c.has_before(2):
                            dve.wait_ge(norm0, c.n - 1)
                        dve.scalar_tensor_tensor(NB[b][:, :], MV[b][:, 0, :, 0], -1.0, RS[b][:, 0, :], ALU.mult, ALU.mult).then_inc(nb, 1)

                    def add_x1(c):
                        dve.wait_ge(wmm, c.n + 1)
                        if c.has_before(8):
                            dve.wait_ge(x1_stored[c.slot(8)], 16 * (c.uses(8) - 1))
                            dve.wait_ge(outsum, c.n - 7)
                        dve.tensor_tensor(X1[c.slot(8)][:, :, :], P_W[0:ROWS, :].rearrange("p (j f) -> p j f", j=TILES),
                                          X[c.slot(4)][:, :, :], ALU.add).then_inc(x1, 1)

                    def stats_1(c):
                        dve.wait_ge(x1, c.n + 1)
                        if c.has_before(2):
                            dve.wait_ge(rstd, c.n + 1)
                            dve.wait_ge(norm1, c.n - 1)
                        stats(c, 1, X1[c.slot(8)], bn1, stat1)

                    def norm_1(c):
                        b = c.slot(2)
                        dve.wait_ge(rstd, c.n + 3)
                        if c.has_before(2):
                            dve.wait_ge(tr1, c.n - 1)
                        for j in range(TILES):
                            i = dve.tensor_scalar(H1N[b][:, j, :], X1[c.slot(8)][:, j, :], MV[b][:, 1, j, 0:1], RS[b][:, 1, j:j + 1],
                                                  ALU.subtract, ALU.mult)
                        i.then_inc(norm1, 1)

                    def reset_gate(c):
                        dve.wait_ge(gates, c.n + 1)
                        dve.wait_ge(r_ready, c.n + 1)
                        if c.has_before(2):
                            dve.wait_ge(nn, c.n - 1)
                        dve.scalar_tensor_tensor(NT[c.slot(2)][:, :], P_N[:, 0:CHUNK], bhh[:, 2:3], R[c.slot(2)][:, :],
                                                 ALU.add, ALU.mult).then_inc(nt, 1)

                    def mix(c):
                        b = c.slot(2)
                        dve.wait_ge(zdiff, c.n + 1)
                        if c.has_before(2):
                            dve.wait_ge(trd, c.n - 1)
                        dve.tensor_tensor(D3[b][:, :], D2[b][:, :], NN[b][:, :], ALU.add).then_inc(summed, 1)

                    def add_out(c):
                        b = c.slot(2)
                        dve.wait_ge(trd, c.n + 1)
                        if c.has_before(2):
                            dve.wait_ge(out_stored[b], 16 * (c.uses(2) - 1))
                        dve.tensor_tensor(OUT[b][:, :, :], P_O[0:ROWS, :].rearrange("p (j f) -> p j f", j=TILES),
                                          X1[c.slot(8)][:, :, :], ALU.add).then_inc(outsum, 1)

                    skewed(dve, NODE_CHUNKS, U, [(1, shift_0), (3, norm_1), (2, add_x1), (7, add_out), (2, stats_1), (0, stats_0),
                                                 (6, mix), (4, reset_gate)])

                @block.scalar
                def _(act):
                    def norm_0(c):
                        b = c.slot(2)
                        act.wait_ge(nb, c.n + 1)
                        if c.has_before(2):
                            act.wait_ge(tr0, c.n - 1)
                        for j in range(TILES):
                            i = act.activation(HN[b][:, j, :], X[c.slot(4)][:, j, :], ACT.Identity, bias=NB[b][:, j:j + 1],
                                               scale=RS[b][:, 0, j:j + 1])
                        i.then_inc(norm0, 1)

                    def relu_0(c):
                        act.wait_ge(tr0, c.n + 1)
                        if c.has_before(2):
                            act.wait_ge(wmm, c.n - 1)
                        act.activation(HT[c.slot(2)][:, :], P_T0[:, 0:CHUNK], ACT.Relu).then_inc(relu0, 1)

                    def relu_1(c):
                        act.wait_ge(tr1, c.n + 1)
                        if c.has_before(4):
                            act.wait_ge(gates, c.n - 3)
                            act.wait_ge(diff, c.n - 3)
                        act.activation(H1T[c.slot(4)][:, :], P_T1[:, 0:CHUNK], ACT.Relu).then_inc(relu1, 1)

                    def sigmoids(c):
                        b = c.slot(2)
                        act.wait_ge(gates, c.n + 1)
                        if c.has_before(2):
                            act.wait_ge(nt, c.n - 1)
                            act.wait_ge(zdiff, c.n - 1)
                        act.activation(R[b][:, :], P_R[:, 0:CHUNK], ACT.Sigmoid, bias=bsum[:, 0:1]).then_inc(r_ready, 1)
                        act.activation(Z[b][:, :], P_Z[:, 0:CHUNK], ACT.Sigmoid, bias=bsum[:, 1:2]).then_inc(z_ready, 1)

                    def tanh(c):
                        b = c.slot(2)
                        act.wait_ge(nt, c.n + 1)
                        if c.has_before(2):
                            act.wait_ge(summed, c.n - 1)
                            act.wait_ge(diff, c.n - 1)
                        act.activation(NN[b][:, :], NT[b][:, :], ACT.Tanh, bias=bih[:, 2:3]).then_inc(nn, 1)

                    skewed(act, NODE_CHUNKS, U, [(5, tanh), (1, norm_0), (4, sigmoids), (3, relu_1), (1, relu_0)])

                @block.tensor
                def _(pe):
                    def transposes(bank_, S, done):
                        for j in range(TILES):
                            i = pe.transpose(bank_[:, j * ROWS:(j + 1) * ROWS], S[:, j, :], ident[0:ROWS, 0:ROWS])
                        i.then_inc(done, 1)

                    def tr_0(c):
                        pe.wait_ge(norm0, c.n + 1)
                        if c.has_before(1):
                            pe.wait_ge(relu0, c.n)
                        transposes(P_T0, HN[c.slot(2)], tr0)

                    def w_mm(c):
                        if c.has_before(1):
                            pe.wait_ge(x1, c.n)
                        pe.matmul(P_W[0:ROWS, :], first_row[:, :], bias_row[:, :, :].rearrange("p j f -> p (j f)"), start=True, stop=False)
                        pe.wait_ge(relu0, c.n + 1)
                        for j in range(TILES):
                            i = pe.matmul(P_W[0:ROWS, j * F:(j + 1) * F], HT[c.slot(2)][:, j * ROWS:(j + 1) * ROWS], W_sb[:, :],
                                          start=False, stop=(j == TILES - 1))
                        i.then_inc(wmm, 1)

                    def tr_1(c):
                        pe.wait_ge(norm1, c.n + 1)
                        if c.has_before(1):
                            pe.wait_ge(relu1, c.n)
                        transposes(P_T1, H1N[c.slot(2)], tr1)

                    def gate_mm(c):
                        pe.wait_ge(relu1, c.n + 1)
                        if c.has_before(1):
                            pe.wait_ge(r_ready, c.n)
                            pe.wait_ge(z_ready, c.n)
                            pe.wait_ge(nt, c.n)
                        for g, P in enumerate((P_R, P_Z, P_N)):
                            i = pe.matmul(P[:, 0:CHUNK], whh_T[:, g, :], H1T[c.slot(4)][:, :], start=True, stop=True)
                        i.then_inc(gates, 1)

                    def tr_out(c):
                        pe.wait_ge(summed, c.n + 1)
                        if c.has_before(1):
                            pe.wait_ge(outsum, c.n)
                        for j in range(TILES):
                            i = pe.transpose(P_O[0:ROWS, j * F:(j + 1) * F], D3[c.slot(2)][:, j * ROWS:(j + 1) * ROWS], ident[:, :])
                        i.then_inc(trd, 1)

                    skewed(pe, NODE_CHUNKS, U, [(2, w_mm), (4, gate_mm), (3, tr_1), (1, tr_0), (6, tr_out)])

        end_phase()

        U = 4

        class EdgeFront:

            def __init__(self, memory, pre):
                def ring(name, depth, shape, dt=F32):
                    return [memory.enter_context(nc.sbuf_tensor(f"{pre}{name}{i}", shape, dt)) for i in range(depth)]

                def sem(name):
                    return new_sem((f"{pre}_{name}"))
                self.ring, self.sem = ring, sem
                self.XG = ring("XG", 4, [ROWS, 2 * TILES, F])
                self.HN = ring("HN", 2, [ROWS, 2 * TILES, F])
                self.H = ring("H", 4, [F, 2, CHUNK])
                self.ST = ring("ST", 2, [ROWS, 2 * TILES, 6])
                self.MV = ring("MV", 2, [ROWS, 2 * TILES, 2])
                self.VE = ring("VE", 2, [ROWS, 2 * TILES])
                self.RS = ring("RS", 2, [ROWS, 2 * TILES])
                self.NB = ring("NB", 2, [ROWS, 2 * TILES])
                self.IX = ring("IX", 4, [ROWS, 2 * TILES], U32)
                self.IE = ring("IE", 4, [ROWS, TILES], U32)
                self.NODE = ring("NODE", 2, [128, CHUNK + 1], I32)
                self.KEEP = ring("KEEP", 2, [F, CHUNK])
                self.OUT = ring("OUT", 4, [ROWS, TILES, F])
                self.gathered = [sem(f"gathered{i}") for i in range(4)]
                self.own_landed = [sem(f"own_landed{i}") for i in range(4)]
                self.node_landed = [sem(f"node_landed{i}") for i in range(2)]
                self.scattered = [sem(f"scattered{i}") for i in range(4)]
                self.sp_passed, self.pool_passed, self.dve_passed = sem("sp_passed"), sem("pool_passed"), sem("dve_passed")
                self.idx, self.ends = sem("idx"), sem("ends")
                self.bn, self.stat = sem("bn"), sem("stat")
                self.ve, self.rstd, self.nb = sem("ve"), sem("rstd"), sem("nb")
                self.norm, self.tr, self.relu = sem("norm"), sem("tr"), sem("relu")
                self.first = sem("first")
                self.keep = sem("keep")
                self.x_out = sem("x_out")

        def load_nodes(sp, s, c):
            b = c.slot(2)
            if c.has_before(2):
                sp.wait_ge(s.keep, c.n - 1)
                pass_on(sp, s.sp_passed)
            if c.known() and c.n == 0:
                sp.dma_start(s.NODE[b][:, 1:CHUNK + 1], dst[0:CHUNK].partition_broadcast(128)).then_inc(s.node_landed[b], 16)
            else:
                sp.dma_start(s.NODE[b][:, :], dst[bass.ds(c.n * CHUNK - 1, CHUNK + 1)].partition_broadcast(128)).then_inc(s.node_landed[b], 16)

        def gather(pool, s, c, table, tiles, freed):
            b = c.slot(4)
            pool.wait_ge(s.idx, c.n + 1)
            if c.has_before(4):
                pool.wait_ge(s.norm, c.n - 3)
                if freed is not None:
                    pool.wait_ge(freed, c.n - 3)
            pass_on(pool, s.pool_passed)
            for j in range(tiles):
                pool.indirect_dma_start(out=s.XG[b][:, j, :], out_offset=None, in_=table,
                                        in_offset=bass.IndirectOffsetOnAxis(ap=s.IX[b][:, j:j + 1], axis=0),
                                        bounds_check=N - 1, oob_is_err=False).then_inc(s.gathered[b], 16)

        def edge_rstd(pool, s, c):
            b = c.slot(2)
            pool.wait_ge(s.stat, c.n + 1)
            if c.has_before(2):
                pool.wait_ge(s.norm, c.n - 1)
                pool.wait_ge(s.nb, c.n - 1)
            pass_on(pool, s.pool_passed)
            pool.tensor_scalar(s.VE[b][:, :], s.MV[b][:, :, 1], EPS, None, ALU.add).then_inc(s.ve, 1)
            pool.wait_ge(s.ve, c.n + 1)
            pool.tensor_tensor(s.RS[b][:, :], s.VE[b][:, :], minus_half[0:ROWS, :], ALU.pow).then_inc(s.rstd, 1)

        def scatter(pool, s, c, to):
            b = c.slot(4)
            pool.wait_ge(s.x_out, c.n + 1)
            pool.wait_ge(s.ends, c.n + 1)
            pass_on(pool, s.pool_passed)
            for j in range(TILES):
                pool.indirect_dma_start(out=to, out_offset=bass.IndirectOffsetOnAxis(ap=s.IE[b][:, j:j + 1], axis=0),
                                        in_=s.OUT[b][:, j, :], in_offset=None,
                                        bounds_check=N - 1, oob_is_err=False).then_inc(s.scattered[b], 16)

        def edge_index(dve, s, c, tiles):
            b = c.slot(4)
            if c.has_before(4):
                dve.wait_ge(s.gathered[b], 16 * tiles * (c.uses(4) - 1))
            i = dve.tensor_copy(s.IX[b][:, 0:TILES], src_idx[:, bass.ds(c.n * TILES, TILES)])
            if tiles > TILES:
                i = dve.tensor_copy(s.IX[b][:, TILES:2 * TILES], dst_idx[:, bass.ds(c.n * TILES, TILES)])
            i.then_inc(s.idx, 1)

        def edge_ends(dve, s, c):
            b = c.slot(4)
            if c.has_before(4):
                dve.wait_ge(s.scattered[b], 16 * TILES * (c.uses(4) - 1))
            dve.tensor_copy(s.IE[b][:, :], end_idx[:, bass.ds(c.n * TILES, TILES)]).then_inc(s.ends, 1)

        def edge_stats(dve, s, c, tiles):
            b = c.slot(2)
            dve.wait_ge(s.gathered[c.slot(4)], 16 * tiles * c.uses(4))
            if tiles == TILES:
                dve.wait_ge(s.own_landed[c.slot(4)], 16 * c.uses(4))
            if c.has_before(2):
                dve.wait_ge(s.rstd, c.n - 1)
            for j in range(2 * TILES):
                i = dve.bn_stats(s.ST[b][:, j, :], s.XG[c.slot(4)][:, j, :])
            i.then_inc(s.bn, 1)
            dve.wait_ge(s.bn, c.n + 1)
            pass_on(dve, s.dve_passed)
            for j in range(2 * TILES):
                i = dve.bn_aggr(s.MV[b][:, j, :], s.ST[b][:, j, :])
            i.then_inc(s.stat, 1)

        def edge_shift(dve, s, c):
            b = c.slot(2)
            dve.wait_ge(s.rstd, c.n + 1)
            if c.has_before(2):
                dve.wait_ge(s.norm, c.n - 1)
            dve.scalar_tensor_tensor(s.NB[b][:, :], s.MV[b][:, :, 0], -1.0, s.RS[b][:, :], ALU.mult, ALU.mult).then_inc(s.nb, 1)

        def edge_norm(act, s, c):
            b = c.slot(2)
            act.wait_ge(s.nb, c.n + 1)
            if c.has_before(2):
                act.wait_ge(s.tr, c.n - 1)
            for j in range(2 * TILES):
                i = act.activation(s.HN[b][:, j, :], s.XG[c.slot(4)][:, j, :], ACT.Identity, bias=s.NB[b][:, j:j + 1],
                                   scale=s.RS[b][:, j:j + 1])
            i.then_inc(s.norm, 1)

        def edge_transposes(pe, s, c, banks):
            b = c.slot(2)
            pe.wait_ge(s.norm, c.n + 1)
            if c.has_before(1):
                pe.wait_ge(s.relu, c.n)
            for j in range(2 * TILES):
                i = pe.transpose(banks[j // TILES][:, j % TILES * ROWS:(j % TILES + 1) * ROWS], s.HN[b][:, j, :], ident[0:ROWS, 0:ROWS])
            i.then_inc(s.tr, 1)

        def edge_relu(act, s, c, banks, used):
            act.wait_ge(s.tr, c.n + 1)
            if c.has_before(4):
                for u in used:
                    act.wait_ge(u, c.n - 3)
            for k in range(2):
                i = act.activation(s.H[c.slot(4)][:, k, :], banks[k][:, 0:CHUNK], ACT.Relu)
            i.then_inc(s.relu, 1)

        def edge_keep(dve, s, c, used):
            b = c.slot(2)
            dve.wait_ge(s.node_landed[b], 16 * c.uses(2))
            if c.known() and c.n == 0:
                dve.memset(s.NODE[b][:, 0:1], -1).then_inc(s.first, 1)
                dve.wait_ge(s.first, 1)
            if c.has_before(2):
                dve.wait_ge(used, c.n - 1)
            dve.tensor_tensor(s.KEEP[b][:, :], s.NODE[b][:, 1:CHUNK + 1], s.NODE[b][:, 0:CHUNK], ALU.is_equal).then_inc(s.keep, 1)

        def wait_scatters(pool, s):
            for i, m in enumerate(s.scattered):
                pool.wait_ge(m, 16 * TILES * fills(EDGE_CHUNKS, 4, i))

        def chunk_rows(table, c):
            return table[bass.ds(c.n * CHUNK, CHUNK), :].rearrange("(j p) f -> p j f", p=ROWS)

        with ExitStack() as gctx:
            s = EdgeFront(gctx, "g")
            ring, sem = s.ring, s.sem
            XB = ring("XB", 4, [ROWS, TILES, F])
            CUT = ring("CUT", 1, [F, CHUNK])[0]
            LR = ring("LR", 2, [F, 2, CHUNK])
            L = ring("L", 1, [F, 2, CHUNK])[0]
            SELF = ring("SELF", 1, [F, CHUNK])[0]
            TOP = ring("TOP", 1, [F, CHUNK])[0]
            LIFT = ring("LIFT", 1, [F, CHUNK])[0]
            MX = ring("MX", 1, [F, CHUNK + 1])[0]
            ARG = ring("ARG", 2, [F, 3, CHUNK])
            EX = ring("EX", 2, [F, 3, CHUNK])
            PV = ring("PV", 1, [F, CHUNK])[0]
            QV = ring("QV", 1, [F, CHUNK])[0]
            UV = ring("UV", 1, [F, CHUNK])[0]
            PQ = ring("PQ", 2, [F, CHUNK])
            ACC = ring("ACC", 2, [F, CHUNK])
            DEN = ring("DEN", 2, [F, CHUNK])
            DENS = ring("DENS", 1, [ROWS, TILES * HEADS])[0]
            RD = ring("RD", 1, [ROWS, TILES * HEADS])[0]
            SCALED = ring("SCALED", 1, [ROWS, TILES * F])[0]
            (values, lmm, logits, leaky, cut, selfl, top, lift, mx, arg, ex, carry, pv, uv, acc, den, dens, rd, scaled, tro, pq,
             xb) = map(sem, "values lmm logits leaky cut selfl top lift mx arg ex carry pv uv acc den dens rd scaled tro pq xb".split())
            own_stored = [sem(f"own_stored{i}") for i in range(4)]
            P_S, P_D, P_VS, P_VD, P_E, P_SELF, P_O, P_DEN = bank
            with nc.Block() as block:
                @block.sync
                def _(sp):
                    def store_own(c):
                        sp.wait_ge(s.x_out, c.n + 1)
                        pass_on(sp, s.sp_passed)
                        sp.dma_start(chunk_rows(x1_edges, c), s.OUT[c.slot(4)][:, :, :]).then_inc(own_stored[c.slot(4)], 16)
                    skewed(sp, EDGE_CHUNKS, U, [(3, lambda c: load_nodes(sp, s, c)), (7, store_own)])
                    for i, m in enumerate(own_stored):
                        sp.wait_ge(m, 16 * fills(EDGE_CHUNKS, 4, i))

                @block.gpsimd
                def _(pool):
                    def add_bias(c):
                        b = c.slot(4)
                        pool.wait_ge(s.gathered[b], 16 * 2 * TILES * c.uses(4))
                        if c.has_before(4):
                            pool.wait_ge(s.x_out, c.n - 3)
                        pool.tensor_tensor(XB[b][:, :, :], s.XG[b][:, TILES:2 * TILES, :], bias_row[0:ROWS, :, :], ALU.add).then_inc(xb, 1)

                    skewed(pool, EDGE_CHUNKS, U, [(7, lambda c: scatter(pool, s, c, x1_table)),
                                                  (0, lambda c: gather(pool, s, c, x, 2 * TILES, xb)),
                                                  (1, lambda c: edge_rstd(pool, s, c)), (3, add_bias)])
                    wait_scatters(pool, s)

                @block.tensor
                def _(pe):
                    def logit_mm(c):
                        b = c.slot(4)
                        pe.wait_ge(s.relu, c.n + 1)
                        if c.has_before(1):
                            pe.wait_ge(logits, 2 * c.n)
                        pe.matmul(P_E[:, 0:CHUNK], Wlog_src[:, :], s.H[b][:, 0, :], start=True, stop=False)
                        pe.matmul(P_E[:, 0:CHUNK], Wlog_dst[:, :], s.H[b][:, 1, :], start=False, stop=True)
                        pe.matmul(P_SELF[:, 0:CHUNK], Wlog_self[:, :], s.H[b][:, 1, :], start=True, stop=True).then_inc(lmm, 1)

                    def value_mm(c):
                        b = c.slot(4)
                        if c.has_before(1):
                            pe.wait_ge(pv, 2 * c.n)
                        pe.matmul(P_VS[:, 0:CHUNK], W_sb[:, :], s.H[b][:, 0, :], start=True, stop=True)
                        pe.matmul(P_VD[:, 0:CHUNK], W_sb[:, :], s.H[b][:, 1, :], start=True, stop=True).then_inc(values, 1)

                    def tr_out(c):
                        b = c.slot(2)
                        pe.wait_ge(den, c.n + 1)
                        if c.has_before(1):
                            pe.wait_ge(scaled, c.n)
                        for j in range(TILES):
                            pe.matmul(P_DEN[0:ROWS, j * HEADS:(j + 1) * HEADS], DEN[b][:, j * ROWS:(j + 1) * ROWS], head_sel[:, :],
                                      start=True, stop=True)
                        pe.wait_ge(acc, c.n + 1)
                        for j in range(TILES):
                            i = pe.transpose(P_O[0:ROWS, j * F:(j + 1) * F], ACC[b][:, j * ROWS:(j + 1) * ROWS], ident[:, :])
                        i.then_inc(tro, 1)

                    skewed(pe, EDGE_CHUNKS, U, [(3, logit_mm), (2, lambda c: edge_transposes(pe, s, c, (P_S, P_D))), (4, value_mm),
                                                (5, tr_out)])

                @block.scalar
                def _(act):
                    def raw_logits(c):
                        b = c.slot(2)
                        act.wait_ge(lmm, c.n + 1)
                        if c.has_before(2):
                            act.wait_ge(leaky, c.n - 1)
                        act.activation(LR[b][:, 0, :], P_E[:, 0:CHUNK], ACT.Copy).then_inc(logits, 1)
                        act.activation(LR[b][:, 1, :], P_SELF[:, 0:CHUNK], ACT.Copy).then_inc(logits, 1)

                    def exps(c):
                        b = c.slot(2)
                        act.wait_ge(arg, 3 * (c.n + 1))
                        if c.has_before(2):
                            act.wait_ge(acc, c.n - 1)
                            act.wait_ge(pq, c.n - 1)
                        act.activation(EX[b][:, :, :], ARG[b][:, :, :], ACT.Exp).then_inc(ex, 1)

                    skewed(act, EDGE_CHUNKS, U, [(2, lambda c: edge_norm(act, s, c)), (3, raw_logits),
                                                 (2, lambda c: edge_relu(act, s, c, (P_S, P_D), (values, lmm))), (4, exps)])

                @block.vector
                def _(dve):
                    def softmax(c):
                        b = c.slot(2)
                        dve.wait_ge(s.keep, c.n + 1)
                        dve.tensor_scalar(CUT[:, :], s.KEEP[b][:, :], 1.0, FAR, ALU.subtract, ALU.mult).then_inc(cut, 1)
                        dve.wait_ge(logits, 2 * (c.n + 1))
                        dve.scalar_tensor_tensor(L[:, :, :], LR[b][:, :, :], SLOPE, LR[b][:, :, :], ALU.mult, ALU.max).then_inc(leaky, 1)
                        dve.wait_ge(leaky, c.n + 1)
                        dve.scalar_tensor_tensor(SELF[:, :], s.KEEP[b][:, :], -FAR, L[:, 1, :], ALU.mult, ALU.add).then_inc(selfl, 1)
                        dve.wait_ge(selfl, c.n + 1)
                        dve.tensor_tensor(TOP[:, :], L[:, 0, :], SELF[:, :], ALU.max).then_inc(top, 1)
                        if c.known() and c.n == 0:
                            dve.memset(MX[:, 0:1], 0.0).then_inc(carry, 1)
                        else:
                            dve.tensor_copy(MX[:, 0:1], MX[:, CHUNK:CHUNK + 1]).then_inc(carry, 1)
                        dve.wait_ge(top, c.n + 1)
                        dve.wait_ge(cut, c.n + 1)
                        dve.wait_ge(carry, c.n + 1)
                        dve.tensor_tensor_scan(MX[:, 1:CHUNK + 1], CUT[:, :], TOP[:, :], MX[:, 0:1], ALU.add, ALU.max).then_inc(mx, 1)
                        dve.wait_ge(mx, c.n + 1)
                        if c.has_before(2):
                            dve.wait_ge(ex, c.n - 1)
                        dve.tensor_tensor(LIFT[:, :], CUT[:, :], MX[:, 0:CHUNK], ALU.add).then_inc(lift, 1)
                        dve.tensor_tensor(ARG[b][:, 0, :], L[:, 0, :], MX[:, 1:CHUNK + 1], ALU.subtract).then_inc(arg, 1)
                        dve.tensor_tensor(ARG[b][:, 1, :], SELF[:, :], MX[:, 1:CHUNK + 1], ALU.subtract).then_inc(arg, 1)
                        dve.wait_ge(lift, c.n + 1)
                        dve.tensor_tensor(ARG[b][:, 2, :], LIFT[:, :], MX[:, 1:CHUNK + 1], ALU.subtract).then_inc(arg, 1)

                    def combine(c):
                        b = c.slot(2)
                        p = 1 - b
                        first = c.known() and c.n == 0
                        dve.wait_ge(ex, c.n + 1)
                        dve.tensor_tensor(PQ[b][:, :], EX[b][:, 0, :], EX[b][:, 1, :], ALU.add).then_inc(pq, 1)
                        dve.wait_ge(values, c.n + 1)
                        dve.tensor_tensor(PV[:, :], P_VS[:, 0:CHUNK], EX[b][:, 0, :], ALU.mult).then_inc(pv, 1)
                        dve.tensor_tensor(QV[:, :], P_VD[:, 0:CHUNK], EX[b][:, 1, :], ALU.mult).then_inc(pv, 1)
                        dve.wait_ge(pq, c.n + 1)
                        if not first:
                            dve.wait_ge(den, c.n)
                        if c.has_before(2):
                            dve.wait_ge(tro, c.n - 1)
                        dve.tensor_tensor_scan(DEN[b][:, :], EX[b][:, 2, :], PQ[b][:, :], 0.0 if first else DEN[p][:, CHUNK - 1:CHUNK],
                                               ALU.mult, ALU.add).then_inc(den, 1)
                        dve.wait_ge(pv, 2 * (c.n + 1))
                        dve.tensor_tensor(UV[:, :], PV[:, :], QV[:, :], ALU.add).then_inc(uv, 1)
                        dve.wait_ge(uv, c.n + 1)
                        if not first:
                            dve.wait_ge(acc, c.n)
                        dve.tensor_tensor_scan(ACC[b][:, :], EX[b][:, 2, :], UV[:, :], 0.0 if first else ACC[p][:, CHUNK - 1:CHUNK],
                                               ALU.mult, ALU.add).then_inc(acc, 1)

                    def finish(c):
                        b = c.slot(4)
                        dve.wait_ge(tro, c.n + 1)
                        dve.tensor_scalar(DENS[:, :], P_DEN[0:ROWS, 0:TILES * HEADS], 1e-16, None, ALU.add).then_inc(dens, 1)
                        dve.wait_ge(dens, c.n + 1)
                        dve.reciprocal(RD[:, :], DENS[:, :]).then_inc(rd, 1)
                        dve.wait_ge(rd, c.n + 1)
                        C = F // HEADS
                        dve.tensor_tensor(SCALED[:, :].rearrange("p (t c) -> p t c", c=C), P_O[0:ROWS, :].rearrange("p (t c) -> p t c", c=C),
                                          RD[:, :].unsqueeze(2).to_broadcast([ROWS, TILES * HEADS, C]), ALU.mult).then_inc(scaled, 1)
                        dve.wait_ge(scaled, c.n + 1)
                        dve.wait_ge(xb, c.n + 1)
                        if c.has_before(4):
                            dve.wait_ge(s.scattered[b], 16 * TILES * (c.uses(4) - 1))
                            dve.wait_ge(own_stored[b], 16 * (c.uses(4) - 1))
                        dve.tensor_tensor(s.OUT[b][:, :, :], SCALED[:, :].rearrange("p (j f) -> p j f", j=TILES), XB[b][:, :, :],
                                          ALU.add).then_inc(s.x_out, 1)

                    skewed(dve, EDGE_CHUNKS, U, [(0, lambda c: edge_index(dve, s, c, 2 * TILES)), (2, lambda c: edge_shift(dve, s, c)),
                                                 (1, lambda c: edge_stats(dve, s, c, 2 * TILES)), (5, combine),
                                                 (4, lambda c: edge_keep(dve, s, c, selfl)), (4, softmax),
                                                 (6, lambda c: edge_ends(dve, s, c)), (6, finish)])

        end_phase()

        with ExitStack() as mctx:
            s = EdgeFront(mctx, "m")
            ring, sem = s.ring, s.sem
            TYPE = ring("TYPE", 2, [128, CHUNK], I32)
            HOT = ring("HOT", 2, [ETYPES, CHUNK])
            HM = ring("HM", 4, [F, CHUNK])
            MS = ring("MS", 2, [F, CHUNK])
            R = ring("R", 2, [F, CHUNK])
            Z = ring("Z", 2, [F, CHUNK])
            NT = ring("NT", 1, [F, CHUNK])[0]
            NT2 = ring("NT2", 2, [F, CHUNK])
            NN = ring("NN", 2, [F, CHUNK])
            D = ring("D", 2, [F, CHUNK])
            D2 = ring("D2", 2, [F, CHUNK])
            D3 = ring("D3", 2, [F, CHUNK])
            X1 = ring("X1", 4, [ROWS, TILES, F])
            type_landed = [sem(f"type_landed{i}") for i in range(2)]
            x1_landed = [sem(f"x1_landed{i}") for i in range(4)]
            masked, hot, msg_used, msg, msum, gates, r_ready, z_ready, nt, nt2, nn, diff, zdiff, summed, tro = map(
                sem, "masked hot msg_used msg msum gates r_ready z_ready nt nt2 nn diff zdiff summed tro".split())
            P_S, P_D, P_M, P_R, P_Z, P_NI, P_NH, P_O = bank
            with nc.Block() as block:
                @block.sync
                def _(sp):
                    def load_own(c):
                        b = c.slot(4)
                        if c.has_before(4):
                            sp.wait_ge(s.norm, c.n - 3)
                            pass_on(sp, s.sp_passed)
                        sp.dma_start(s.XG[b][:, TILES:2 * TILES, :], chunk_rows(x1_edges, c)).then_inc(s.own_landed[b], 16)

                    def load_types(c):
                        b = c.slot(2)
                        if c.has_before(2):
                            sp.wait_ge(masked, ETYPES * (c.n - 1))
                            sp.wait_ge(hot, c.n - 1)
                            pass_on(sp, s.sp_passed)
                        sp.dma_start(TYPE[b][:, :], etype[bass.ds(c.n * CHUNK, CHUNK)].partition_broadcast(128)).then_inc(type_landed[b], 16)

                    def load_x1(c):
                        b = c.slot(4)
                        if c.has_before(4):
                            sp.wait_ge(s.x_out, c.n - 3)
                            pass_on(sp, s.sp_passed)
                        sp.dma_start(X1[b][:, :, :], chunk_rows(x1_edges, c)).then_inc(x1_landed[b], 16)

                    skewed(sp, EDGE_CHUNKS, U, [(0, load_own), (1, load_types), (1, lambda c: load_nodes(sp, s, c)), (4, load_x1)])

                @block.gpsimd
                def _(pool):
                    def h_minus_n(c):
                        b = c.slot(2)
                        pool.wait_ge(nn, c.n + 1)
                        pool.tensor_tensor(D[b][:, :], s.H[c.slot(4)][:, 1, :], NN[b][:, :], ALU.subtract).then_inc(diff, 1)
                        pool.wait_ge(diff, c.n + 1)
                        if c.has_before(2):
                            pool.wait_ge(summed, c.n - 1)
                        pool.tensor_tensor(D2[b][:, :], Z[b][:, :], D[b][:, :], ALU.mult).then_inc(zdiff, 1)

                    skewed(pool, EDGE_CHUNKS, U, [(8, lambda c: scatter(pool, s, c, out)),
                                                  (0, lambda c: gather(pool, s, c, x1_table, TILES, None)),
                                                  (1, lambda c: edge_rstd(pool, s, c)), (5, h_minus_n)])
                    wait_scatters(pool, s)

                @block.tensor
                def _(pe):
                    def messages(c):
                        if c.has_before(1):
                            pe.wait_ge(msum, c.n)
                        for t in range(ETYPES):
                            pe.wait_ge(masked, ETYPES * c.n + t + 1)
                            pe.matmul(P_M[:, 0:CHUNK], msgW_sb[:, t, :], HM[t % 4][:, :], start=(t == 0), stop=False).then_inc(msg_used, 1)
                        pe.wait_ge(hot, c.n + 1)
                        pe.matmul(P_M[:, 0:CHUNK], msgb_sb[:, :], HOT[c.slot(2)][:, :], start=False, stop=True).then_inc(msg, 1)

                    def gate_mm(c):
                        b = c.slot(4)
                        if c.has_before(1):
                            pe.wait_ge(r_ready, c.n)
                            pe.wait_ge(z_ready, c.n)
                            pe.wait_ge(nt, c.n)
                        pe.wait_ge(s.relu, c.n + 1)
                        for g, P in enumerate((P_R, P_Z)):
                            pe.matmul(P[:, 0:CHUNK], whh_T[:, g, :], s.H[b][:, 1, :], start=True, stop=False)
                        pe.matmul(P_NH[:, 0:CHUNK], whh_T[:, 2, :], s.H[b][:, 1, :], start=True, stop=True)
                        if c.has_before(1):
                            pe.wait_ge(nt2, c.n)
                        pe.wait_ge(msum, c.n + 1)
                        for g, P in enumerate((P_R, P_Z)):
                            pe.matmul(P[:, 0:CHUNK], wih_T[:, g, :], MS[c.slot(2)][:, :], start=False, stop=True)
                        pe.matmul(P_NI[:, 0:CHUNK], wih_T[:, 2, :], MS[c.slot(2)][:, :], start=True, stop=True).then_inc(gates, 1)

                    def tr_out(c):
                        pe.wait_ge(summed, c.n + 1)
                        if c.has_before(1):
                            pe.wait_ge(s.x_out, c.n)
                        for j in range(TILES):
                            i = pe.transpose(P_O[0:ROWS, j * F:(j + 1) * F], D3[c.slot(2)][:, j * ROWS:(j + 1) * ROWS], ident[:, :])
                        i.then_inc(tro, 1)

                    skewed(pe, EDGE_CHUNKS, U, [(4, gate_mm), (2, lambda c: edge_transposes(pe, s, c, (P_S, P_D))), (6, tr_out),
                                                (3, messages)])

                @block.scalar
                def _(act):
                    def sigmoids(c):
                        b = c.slot(2)
                        act.wait_ge(gates, c.n + 1)
                        if c.has_before(2):
                            act.wait_ge(nt, c.n - 1)
                            act.wait_ge(zdiff, c.n - 1)
                        act.activation(R[b][:, :], P_R[:, 0:CHUNK], ACT.Sigmoid, bias=bsum[:, 0:1]).then_inc(r_ready, 1)
                        act.activation(Z[b][:, :], P_Z[:, 0:CHUNK], ACT.Sigmoid, bias=bsum[:, 1:2]).then_inc(z_ready, 1)

                    def tanh(c):
                        b = c.slot(2)
                        act.wait_ge(nt2, c.n + 1)
                        if c.has_before(2):
                            act.wait_ge(summed, c.n - 1)
                            act.wait_ge(diff, c.n - 1)
                        act.activation(NN[b][:, :], NT2[b][:, :], ACT.Tanh, bias=bih[:, 2:3]).then_inc(nn, 1)

                    skewed(act, EDGE_CHUNKS, U, [(2, lambda c: edge_norm(act, s, c)), (5, tanh),
                                                 (2, lambda c: edge_relu(act, s, c, (P_S, P_D), (diff,))), (4, sigmoids)])

                @block.vector
                def _(dve):
                    def mask(c):
                        b = c.slot(2)
                        dve.wait_ge(type_landed[b], 16 * c.uses(2))
                        if c.has_before(2):
                            dve.wait_ge(msg, c.n - 1)
                        dve.tensor_scalar(HOT[b][:, :], TYPE[b][0:ETYPES, :], type_id[:, 0:1], None, ALU.is_equal).then_inc(hot, 1)
                        dve.wait_ge(s.relu, c.n + 1)
                        for t in range(ETYPES):
                            if t >= 4 or c.has_before(1):
                                dve.wait_ge(msg_used, ETYPES * c.n + t - 3)
                            dve.scalar_tensor_tensor(HM[t % 4][:, :], TYPE[b][:, :], float(t), s.H[c.slot(4)][:, 0, :],
                                                     ALU.is_equal, ALU.mult).then_inc(masked, 1)

                    def total(c):
                        b = c.slot(2)
                        first = c.known() and c.n == 0
                        dve.wait_ge(msg, c.n + 1)
                        dve.wait_ge(s.keep, c.n + 1)
                        if not first:
                            dve.wait_ge(msum, c.n)
                        if c.has_before(2):
                            dve.wait_ge(gates, c.n - 1)
                        dve.tensor_tensor_scan(MS[b][:, :], s.KEEP[b][:, :], P_M[:, 0:CHUNK], 0.0 if first else MS[1 - b][:, CHUNK - 1:CHUNK],
                                               ALU.mult, ALU.add).then_inc(msum, 1)

                    def candidate(c):
                        b = c.slot(2)
                        dve.wait_ge(gates, c.n + 1)
                        dve.wait_ge(r_ready, c.n + 1)
                        dve.scalar_tensor_tensor(NT[:, :], P_NH[:, 0:CHUNK], bhh[:, 2:3], R[b][:, :], ALU.add, ALU.mult).then_inc(nt, 1)
                        dve.wait_ge(nt, c.n + 1)
                        if c.has_before(2):
                            dve.wait_ge(nn, c.n - 1)
                        dve.tensor_tensor(NT2[b][:, :], P_NI[:, 0:CHUNK], NT[:, :], ALU.add).then_inc(nt2, 1)

                    def mix(c):
                        b = c.slot(2)
                        dve.wait_ge(zdiff, c.n + 1)
                        if c.has_before(2):
                            dve.wait_ge(tro, c.n - 1)
                        dve.tensor_tensor(D3[b][:, :], D2[b][:, :], NN[b][:, :], ALU.add).then_inc(summed, 1)

                    def add_rows(c):
                        b = c.slot(4)
                        dve.wait_ge(tro, c.n + 1)
                        dve.wait_ge(x1_landed[b], 16 * c.uses(4))
                        if c.has_before(4):
                            dve.wait_ge(s.scattered[b], 16 * TILES * (c.uses(4) - 1))
                        dve.tensor_tensor(s.OUT[b][:, :, :], P_O[0:ROWS, :].rearrange("p (j f) -> p j f", j=TILES),
                                          X1[b][:, :, :], ALU.add).then_inc(s.x_out, 1)

                    skewed(dve, EDGE_CHUNKS, U, [(0, lambda c: edge_index(dve, s, c, TILES)), (2, lambda c: edge_shift(dve, s, c)),
                                                 (1, lambda c: edge_stats(dve, s, c, TILES)), (5, candidate),
                                                 (7, lambda c: edge_ends(dve, s, c)), (7, add_rows), (6, mix),
                                                 (3, lambda c: edge_keep(dve, s, c, msum)), (3, mask), (3, total)])


_INS = ['x', 'src', 'dst', 'edge_type_8', 'L0_gnn_W', 'L0_gnn_att_src', 'L0_gnn_att_dst', 'L0_gnn_bias',
        'L1_gnn_message_W', 'L1_gnn_message_b', 'L1_gnn_gru_w_ih', 'L1_gnn_gru_w_hh', 'L1_gnn_gru_b_ih', 'L1_gnn_gru_b_hh']


def kernel(**inputs):
    import numpy as _np
    import concourse.bacc as _bacc
    from concourse import mybir as _mybir
    from concourse.bass_utils import run_bass_kernel_spmd as _run

    nc = _bacc.Bacc("TRN2", target_bir_lowering=False, num_devices=1)
    arrays, args = {}, []
    for name in _INS:
        a = _np.ascontiguousarray(inputs[name])
        arrays[f"in_{name}"] = a
        args.append(nc.dram_tensor(f"in_{name}", a.shape, _mybir.dt.from_np(a.dtype), kind="ExternalInput").ap())
    args.append(nc.dram_tensor("out_0", inputs['x'].shape, _mybir.dt.float32, kind="ExternalOutput").ap())
    build(nc, *args)
    r = _run(nc, [arrays], core_ids=[0])
    return r.results[0]["out_0"]
```

```python
from contextlib import ExitStack

import concourse.bass as bass
from concourse import mybir

ALU = mybir.AluOpType
ACT = mybir.ActivationFunctionType
F32 = mybir.dt.float32
BF16 = mybir.dt.bfloat16
I32 = mybir.dt.int32
U32 = mybir.dt.uint32

F = 128
ROWS = 125
TILES = 4
CHUNK = ROWS * TILES
HEADS = 4
ETYPES = 8
EPS = 1e-5
SLOPE = 0.2
FAR = 2.0 ** 100
PARTS = 3
SKIP = 1 << 20


class Step:

    def __init__(self, unroll, turn, lane):
        self.unroll, self.turn, self.lane = unroll, turn, lane
        self.n = turn * unroll + lane

    def before(self, k):
        return Step(self.unroll, self.turn + (self.lane - k) // self.unroll, (self.lane - k) % self.unroll)

    def known(self):
        return isinstance(self.n, int)

    def has_before(self, depth):
        return not self.known() or self.n >= depth

    def uses(self, depth):
        return self.turn * (self.unroll // depth) + self.lane // depth + 1

    def slot(self, depth):
        return self.lane % depth


def pass_on(eng, passed):
    eng.sem_inc(passed, 1)


def skewed(eng, chunks, unroll, stages):
    stages = [(st[0], st[1], st[2] if len(st) > 2 else 0) for st in stages]
    last_lag = max(lag + more for lag, _, more in stages)
    first = -(-(last_lag + unroll) // unroll)
    last = chunks // unroll

    def step(turn, lane, known):
        for lag, body, more in stages:
            if known and not 0 <= turn * unroll + lane - lag < chunks + more:
                continue
            body(Step(unroll, turn + (lane - lag) // unroll, (lane - lag) % unroll))

    for s in range(first * unroll):
        step(s // unroll, s % unroll, True)
    with eng.Fori(first, last) as turn:
        for lane in range(unroll):
            step(turn, lane, False)
    for s in range(last * unroll, chunks + last_lag):
        step(s // unroll, s % unroll, True)


def fills(chunks, depth, slot):
    return (chunks - slot + depth - 1) // depth


def moments(dve, ST, SS, MM, DD, done):
    dve.scalar_tensor_tensor(SS, ST[..., 2], EPS * F, ST[..., 5], ALU.add, ALU.add)
    dve.tensor_tensor(MM, ST[..., 1], ST[..., 4], ALU.add)
    dve.tensor_tensor(DD, ST[..., 1], ST[..., 4], ALU.subtract).then_inc(done, 1)


def build(nc, x, src, dst, etype, W, att_src, att_dst, bias, msg_W, msg_b, w_ih, w_hh, b_ih, b_hh, out):
    N, E = x.shape[0], src.shape[0]
    NODE_CHUNKS, EDGE_CHUNKS, EDGE_TILES = N // CHUNK, E // CHUNK, E // ROWS
    HALF = EDGE_TILES // 2
    assert N % (4 * CHUNK) == 0 and E % (2 * CHUNK) == 0 and HALF <= 128 and W.shape[0] == F

    x1_table = nc.dram_tensor("x1_table", (N, F), F32).ap()
    x1_edges = nc.dram_tensor("x1_edges", (E, F), F32).ap()

    with ExitStack() as ctx:
        def sb(name, shape, dt=F32):
            return ctx.enter_context(nc.sbuf_tensor(name, shape, dt))

        phase_sems = []

        def new_sem(name):
            phase_sems.append(nc.alloc_semaphore(name=name))
            return phase_sems[-1]

        def end_phase():
            nc.clear_and_free_semaphores(phase_sems)
            phase_sems.clear()
            nc.all_engine_barrier()

        bank = [ctx.enter_context(nc.psum_tensor(f"bank{i}", [128, 512], F32)) for i in range(8)]

        e_dst = nc.dram_tensor("e_dst", (E + 2,), I32).ap()
        e_type = nc.dram_tensor("e_type", (E,), I32).ap()
        e_keep_cut = nc.dram_tensor("e_keep_cut", (2, E), F32).ap()
        sorted_edges = nc.dram_tensor("sorted_edges", (E, 4), I32).ap()

        def tile_rows(a, shift=0):
            return a[shift:shift + E].rearrange("(h t p) -> t h p", h=2, p=ROWS)

        ident = sb("ident", [128, 128])
        src_idx = sb("src_idx", [ROWS, EDGE_TILES], U32)
        dst_idx = sb("dst_idx", [ROWS, EDGE_TILES], U32)
        end_idx = sb("end_idx", [ROWS, EDGE_TILES], U32)

        def wide(P):
            return P[0:ROWS, 0:EDGE_TILES].rearrange("p (h t) -> p h t", h=2)

        with ExitStack() as ectx:
            def tmp(name, shape, dt=F32):
                return ectx.enter_context(nc.sbuf_tensor(name, shape, dt))
            S_, D_, T_ = range(3)
            rows_i = tmp("rows_i", [HALF, 3, 2, ROWS], I32)
            rows_f = tmp("rows_f", [HALF, 3, 2, ROWS])
            near_i = tmp("near_i", [HALF, 2, 2, ROWS], I32)
            near_f = tmp("near_f", [HALF, 2, 2, ROWS])
            flags = tmp("flags", [HALF, 2, ROWS])
            n_flags = tmp("n_flags", [HALF, 1])
            ones = tmp("ones", [HALF, 128])
            unsorted_i = tmp("unsorted_i", [128, 1], I32)
            minus_one = tmp("minus_one", [1, 1], I32)
            cols = tmp("cols", [ROWS, EDGE_TILES, 4])
            keep_cut = tmp("keep_cut", [HALF, 2, 2, ROWS])
            end_row = tmp("end_row", [HALF, 2, ROWS])
            landed, dst_stored, near_landed, const_set, ident_set, in_f, near_set, flagged, counted, total, cols_ps = map(
                new_sem, "landed dst_stored near_landed const_set ident_set in_f near_set flagged counted total cols_ps".split())
            with nc.Block() as block:
                @block.sync
                def _(sp):
                    for k, a in enumerate((src, dst, etype)):
                        sp.dma_start(rows_i[:, k, :, :], tile_rows(a)).then_inc(landed, 16)
                    sp.wait_ge(const_set, 3)
                    for end in (0, E + 1):
                        sp.dma_start(e_dst[end:end + 1].rearrange("(a b) -> a b", a=1), minus_one[:, :]).then_inc(dst_stored, 16)
                    sp.wait_ge(landed, 48)
                    sp.dma_start(tile_rows(e_dst, 1), rows_i[:, D_, :, :]).then_inc(dst_stored, 16)
                    sp.wait_ge(dst_stored, 48)
                    sp.dma_start(near_i[:, 1, :, :], tile_rows(e_dst, 2)).then_inc(near_landed, 16)
                    sp.wait_ge(near_landed, 16)

                @block.gpsimd
                def _(pool):
                    pool.memset(minus_one[:, :], -1).then_inc(const_set, 1)
                    pool.memset(ones[:, :], 1.0).then_inc(const_set, 1)
                    pool.memset(ident[:, :], 0.0).then_inc(const_set, 1)
                    pool.wait_ge(const_set, 3)
                    pool.affine_select(out=ident[:, :], in_=ident[:, :], compare_op=ALU.not_equal, fill=1.0, base=0,
                                       pattern=[[-1, 128]], channel_multiplier=1).then_inc(ident_set, 1)

                @block.vector
                def _(dve):
                    dve.wait_ge(landed, 48)
                    dve.tensor_copy(rows_f[:, :, :, :], rows_i[:, :, :, :]).then_inc(in_f, 1)
                    dve.wait_ge(near_landed, 16)
                    dve.tensor_copy(near_f[:, 1, :, :], near_i[:, 1, :, :]).then_inc(near_set, 1)
                    dve.memset(near_f[:, 0, :, :], 0.0)
                    dve.memset(cols[:, :, 3:4], 0.0)
                    dve.wait_ge(in_f, 1)
                    dve.wait_ge(near_set, 1)
                    dve.tensor_tensor(flags[:, :, :], rows_f[:, D_, :, :], near_f[:, 1, :, :], ALU.is_gt).then_inc(flagged, 1)
                    dve.wait_ge(flagged, 1)
                    dve.reduce_sum(n_flags[:, :], flags[:, :, :], mybir.AxisListType.XY).then_inc(counted, 1)
                    dve.wait_ge(total, 1)
                    dve.tensor_scalar(unsorted_i[:, :], bank[0][:, 0:1], 1.0, None, ALU.subtract)
                    dve.wait_ge(cols_ps, 1)
                    for k in range(3):
                        dve.tensor_copy(cols[:, :, k], bank[1 + k][0:ROWS, 0:EDGE_TILES])

                @block.tensor
                def _(pe):
                    pe.wait_ge(ident_set, 1)
                    pe.wait_ge(in_f, 1)
                    for k in range(3):
                        for h in range(2):
                            i = pe.transpose(wide(bank[1 + k])[:, h, :], rows_f[:, k, h, :], ident[0:HALF, 0:HALF])
                    i.then_inc(cols_ps, 1)
                    pe.wait_ge(const_set, 3)
                    pe.wait_ge(counted, 1)
                    pe.matmul(bank[0][:, 0:1], ones[:, :], n_flags[:, :], start=True, stop=True).then_inc(total, 1)

            end_phase()

            with ExitStack() as fctx:
                def ftmp(name, shape, dt=F32):
                    return fctx.enter_context(nc.sbuf_tensor(name, shape, dt))
                PIECE = E // 5
                all_i = ftmp("all_i", [ROWS, PIECE], I32)
                all_f = ftmp("all_f", [ROWS, PIECE])
                number = ftmp("number", [ROWS, PIECE])
                own = ftmp("own", [ROWS, EDGE_TILES])
                early = ftmp("early", [ROWS, PIECE])
                before = ftmp("before", [ROWS, PIECE])
                own_col = ftmp("own_col", [ROWS, 1])
                neg_dst = ftmp("neg_dst", [ROWS, 1])
                n_before = ftmp("n_before", [ROWS, 1])
                rank = ftmp("rank", [ROWS, EDGE_TILES])
                rank_col = ftmp("rank_col", [ROWS, 1], U32)
                row_out = ftmp("row_out", [ROWS, 4], I32)
                back = ftmp("back", [HALF, 2, ROWS * 4], I32)
                zero, piece_landed, numbered, piece_f, piece_done, ranked, col_set, row_sent, back_landed, chain = map(
                    new_sem, "zero piece_landed numbered piece_f piece_done ranked col_set row_sent back_landed chain".split())
                with nc.Block() as block:
                    @block.gpsimd
                    def _(pool):
                        unsorted = pool.value_load(unsorted_i[0:1, 0:1], min_val=0, max_val=E)
                        with pool.If(unsorted > 0):
                            pool.iota(own[:, :], [[ROWS, EDGE_TILES]], base=0, channel_multiplier=1,
                                      allow_small_or_imprecise_dtypes=True).then_inc(numbered, 1)
                            for piece in range(5):
                                if piece:
                                    pool.wait_ge(piece_done, piece)
                                pool.iota(number[:, :], [[1, PIECE]], base=piece * PIECE, channel_multiplier=0,
                                          allow_small_or_imprecise_dtypes=True).then_inc(numbered, 1)
                                pool.dma_start(all_i[:, :], e_dst[1 + piece * PIECE:1 + (piece + 1) * PIECE]
                                               .partition_broadcast(ROWS)).then_inc(piece_landed, 16)
                            with pool.Fori(0, EDGE_TILES) as t:
                                pool.wait_ge(col_set, t + 1)
                                pass_on(pool, chain)
                                pool.indirect_dma_start(out=sorted_edges, out_offset=bass.IndirectOffsetOnAxis(ap=rank_col[:, 0:1], axis=0),
                                                        in_=row_out[:, :], in_offset=None,
                                                        bounds_check=E - 1, oob_is_err=False).then_inc(row_sent, 16)
                            pool.wait_ge(row_sent, 16 * EDGE_TILES)
                            pool.dma_start(back[:, :, :], sorted_edges.rearrange("(h t p) f -> t h (p f)", h=2, p=ROWS)).then_inc(back_landed, 16)

                    @block.vector
                    def _(dve):
                        unsorted = dve.value_load(unsorted_i[0:1, 0:1], min_val=0, max_val=E)
                        with dve.If(unsorted > 0):
                            dve.memset(rank[:, :], 0.0).then_inc(zero, 1)
                            dve.wait_ge(zero, 1)
                            PER = 6
                            for piece in range(5):
                                dve.wait_ge(piece_landed, 16 * (piece + 1))
                                dve.wait_ge(numbered, piece + 2)
                                dve.tensor_copy(all_f[:, :], all_i[:, :]).then_inc(piece_f, 1)
                                dve.wait_ge(piece_f, piece + 1)
                                with dve.Fori(0, EDGE_TILES) as t:
                                    done = t * PER + piece * PER * EDGE_TILES
                                    dve.tensor_copy(own_col[:, :], own[:, bass.ds(t, 1)]).then_inc(ranked, 1)
                                    dve.tensor_scalar(neg_dst[:, :], cols[:, bass.ds(t, 1), 1], -1.0, None, ALU.mult).then_inc(ranked, 1)
                                    dve.wait_ge(ranked, done + 2)
                                    dve.scalar_tensor_tensor(early[:, :], number[:, :], own_col[:, 0:1], all_f[:, :],
                                                             ALU.is_lt, ALU.subtract).then_inc(ranked, 1)
                                    dve.wait_ge(ranked, done + 3)
                                    dve.tensor_scalar(before[:, :], early[:, :], neg_dst[:, 0:1], None, ALU.is_gt).then_inc(ranked, 1)
                                    dve.wait_ge(ranked, done + 4)
                                    dve.reduce_sum(n_before[:, :], before[:, :], mybir.AxisListType.X).then_inc(ranked, 1)
                                    dve.wait_ge(ranked, done + 5)
                                    dve.tensor_tensor(rank[:, bass.ds(t, 1)], rank[:, bass.ds(t, 1)], n_before[:, :], ALU.add).then_inc(ranked, 1)
                                    dve.wait_ge(ranked, done + 6)
                                dve.sem_inc(piece_done, 1)
                            dve.tensor_copy(rank_col[:, :], rank[:, 0:1])
                            dve.tensor_copy(row_out[:, :], cols[:, 0, :]).then_inc(col_set, 1)
                            with dve.Fori(1, EDGE_TILES) as t:
                                dve.wait_ge(row_sent, t * 16)
                                dve.tensor_copy(rank_col[:, :], rank[:, bass.ds(t, 1)])
                                dve.tensor_copy(row_out[:, :], cols[:, bass.ds(t, 1), :].rearrange("p a f -> p (a f)")).then_inc(col_set, 1)
                            dve.wait_ge(back_landed, 16)
                            for k in range(3):
                                dve.tensor_copy(rows_i[:, k, :, :], back[:, :, :].rearrange("t h (p f) -> t h p f", f=4)[:, :, :, k])

            end_phase()

            landed, dst_stored, near_landed, in_f, near_set, cut_set, keep_set, end_set, stored, idx_ps = map(
                new_sem, "landed2 dst_stored2 near_landed2 in_f2 near_set2 cut_set keep_set end_set stored idx_ps".split())
            with nc.Block() as block:
                @block.sync
                def _(sp):
                    sp.dma_start(tile_rows(e_dst, 1), rows_i[:, D_, :, :]).then_inc(dst_stored, 16)
                    sp.dma_start(tile_rows(e_type), rows_i[:, T_, :, :]).then_inc(stored, 16)
                    sp.wait_ge(dst_stored, 16)
                    sp.dma_start(near_i[:, 0, :, :], tile_rows(e_dst, 0)).then_inc(near_landed, 16)
                    sp.dma_start(near_i[:, 1, :, :], tile_rows(e_dst, 2)).then_inc(near_landed, 16)
                    sp.wait_ge(cut_set, 1)
                    for k in range(2):
                        sp.dma_start(tile_rows(e_keep_cut[k, :]), keep_cut[:, k, :, :]).then_inc(stored, 16)
                    sp.wait_ge(stored, 48)

                @block.vector
                def _(dve):
                    dve.tensor_copy(rows_f[:, :, :, :], rows_i[:, :, :, :]).then_inc(in_f, 1)
                    dve.wait_ge(near_landed, 32)
                    dve.tensor_copy(near_f[:, :, :, :], near_i[:, :, :, :]).then_inc(near_set, 1)
                    dve.wait_ge(in_f, 1)
                    dve.wait_ge(near_set, 1)
                    dve.tensor_tensor(keep_cut[:, 0, :, :], rows_f[:, D_, :, :], near_f[:, 0, :, :], ALU.is_equal).then_inc(keep_set, 1)
                    dve.tensor_tensor(end_row[:, :, :], rows_f[:, D_, :, :], near_f[:, 1, :, :], ALU.is_equal).then_inc(keep_set, 1)
                    dve.wait_ge(keep_set, 2)
                    dve.tensor_scalar(keep_cut[:, 1, :, :], keep_cut[:, 0, :, :], 1.0, FAR, ALU.subtract, ALU.mult).then_inc(cut_set, 1)
                    dve.scalar_tensor_tensor(end_row[:, :, :], end_row[:, :, :], float(SKIP), rows_f[:, D_, :, :],
                                             ALU.mult, ALU.add).then_inc(end_set, 1)
                    dve.wait_ge(idx_ps, 1)
                    for k, o in enumerate((src_idx, dst_idx, end_idx)):
                        dve.tensor_copy(o[:, :], bank[4 + k][0:ROWS, 0:EDGE_TILES])

                @block.tensor
                def _(pe):
                    pe.wait_ge(in_f, 1)
                    pe.wait_ge(end_set, 1)
                    for h in range(2):
                        pe.transpose(wide(bank[4])[:, h, :], rows_f[:, S_, h, :], ident[0:HALF, 0:HALF])
                        pe.transpose(wide(bank[5])[:, h, :], rows_f[:, D_, h, :], ident[0:HALF, 0:HALF])
                        i = pe.transpose(wide(bank[6])[:, h, :], end_row[:, h, :], ident[0:HALF, 0:HALF])
                    i.then_inc(idx_ps, 1)

            end_phase()

        W_sb = sb("W_sb", [F, F])
        Wlog_src = sb("Wlog_src", [F, F])
        Wlog_dst = sb("Wlog_dst", [F, F])
        Wlog_self = sb("Wlog_self", [F, F])
        whh_T = sb("whh_T", [F, 3, F])
        wih_T = sb("wih_T", [F, 3, F])
        bih = sb("bih", [F, 3])
        bhh = sb("bhh", [F, 3])
        bsum = sb("bsum", [F, 3])
        bias_parts = sb("bias_parts", [PARTS, TILES, F], BF16)
        ones_bf = sb("ones_bf", [PARTS, 128], BF16)
        bias_col = sb("bias_col", [F, 1])
        msgW_sb = sb("msgW_sb", [F, ETYPES, F])
        msgb_parts = sb("msgb_parts", [PARTS * ETYPES, F], BF16)
        minus_half = sb("minus_half", [128, 4 * TILES])
        type_id = sb("type_id", [PARTS * ETYPES, 1])
        far_row = sb("far_row", [128, 128])
        head_sel = sb("head_sel", [F, HEADS])
        with ExitStack() as sctx:
            def tmp(name, shape, dt=F32):
                return sctx.enter_context(nc.sbuf_tensor(name, shape, dt))
            wt_rows = tmp("wt_rows", [F, 6, F])
            att_col = tmp("att_col", [F, 2])
            head_of = tmp("head_of", [F, F])
            att_blk = tmp("att_blk", [F, 2, F])
            W_T = tmp("W_T", [F, F])
            G = PARTS * ETYPES
            bias_all = tmp("bias_all", [PARTS, TILES * F])
            msgb_all = tmp("msgb_all", [G, F])
            part_of = tmp("part_of", [G, PARTS])
            split = [(tmp(f"part{i}", [P, w], BF16), tmp(f"left{i}", [P, w]), tmp(f"chosen{i}", [P, w]))
                     for i, (P, w) in enumerate(((PARTS, TILES * F), (G, F)))]
            type_sum = tmp("type_sum", [G, 1])
            w_landed, consts, headmask, attblk, wt_ps, wt_sb, log_ps, log_sb, parts, typed = map(
                new_sem, "w_landed consts headmask attblk wt_ps wt_sb log_ps log_sb parts typed".split())
            loads = [(W_sb[:, :], W), (wt_rows[:, 0:3, :], w_ih.rearrange("(g o) k -> o g k", g=3)),
                     (wt_rows[:, 3:6, :], w_hh.rearrange("(g o) k -> o g k", g=3)),
                     (msgW_sb[:, :, :], msg_W.rearrange("t k o -> k t o")),
                     (att_col[:, 0:1], att_src.rearrange("h (c a) -> (h c) a", a=1)),
                     (att_col[:, 1:2], att_dst.rearrange("h (c a) -> (h c) a", a=1)),
                     (bih[:, :], b_ih.rearrange("(g p) -> p g", g=3)), (bhh[:, :], b_hh.rearrange("(g p) -> p g", g=3)),
                     (bias_col[:, :], bias.rearrange("(p a) -> p a", a=1))]
            loads += [(bias_all[:, j * F:(j + 1) * F], bias.partition_broadcast(PARTS)) for j in range(TILES)]
            loads += [(msgb_all[k * ETYPES:(k + 1) * ETYPES, :], msg_b) for k in range(PARTS)]
            with nc.Block() as block:
                @block.sync
                def _(sp):
                    for o, i in loads:
                        with nc.allow_non_contiguous_dma(reason="small"):
                            sp.dma_start(o, i).then_inc(w_landed, 16)

                @block.gpsimd
                def _(pool):
                    pool.memset(minus_half[:, :], -0.5).then_inc(consts, 1)
                    pool.memset(head_of[:, :], 1.0).then_inc(consts, 1)
                    pool.memset(part_of[:, :], 1.0).then_inc(consts, 1)
                    pool.memset(far_row[:, :], 0.0).then_inc(consts, 1)
                    pool.memset(head_sel[:, :], 0.0).then_inc(consts, 1)
                    pool.iota(type_id[:, :], [[0, 1]], base=0, channel_multiplier=1, allow_small_or_imprecise_dtypes=True).then_inc(consts, 1)
                    pool.wait_ge(consts, 6)
                    pool.affine_select(out=far_row[:, :], in_=far_row[:, :], compare_op=ALU.not_equal, fill=-FAR, base=0,
                                       pattern=[[0, 128]], channel_multiplier=1)
                    pool.affine_select(out=part_of[:, :], in_=part_of[:, :], compare_op=ALU.is_ge, fill=0.0, base=0,
                                       pattern=[[-ETYPES, PARTS]], channel_multiplier=1).then_inc(typed, 1)
                    pool.wait_ge(typed, 1)
                    pool.affine_select(out=part_of[:, :], in_=part_of[:, :], compare_op=ALU.is_ge, fill=0.0, base=ETYPES - 1,
                                       pattern=[[ETYPES, PARTS]], channel_multiplier=-1).then_inc(typed, 1)
                    pool.affine_select(out=head_sel[:, :], in_=head_sel[:, :], compare_op=ALU.not_equal, fill=1.0, base=0,
                                       pattern=[[-(F // HEADS), HEADS]], channel_multiplier=1)
                    C = F // HEADS
                    v = head_of[:, :].rearrange("p (h c) -> p h c", h=HEADS)
                    pool.affine_select(out=v, in_=v, compare_op=ALU.is_ge, fill=0.0, base=0,
                                       pattern=[[-C, HEADS], [0, C]], channel_multiplier=1).then_inc(headmask, 1)
                    pool.wait_ge(headmask, 1)
                    pool.affine_select(out=v, in_=v, compare_op=ALU.is_ge, fill=0.0, base=C - 1,
                                       pattern=[[C, HEADS], [0, C]], channel_multiplier=-1).then_inc(headmask, 1)

                @block.vector
                def _(dve):
                    dve.wait_ge(w_landed, 16 * len(loads))
                    dve.wait_ge(headmask, 2)
                    for k in range(2):
                        dve.tensor_scalar(att_blk[:, k, :], head_of[:, :], att_col[:, k:k + 1], None, ALU.mult).then_inc(attblk, 1)
                    dve.tensor_tensor(bsum[:, :], bih[:, :], bhh[:, :], ALU.add)
                    dve.memset(ones_bf[:, :], 1.0)
                    dve.wait_ge(typed, 2)
                    dve.scalar_tensor_tensor(type_sum[:, :], part_of[:, 1:2], -float(ETYPES), type_id[:, :], ALU.mult, ALU.add).then_inc(typed, 1)
                    dve.wait_ge(typed, 3)
                    dve.scalar_tensor_tensor(type_id[:, :], part_of[:, 2:3], -2.0 * ETYPES, type_sum[:, :], ALU.mult, ALU.add)
                    done = 0
                    for (part, left, chosen), value, mine, out_ in zip(split, (bias_all, msgb_all), (ident[0:PARTS, 0:PARTS], part_of[:, :]),
                                                                       (bias_parts[:, :, :].rearrange("p j f -> p (j f)"), msgb_parts[:, :])):
                        for k in range(PARTS):
                            rest = value if k == 0 else left
                            dve.tensor_copy(part[:, :], rest[:, :]).then_inc(parts, 1)
                            dve.wait_ge(parts, done + 1)
                            if k == 0:
                                dve.tensor_scalar(chosen[:, :], part[:, :], mine[:, 0:1], None, ALU.mult).then_inc(parts, 1)
                            else:
                                dve.scalar_tensor_tensor(chosen[:, :], part[:, :], mine[:, k:k + 1], chosen[:, :], ALU.mult, ALU.add).then_inc(parts, 1)
                            dve.tensor_tensor(left[:, :], rest[:, :], part[:, :], ALU.subtract).then_inc(parts, 1)
                            dve.wait_ge(parts, done + 3)
                            done += 3
                        dve.tensor_copy(out_, chosen[:, :])
                    dve.wait_ge(wt_ps, 1)
                    dve.tensor_copy(wih_T[:, :, :], bank[0][:, 0:384].rearrange("p (g k) -> p g k", g=3)).then_inc(wt_sb, 1)
                    dve.tensor_copy(whh_T[:, :, :], bank[1][:, 0:384].rearrange("p (g k) -> p g k", g=3)).then_inc(wt_sb, 1)
                    dve.tensor_copy(W_T[:, :], bank[2][:, 0:F]).then_inc(wt_sb, 1)
                    dve.wait_ge(log_ps, 1)
                    dve.tensor_copy(Wlog_src[:, :], bank[3][:, 0:F]).then_inc(log_sb, 1)
                    dve.tensor_copy(Wlog_dst[:, :], bank[3][:, F:2 * F]).then_inc(log_sb, 1)
                    dve.wait_ge(log_sb, 2)
                    dve.tensor_tensor(Wlog_self[:, :], Wlog_src[:, :], Wlog_dst[:, :], ALU.add)

                @block.tensor
                def _(pe):
                    pe.wait_ge(w_landed, 16 * len(loads))
                    for g in range(3):
                        pe.transpose(bank[0][:, g * F:(g + 1) * F], wt_rows[:, g, :], ident[:, :])
                        pe.transpose(bank[1][:, g * F:(g + 1) * F], wt_rows[:, 3 + g, :], ident[:, :])
                    pe.transpose(bank[2][:, 0:F], W_sb[:, :], ident[:, :]).then_inc(wt_ps, 1)
                    pe.wait_ge(wt_sb, 3)
                    pe.wait_ge(attblk, 2)
                    for k in range(2):
                        mm = pe.matmul(bank[3][:, k * F:(k + 1) * F], W_T[:, :], att_blk[:, k, :], start=True, stop=True)
                    mm.then_inc(log_ps, 1)

        end_phase()

        with ExitStack() as dctx:
            def ring(name, depth, shape, dt=F32):
                return [dctx.enter_context(nc.sbuf_tensor(f"{name}{i}", shape, dt)) for i in range(depth)]

            def sem(name):
                return new_sem(("n_" + name))
            U = 8
            NORM_ACT = 2
            node_major = [ROWS, TILES, F]
            X = ring("nX", 8, node_major)
            HN = ring("nHN", 2, node_major)
            HT = ring("nHT", 2, [F, CHUNK])
            X1 = ring("nX1", 8, node_major)
            H1N = ring("nH1N", 2, node_major)
            H1T = ring("nH1T", 4, [F, CHUNK])
            ST = ring("nST", 4, [ROWS, 2, TILES, 6])
            SS = ring("nSS", 4, [ROWS, 2, TILES])
            MM = ring("nMM", 4, [ROWS, 2, TILES])
            DD = ring("nDD", 4, [ROWS, 2, TILES])
            QQ = ring("nQQ", 4, [ROWS, 2, TILES])
            VE = ring("nVE", 4, [ROWS, 2, TILES])
            RS = ring("nRS", 4, [ROWS, 2, TILES])
            NB = ring("nNB", 4, [ROWS, 2, TILES])
            R = ring("nR", 2, [F, CHUNK])
            Z = ring("nZ", 2, [F, CHUNK])
            NT = ring("nNT", 2, [F, CHUNK])
            NN = ring("nNN", 2, [F, CHUNK])
            D = ring("nD", 2, [F, CHUNK])
            D2 = ring("nD2", 2, [F, CHUNK])
            D3 = ring("nD3", 2, [F, CHUNK])
            OUT = ring("nOUT", 4, node_major)
            x_landed = [sem(f"x_landed{i}") for i in range(8)]
            x1_stored = [sem(f"x1_stored{i}") for i in range(8)]
            out_stored = [sem(f"out_stored{i}") for i in range(4)]
            bn0, sums, squared, ve, rstd, nb, norm1a, norm0, tr0, relu0 = map(
                sem, "bn0 sums squared ve rstd nb norm1a norm0 tr0 relu0".split())
            wmm, x1, bn1, norm1, tr1, relu1 = map(sem, "wmm x1 bn1 norm1 tr1 relu1".split())
            gates, r_ready, z_ready, nt, nn, diff, zdiff, summed, trd, outsum = map(
                sem, "gates r_ready z_ready nt nn diff zdiff summed trd outsum".split())
            sp_passed, filled = map(sem, "sp_passed filled".split())
            P_T0, P_W, P_T1, P_R, P_Z, P_O = bank[0:6]
            P_N = bank[6:8]

            def rows_of(table, c):
                return table[bass.ds(c.n * CHUNK, CHUNK), :].rearrange("(p j) f -> p j f", j=TILES)

            with nc.Block() as block:
                @block.sync
                def _(sp):
                    def load(c):
                        if c.has_before(8):
                            sp.wait_ge(norm0, c.n - 7)
                            sp.wait_ge(x1, c.n - 7)
                            pass_on(sp, sp_passed)
                        sp.dma_start(X[c.slot(8)][:, :, :], rows_of(x, c)).then_inc(x_landed[c.slot(8)], 16)

                    def store_x1(c):
                        sp.wait_ge(x1, c.n + 1)
                        pass_on(sp, sp_passed)
                        sp.dma_start(rows_of(x1_table, c), X1[c.slot(8)][:, :, :]).then_inc(x1_stored[c.slot(8)], 16)

                    def store_out(c):
                        sp.wait_ge(outsum, c.n + 1)
                        pass_on(sp, sp_passed)
                        sp.dma_start(rows_of(out, c), OUT[c.slot(4)][:, :, :]).then_inc(out_stored[c.slot(4)], 16)

                    skewed(sp, NODE_CHUNKS, U, [(0, load), (6, store_x1), (14, store_out)])
                    for i, s in enumerate(x1_stored):
                        sp.wait_ge(s, 16 * fills(NODE_CHUNKS, 8, i))
                    for i, s in enumerate(out_stored):
                        sp.wait_ge(s, 16 * fills(NODE_CHUNKS, 4, i))

                @block.gpsimd
                def _(pool):
                    def rstds(c):
                        b = c.slot(4)
                        pool.wait_ge(ve, c.n + 1)
                        if c.has_before(4):
                            pool.wait_ge(norm0, c.n - 3)
                            pool.wait_ge(nb, c.n - 3)
                        if c.has_before(7):
                            pool.wait_ge(norm1, c.n - 6)
                            pool.wait_ge(norm1a, c.n - 6)
                        pool.tensor_tensor(RS[b][:, :, :], VE[b][:, :, :], minus_half[0:ROWS, 0:2 * TILES].rearrange("p (k j) -> p k j", k=2),
                                           ALU.pow).then_inc(rstd, 1)

                    def h_minus_n(c):
                        b = c.slot(2)
                        pool.wait_ge(nn, c.n + 1)
                        pool.tensor_tensor(D[b][:, :], H1T[c.slot(4)][:, :], NN[b][:, :], ALU.subtract).then_inc(diff, 1)
                        pool.wait_ge(diff, c.n + 1)
                        if c.has_before(2):
                            pool.wait_ge(summed, c.n - 1)
                        pool.tensor_tensor(D2[b][:, :], Z[b][:, :], D[b][:, :], ALU.mult).then_inc(zdiff, 1)

                    skewed(pool, NODE_CHUNKS, U, [(1, rstds, 3), (8, h_minus_n)])

                @block.vector
                def _(dve):
                    for b in range(4):
                        dve.memset(ST[b][:, :, :, :], 1.0).then_inc(filled, 1)
                    dve.wait_ge(filled, 4)

                    def stats_0(c):
                        dve.wait_ge(x_landed[c.slot(8)], 16 * c.uses(8))
                        if c.has_before(4):
                            dve.wait_ge(sums, c.n - 3)
                        for j in range(TILES):
                            i = dve.bn_stats(ST[c.slot(4)][:, 0, j, :], X[c.slot(8)][:, j, :])
                        i.then_inc(bn0, 1)

                    def stats_1(c):
                        dve.wait_ge(x1, c.n + 1)
                        if c.has_before(1):
                            dve.wait_ge(sums, c.n)
                        for j in range(TILES):
                            i = dve.bn_stats(ST[c.before(-3).slot(4)][:, 1, j, :], X1[c.slot(8)][:, j, :])
                        i.then_inc(bn1, 1)

                    def sum_halves(c):
                        b = c.slot(4)
                        if not c.known() or c.n < NODE_CHUNKS:
                            dve.wait_ge(bn0, c.n + 1)
                        if c.has_before(3):
                            dve.wait_ge(bn1, c.n - 2)
                        if c.has_before(4):
                            dve.wait_ge(nb, c.n - 3)
                            dve.wait_ge(ve, c.n - 3)
                        moments(dve, ST[b], SS[b][:, :, :], MM[b][:, :, :], DD[b][:, :, :], sums)

                    def square(c):
                        b = c.slot(4)
                        dve.wait_ge(sums, c.n + 1)
                        dve.scalar_tensor_tensor(QQ[b][:, :, :], DD[b][:, :, :], 0.25, DD[b][:, :, :], ALU.mult, ALU.mult).then_inc(squared, 1)

                    def variance(c):
                        b = c.slot(4)
                        dve.wait_ge(squared, c.n + 1)
                        if c.has_before(4):
                            dve.wait_ge(rstd, c.n - 3)
                        dve.scalar_tensor_tensor(VE[b][:, :, :], SS[b][:, :, :], 1.0 / F, QQ[b][:, :, :], ALU.mult, ALU.add).then_inc(ve, 1)

                    def shift(c):
                        b = c.slot(4)
                        dve.wait_ge(rstd, c.n + 1)
                        if c.has_before(4):
                            dve.wait_ge(norm0, c.n - 3)
                        if c.has_before(7):
                            dve.wait_ge(norm1, c.n - 6)
                            dve.wait_ge(norm1a, c.n - 6)
                        dve.scalar_tensor_tensor(NB[b][:, :, :], MM[b][:, :, :], -0.5, RS[b][:, :, :], ALU.mult, ALU.mult).then_inc(nb, 1)

                    def add_x1(c):
                        dve.wait_ge(wmm, c.n + 1)
                        if c.has_before(8):
                            dve.wait_ge(x1_stored[c.slot(8)], 16 * (c.uses(8) - 1))
                            dve.wait_ge(outsum, c.n - 7)
                        dve.tensor_tensor(X1[c.slot(8)][:, :, :], P_W[0:ROWS, :].rearrange("p (j f) -> p j f", j=TILES),
                                          X[c.slot(8)][:, :, :], ALU.add).then_inc(x1, 1)

                    def norm_1(c):
                        b = c.before(-3).slot(4)
                        dve.wait_ge(nb, c.n + 4)
                        if c.has_before(2):
                            dve.wait_ge(tr1, c.n - 1)
                        for j in range(NORM_ACT, TILES):
                            i = dve.tensor_scalar(H1N[c.slot(2)][:, j, :], X1[c.slot(8)][:, j, :], RS[b][:, 1, j:j + 1], NB[b][:, 1, j:j + 1],
                                                  ALU.mult, ALU.add)
                        i.then_inc(norm1, 1)

                    def reset_gate(c):
                        dve.wait_ge(gates, c.n + 1)
                        dve.wait_ge(r_ready, c.n + 1)
                        if c.has_before(2):
                            dve.wait_ge(nn, c.n - 1)
                        dve.scalar_tensor_tensor(NT[c.slot(2)][:, :], P_N[c.slot(2)][:, 0:CHUNK], bhh[:, 2:3], R[c.slot(2)][:, :],
                                                 ALU.add, ALU.mult).then_inc(nt, 1)

                    def mix(c):
                        b = c.slot(2)
                        dve.wait_ge(zdiff, c.n + 1)
                        if c.has_before(2):
                            dve.wait_ge(trd, c.n - 1)
                        dve.tensor_tensor(D3[b][:, :], D2[b][:, :], NN[b][:, :], ALU.add).then_inc(summed, 1)

                    def add_out(c):
                        b = c.slot(4)
                        dve.wait_ge(trd, c.n + 1)
                        if c.has_before(4):
                            dve.wait_ge(out_stored[b], 16 * (c.uses(4) - 1))
                        dve.tensor_tensor(OUT[b][:, :, :], P_O[0:ROWS, :].rearrange("p (j f) -> p j f", j=TILES),
                                          X1[c.slot(8)][:, :, :], ALU.add).then_inc(outsum, 1)

                    skewed(dve, NODE_CHUNKS, U, [(2, shift, 3), (1, square, 3), (0, stats_0), (1, variance, 3), (5, norm_1),
                                                 (11, add_out), (9, mix), (3, add_x1), (3, stats_1), (7, reset_gate),
                                                 (0, sum_halves, 3)])

                @block.scalar
                def _(act):
                    def norm_0(c):
                        b = c.slot(4)
                        act.wait_ge(nb, c.n + 1)
                        if c.has_before(2):
                            act.wait_ge(tr0, c.n - 1)
                        for j in range(TILES):
                            i = act.activation(HN[c.slot(2)][:, j, :], X[c.slot(8)][:, j, :], ACT.Identity, bias=NB[b][:, 0, j:j + 1],
                                               scale=RS[b][:, 0, j:j + 1])
                        i.then_inc(norm0, 1)

                    def norm_1(c):
                        b = c.before(-3).slot(4)
                        act.wait_ge(nb, c.n + 4)
                        if c.has_before(2):
                            act.wait_ge(tr1, c.n - 1)
                        for j in range(NORM_ACT):
                            i = act.activation(H1N[c.slot(2)][:, j, :], X1[c.slot(8)][:, j, :], ACT.Identity, bias=NB[b][:, 1, j:j + 1],
                                               scale=RS[b][:, 1, j:j + 1])
                        i.then_inc(norm1a, 1)

                    def relu_0(c):
                        act.wait_ge(tr0, c.n + 1)
                        if c.has_before(2):
                            act.wait_ge(wmm, c.n - 1)
                        act.activation(HT[c.slot(2)][:, :], P_T0[:, 0:CHUNK], ACT.Relu).then_inc(relu0, 1)

                    def relu_1(c):
                        act.wait_ge(tr1, c.n + 1)
                        if c.has_before(4):
                            act.wait_ge(gates, c.n - 3)
                            act.wait_ge(diff, c.n - 3)
                        act.activation(H1T[c.slot(4)][:, :], P_T1[:, 0:CHUNK], ACT.Relu).then_inc(relu1, 1)

                    def sigmoids(c):
                        b = c.slot(2)
                        act.wait_ge(gates, c.n + 1)
                        if c.has_before(2):
                            act.wait_ge(nt, c.n - 1)
                            act.wait_ge(zdiff, c.n - 1)
                        act.activation(R[b][:, :], P_R[:, 0:CHUNK], ACT.Sigmoid, bias=bsum[:, 0:1]).then_inc(r_ready, 1)
                        act.activation(Z[b][:, :], P_Z[:, 0:CHUNK], ACT.Sigmoid, bias=bsum[:, 1:2]).then_inc(z_ready, 1)

                    def tanh(c):
                        b = c.slot(2)
                        act.wait_ge(nt, c.n + 1)
                        if c.has_before(2):
                            act.wait_ge(summed, c.n - 1)
                            act.wait_ge(diff, c.n - 1)
                        act.activation(NN[b][:, :], NT[b][:, :], ACT.Tanh, bias=bih[:, 2:3]).then_inc(nn, 1)

                    skewed(act, NODE_CHUNKS, U, [(3, relu_0), (8, tanh), (5, norm_1), (2, norm_0), (7, sigmoids), (5, relu_1)])

                @block.tensor
                def _(pe):
                    def transposes(bank_, S, done):
                        for j in range(TILES):
                            i = pe.transpose(bank_[:, j * ROWS:(j + 1) * ROWS], S[:, j, :], ident[0:ROWS, 0:ROWS])
                        i.then_inc(done, 1)

                    def tr_0(c):
                        pe.wait_ge(norm0, c.n + 1)
                        if c.has_before(1):
                            pe.wait_ge(relu0, c.n)
                        transposes(P_T0, HN[c.slot(2)], tr0)

                    def w_mm(c):
                        if c.has_before(1):
                            pe.wait_ge(x1, c.n)
                        pe.matmul(P_W[0:ROWS, :], ones_bf[:, 0:ROWS], bias_parts[:, :, :].rearrange("p j f -> p (j f)"), start=True, stop=False)
                        pe.wait_ge(relu0, c.n + 1)
                        for j in range(TILES):
                            i = pe.matmul(P_W[0:ROWS, j * F:(j + 1) * F], HT[c.slot(2)][:, j * ROWS:(j + 1) * ROWS], W_sb[:, :],
                                          start=False, stop=(j == TILES - 1))
                        i.then_inc(wmm, 1)

                    def tr_1(c):
                        pe.wait_ge(norm1, c.n + 1)
                        pe.wait_ge(norm1a, c.n + 1)
                        if c.has_before(1):
                            pe.wait_ge(relu1, c.n)
                        transposes(P_T1, H1N[c.slot(2)], tr1)

                    def gate_mm(c):
                        pe.wait_ge(relu1, c.n + 1)
                        if c.has_before(1):
                            pe.wait_ge(r_ready, c.n)
                            pe.wait_ge(z_ready, c.n)
                        if c.has_before(2):
                            pe.wait_ge(nt, c.n - 1)
                        for g, P in enumerate((P_R, P_Z, P_N[c.slot(2)])):
                            i = pe.matmul(P[:, 0:CHUNK], whh_T[:, g, :], H1T[c.slot(4)][:, :], start=True, stop=True)
                        i.then_inc(gates, 1)

                    def tr_out(c):
                        pe.wait_ge(summed, c.n + 1)
                        if c.has_before(1):
                            pe.wait_ge(outsum, c.n)
                        for j in range(TILES):
                            i = pe.transpose(P_O[0:ROWS, j * F:(j + 1) * F], D3[c.slot(2)][:, j * ROWS:(j + 1) * ROWS], ident[:, :])
                        i.then_inc(trd, 1)

                    skewed(pe, NODE_CHUNKS, U, [(7, gate_mm), (3, w_mm), (5, tr_1), (10, tr_out), (2, tr_0)])

        end_phase()

        U = 8

        class EdgeFront:

            def __init__(self, memory, pre):
                def ring(name, depth, shape, dt=F32):
                    return [memory.enter_context(nc.sbuf_tensor(f"{pre}{name}{i}", shape, dt)) for i in range(depth)]

                def sem(name):
                    return new_sem((f"{pre}_{name}"))
                self.ring, self.sem = ring, sem
                self.XS = ring("XS", 4, [ROWS, TILES, F])
                self.XD = ring("XD", 8 if pre == "g" else 4, [ROWS, TILES, F])
                self.HN = ring("HN", 2, [ROWS, 2 * TILES, F])
                self.H = ring("H", 4 if pre == "g" else 8, [F, 2, CHUNK])
                self.ST = ring("ST", 2, [ROWS, 2 * TILES, 6])
                self.SS = ring("SS", 2, [ROWS, 2 * TILES])
                self.MM = ring("MM", 4, [ROWS, 2 * TILES])
                self.DD = ring("DD", 2, [ROWS, 2 * TILES])
                self.QQ = ring("QQ", 2, [ROWS, 2 * TILES])
                self.VE = ring("VE", 2, [ROWS, 2, 2 * TILES])
                self.RS = ring("RS", 2, [ROWS, 2, 2 * TILES])
                self.NB = ring("NB", 2, [ROWS, 2 * TILES])
                self.IX = ring("IX", 4, [ROWS, 2 * TILES], U32)
                self.IE = ring("IE", 4, [ROWS, TILES], U32)
                self.KC = ring("KC", 4, [F, 2, CHUNK])
                self.OUT = ring("OUT", 4, [ROWS, TILES, F])
                self.gathered = [sem(f"gathered{i}") for i in range(4)]
                self.own_landed = [sem(f"own_landed{i}") for i in range(4)]
                self.kc_landed = [sem(f"kc_landed{i}") for i in range(4)]
                self.scattered = [sem(f"scattered{i}") for i in range(4)]
                self.sp_passed, self.pool_passed = sem("sp_passed"), sem("pool_passed")
                self.idx, self.ends = sem("idx"), sem("ends")
                self.bn, self.sums, self.squared = sem("bn"), sem("sums"), sem("squared")
                self.ve, self.rstd, self.nb = sem("ve"), sem("rstd"), sem("nb")
                self.norm, self.tr, self.relu = sem("norm"), sem("tr"), sem("relu")
                self.x_out = sem("x_out")

        def load_keep_cut(sp, s, c, used):
            b = c.slot(4)
            if c.has_before(4):
                for u in used:
                    sp.wait_ge(u, c.n - 3)
                pass_on(sp, s.sp_passed)
            sp.dma_start(s.KC[b][:, :, :], e_keep_cut[:, bass.ds(c.n * CHUNK, CHUNK)].partition_broadcast(128)).then_inc(s.kc_landed[b], 16)

        def rows_at(s, c, j):
            X = s.XS if j < TILES else s.XD
            return X[c.slot(len(X))][:, j % TILES, :]

        def gather(pool, s, c, table, tiles):
            b = c.slot(4)
            pool.wait_ge(s.idx, c.n + 1)
            if c.has_before(4):
                pool.wait_ge(s.norm, c.n - 3)
            pass_on(pool, s.pool_passed)
            for j in range(tiles):
                if j == TILES and c.has_before(8):
                    pool.wait_ge(s.x_out, c.n - 7)
                    pass_on(pool, s.pool_passed)
                pool.indirect_dma_start(out=rows_at(s, c, j), out_offset=None, in_=table,
                                        in_offset=bass.IndirectOffsetOnAxis(ap=s.IX[b][:, j:j + 1], axis=0),
                                        bounds_check=N - 1, oob_is_err=False).then_inc(s.gathered[b], 16)

        def edge_rstd(pool, s, c):
            if c.slot(2) == 0:
                return
            p = c.slot(4) // 2
            pool.wait_ge(s.ve, c.n + 1)
            if c.has_before(4):
                pool.wait_ge(s.norm, c.n - 3)
                pool.wait_ge(s.nb, c.n - 3)
            pool.tensor_tensor(s.RS[p][:, :, :], s.VE[p][:, :, :], minus_half[0:ROWS, :].rearrange("p (k j) -> p k j", k=2),
                               ALU.pow).then_inc(s.rstd, 1)

        def scatter(pool, s, c, to):
            b = c.slot(4)
            pool.wait_ge(s.x_out, c.n + 1)
            pool.wait_ge(s.ends, c.n + 1)
            pass_on(pool, s.pool_passed)
            for j in range(TILES):
                pool.indirect_dma_start(out=to, out_offset=bass.IndirectOffsetOnAxis(ap=s.IE[b][:, j:j + 1], axis=0),
                                        in_=s.OUT[b][:, j, :], in_offset=None,
                                        bounds_check=N - 1, oob_is_err=False).then_inc(s.scattered[b], 16)

        def edge_index(dve, s, c, tiles):
            b = c.slot(4)
            if c.has_before(4):
                dve.wait_ge(s.gathered[b], 16 * tiles * (c.uses(4) - 1))
            i = dve.tensor_copy(s.IX[b][:, 0:TILES], src_idx[:, bass.ds(c.n * TILES, TILES)])
            if tiles > TILES:
                i = dve.tensor_copy(s.IX[b][:, TILES:2 * TILES], dst_idx[:, bass.ds(c.n * TILES, TILES)])
            i.then_inc(s.idx, 1)

        AHEAD = 2

        def first_indices(dve, s, tiles):
            for n in range(AHEAD):
                edge_index(dve, s, Step(U, 0, n), tiles)

        def next_index(dve, s, c, tiles):
            c = c.before(-AHEAD)
            if not c.known() or c.n < EDGE_CHUNKS:
                edge_index(dve, s, c, tiles)

        def edge_ends(dve, s, c):
            b = c.slot(4)
            if c.has_before(4):
                dve.wait_ge(s.scattered[b], 16 * TILES * (c.uses(4) - 1))
            dve.tensor_copy(s.IE[b][:, :], end_idx[:, bass.ds(c.n * TILES, TILES)]).then_inc(s.ends, 1)

        def edge_stats(dve, s, c, tiles):
            b = c.slot(2)
            dve.wait_ge(s.gathered[c.slot(4)], 16 * tiles * c.uses(4))
            if tiles == TILES:
                dve.wait_ge(s.own_landed[c.slot(4)], 16 * c.uses(4))
            if c.has_before(2):
                dve.wait_ge(s.sums, c.n - 1)
            for j in range(2 * TILES):
                i = dve.bn_stats(s.ST[b][:, j, :], rows_at(s, c, j))
            i.then_inc(s.bn, 1)

        def edge_sums(dve, s, c):
            b = c.slot(2)
            dve.wait_ge(s.bn, c.n + 1)
            if c.has_before(4):
                dve.wait_ge(s.nb, c.n - 3)
            if c.has_before(2):
                dve.wait_ge(s.ve, c.n - 1)
            moments(dve, s.ST[b], s.SS[b][:, :], s.MM[c.slot(4)][:, :], s.DD[b][:, :], s.sums)

        def edge_square(dve, s, c):
            b = c.slot(2)
            dve.wait_ge(s.sums, c.n + 1)
            dve.scalar_tensor_tensor(s.QQ[b][:, :], s.DD[b][:, :], 0.25, s.DD[b][:, :], ALU.mult, ALU.mult).then_inc(s.squared, 1)

        def edge_variance(dve, s, c):
            b = c.slot(2)
            dve.wait_ge(s.squared, c.n + 1)
            if c.has_before(4):
                dve.wait_ge(s.rstd, c.uses(2) - 2)
            dve.scalar_tensor_tensor(s.VE[c.slot(4) // 2][:, b, :], s.SS[b][:, :], 1.0 / F, s.QQ[b][:, :], ALU.mult, ALU.add).then_inc(s.ve, 1)

        def edge_shift(dve, s, c):
            b = c.slot(2)
            dve.wait_ge(s.rstd, c.uses(2))
            if c.has_before(2):
                dve.wait_ge(s.norm, c.n - 1)
            dve.scalar_tensor_tensor(s.NB[b][:, :], s.MM[c.slot(4)][:, :], -0.5, s.RS[c.slot(4) // 2][:, b, :], ALU.mult, ALU.mult).then_inc(s.nb, 1)

        def edge_norm(act, s, c):
            b = c.slot(2)
            act.wait_ge(s.nb, c.n + 1)
            if c.has_before(2):
                act.wait_ge(s.tr, c.n - 1)
            for j in range(2 * TILES):
                i = act.activation(s.HN[b][:, j, :], rows_at(s, c, j), ACT.Identity, bias=s.NB[b][:, j:j + 1],
                                   scale=s.RS[c.slot(4) // 2][:, b, j:j + 1])
            i.then_inc(s.norm, 1)

        def edge_transposes(pe, s, c, banks):
            b = c.slot(2)
            pe.wait_ge(s.norm, c.n + 1)
            if c.has_before(1):
                pe.wait_ge(s.relu, c.n)
            for j in range(2 * TILES):
                i = pe.transpose(banks[j // TILES][:, j % TILES * ROWS:(j % TILES + 1) * ROWS], s.HN[b][:, j, :], ident[0:ROWS, 0:ROWS])
            i.then_inc(s.tr, 1)

        def edge_relu(act, s, c, banks, used):
            act.wait_ge(s.tr, c.n + 1)
            depth = len(s.H)
            if c.has_before(depth):
                for u in used:
                    act.wait_ge(u, c.n + 1 - depth)
            for k in range(2):
                i = act.activation(s.H[c.slot(len(s.H))][:, k, :], banks[k][:, 0:CHUNK], ACT.Relu)
            i.then_inc(s.relu, 1)

        def wait_scatters(pool, s):
            for i, m in enumerate(s.scattered):
                pool.wait_ge(m, 16 * TILES * fills(EDGE_CHUNKS, 4, i))

        def chunk_rows(table, c):
            return table[bass.ds(c.n * CHUNK, CHUNK), :].rearrange("(j p) f -> p j f", p=ROWS)

        with ExitStack() as gctx:
            s = EdgeFront(gctx, "g")
            ring, sem = s.ring, s.sem
            LR = ring("LR", 2, [F, 2, CHUNK])
            L = ring("L", 1, [F, 2, CHUNK])[0]
            TOP = ring("TOP", 1, [F, CHUNK])[0]
            LIFT = ring("LIFT", 1, [F, CHUNK])[0]
            MX = ring("MX", 1, [F, CHUNK + 1])[0]
            ARG = ring("ARG", 2, [F, 3, CHUNK])
            EX = ring("EX", 2, [F, 3, CHUNK])
            PV = ring("PV", 1, [F, CHUNK])[0]
            QV = ring("QV", 1, [F, CHUNK])[0]
            UV = ring("UV", 1, [F, CHUNK])[0]
            PQ = ring("PQ", 2, [F, CHUNK])
            ACC = ring("ACC", 2, [F, CHUNK])
            DEN = ring("DEN", 2, [F, CHUNK])
            DENS = ring("DENS", 1, [ROWS, TILES * HEADS])[0]
            RD = ring("RD", 2, [ROWS, TILES * HEADS])
            SCALED = ring("SCALED", 2, [ROWS, TILES * F])
            (values, lmm, logits, leaky, top, lift, mx, arg, ex, carry, pv, uv, acc, den, dens, rd, scaled, tro, pq) = map(
                sem, "values lmm logits leaky top lift mx arg ex carry pv uv acc den dens rd scaled tro pq".split())
            own_stored = [sem(f"own_stored{i}") for i in range(4)]
            P_S, P_D, P_VS, P_VD, P_E, P_SELF, P_O, P_DEN = bank
            with nc.Block() as block:
                @block.sync
                def _(sp):
                    def store_own(c):
                        sp.wait_ge(s.x_out, c.n + 1)
                        pass_on(sp, s.sp_passed)
                        sp.dma_start(chunk_rows(x1_edges, c), s.OUT[c.slot(4)][:, :, :]).then_inc(own_stored[c.slot(4)], 16)
                    skewed(sp, EDGE_CHUNKS, U, [(2, lambda c: load_keep_cut(sp, s, c, (lmm, mx, lift))), (9, store_own)])
                    for i, m in enumerate(own_stored):
                        sp.wait_ge(m, 16 * fills(EDGE_CHUNKS, 4, i))

                @block.gpsimd
                def _(pool):
                    skewed(pool, EDGE_CHUNKS, U, [(0, lambda c: gather(pool, s, c, x, 2 * TILES)),
                                                  (1, lambda c: edge_rstd(pool, s, c)),
                                                  (9, lambda c: scatter(pool, s, c, x1_table))])
                    wait_scatters(pool, s)

                @block.tensor
                def _(pe):
                    def logit_mm(c):
                        b = c.slot(4)
                        pe.wait_ge(s.relu, c.n + 1)
                        if c.has_before(1):
                            pe.wait_ge(logits, 2 * c.n)
                        pe.matmul(P_E[:, 0:CHUNK], Wlog_src[:, :], s.H[b][:, 0, :], start=True, stop=False)
                        pe.matmul(P_E[:, 0:CHUNK], Wlog_dst[:, :], s.H[b][:, 1, :], start=False, stop=True)
                        pe.matmul(P_SELF[:, 0:CHUNK], Wlog_self[:, :], s.H[b][:, 1, :], start=True, stop=False)
                        pe.wait_ge(s.kc_landed[b], 16 * c.uses(4))
                        pe.matmul(P_SELF[:, 0:CHUNK], far_row[:, :], s.KC[b][:, 0, :], start=False, stop=True).then_inc(lmm, 1)

                    def value_mm(c):
                        b = c.slot(4)
                        if c.has_before(1):
                            pe.wait_ge(pv, 2 * c.n)
                        pe.matmul(P_VS[:, 0:CHUNK], W_sb[:, :], s.H[b][:, 0, :], start=True, stop=True)
                        pe.matmul(P_VD[:, 0:CHUNK], W_sb[:, :], s.H[b][:, 1, :], start=True, stop=True).then_inc(values, 1)

                    def tr_out(c):
                        b = c.slot(2)
                        pe.wait_ge(den, c.n + 1)
                        if c.has_before(1):
                            pe.wait_ge(scaled, c.n)
                        for j in range(TILES):
                            pe.matmul(P_DEN[0:ROWS, j * HEADS:(j + 1) * HEADS], DEN[b][:, j * ROWS:(j + 1) * ROWS], head_sel[:, :],
                                      start=True, stop=True)
                        pe.wait_ge(acc, c.n + 1)
                        for j in range(TILES):
                            i = pe.transpose(P_O[0:ROWS, j * F:(j + 1) * F], ACC[b][:, j * ROWS:(j + 1) * ROWS], ident[:, :])
                        i.then_inc(tro, 1)

                    skewed(pe, EDGE_CHUNKS, U, [(4, logit_mm), (3, lambda c: edge_transposes(pe, s, c, (P_S, P_D))), (5, value_mm),
                                                (6, tr_out)])

                @block.scalar
                def _(act):
                    def raw_logits(c):
                        b = c.slot(2)
                        act.wait_ge(lmm, c.n + 1)
                        if c.has_before(2):
                            act.wait_ge(leaky, c.n - 1)
                        act.activation(LR[b][:, 0, :], P_E[:, 0:CHUNK], ACT.Copy).then_inc(logits, 1)
                        act.activation(LR[b][:, 1, :], P_SELF[:, 0:CHUNK], ACT.Copy).then_inc(logits, 1)

                    def exps(c):
                        b = c.slot(2)
                        act.wait_ge(arg, 3 * (c.n + 1))
                        if c.has_before(2):
                            act.wait_ge(acc, c.n - 1)
                            act.wait_ge(pq, c.n - 1)
                        act.activation(EX[b][:, :, :], ARG[b][:, :, :], ACT.Exp).then_inc(ex, 1)

                    def divide(c):
                        b = c.slot(2)
                        C = F // HEADS
                        act.wait_ge(rd, c.n + 1)
                        if c.has_before(2):
                            act.wait_ge(s.x_out, c.n - 1)
                        for k in range(TILES * HEADS):
                            i = act.activation(SCALED[b][:, k * C:(k + 1) * C], P_O[0:ROWS, k * C:(k + 1) * C], ACT.Copy,
                                               scale=RD[b][:, k:k + 1])
                        i.then_inc(scaled, 1)

                    skewed(act, EDGE_CHUNKS, U, [(3, lambda c: edge_norm(act, s, c)), (7, divide), (4, raw_logits),
                                                 (3, lambda c: edge_relu(act, s, c, (P_S, P_D), (values, lmm))), (5, exps)])

                @block.vector
                def _(dve):
                    def attend(c):
                        new = not c.known() or c.n < EDGE_CHUNKS
                        old = c.has_before(1)
                        b = c.slot(2)
                        o = 1 - b
                        KC = s.KC[c.slot(4)]
                        d = c.before(1)
                        first = d.known() and d.n == 0
                        if old:
                            dve.wait_ge(ex, d.n + 1)
                            dve.tensor_tensor(PQ[o][:, :], EX[o][:, 0, :], EX[o][:, 1, :], ALU.add).then_inc(pq, 1)
                        if new:
                            dve.wait_ge(logits, 2 * (c.n + 1))
                            dve.scalar_tensor_tensor(L[:, :, :], LR[b][:, :, :], SLOPE, LR[b][:, :, :], ALU.mult, ALU.max).then_inc(leaky, 1)
                            if c.known() and c.n == 0:
                                dve.memset(MX[:, 0:1], 0.0).then_inc(carry, 1)
                            else:
                                dve.tensor_copy(MX[:, 0:1], MX[:, CHUNK:CHUNK + 1]).then_inc(carry, 1)
                        if old:
                            dve.wait_ge(values, d.n + 1)
                            dve.scalar_tensor_tensor(PV[:, :], P_VS[:, 0:CHUNK], bias_col[:, 0:1], EX[o][:, 0, :],
                                                     ALU.add, ALU.mult).then_inc(pv, 1)
                        if new:
                            dve.wait_ge(leaky, c.n + 1)
                            dve.tensor_tensor(TOP[:, :], L[:, 0, :], L[:, 1, :], ALU.max).then_inc(top, 1)
                        if old:
                            dve.scalar_tensor_tensor(QV[:, :], P_VD[:, 0:CHUNK], bias_col[:, 0:1], EX[o][:, 1, :],
                                                     ALU.add, ALU.mult).then_inc(pv, 1)
                        if new:
                            dve.wait_ge(s.kc_landed[c.slot(4)], 16 * c.uses(4))
                            dve.wait_ge(top, c.n + 1)
                            dve.wait_ge(carry, c.n + 1)
                            dve.tensor_tensor_scan(MX[:, 1:CHUNK + 1], KC[:, 1, :], TOP[:, :], MX[:, 0:1], ALU.add, ALU.max).then_inc(mx, 1)
                        if old:
                            dve.wait_ge(pq, d.n + 1)
                            if not first:
                                dve.wait_ge(den, d.n)
                            if d.has_before(2):
                                dve.wait_ge(tro, d.n - 1)
                            dve.tensor_tensor_scan(DEN[o][:, :], EX[o][:, 2, :], PQ[o][:, :], 0.0 if first else DEN[b][:, CHUNK - 1:CHUNK],
                                                   ALU.mult, ALU.add).then_inc(den, 1)
                        if new:
                            dve.wait_ge(mx, c.n + 1)
                            dve.tensor_tensor(LIFT[:, :], KC[:, 1, :], MX[:, 0:CHUNK], ALU.add).then_inc(lift, 1)
                        if old:
                            dve.wait_ge(pv, 2 * (d.n + 1))
                            dve.tensor_tensor(UV[:, :], PV[:, :], QV[:, :], ALU.add).then_inc(uv, 1)
                        if new:
                            if c.has_before(2):
                                dve.wait_ge(ex, c.n - 1)
                            dve.wait_ge(lift, c.n + 1)
                            dve.tensor_tensor(ARG[b][:, 2, :], LIFT[:, :], MX[:, 1:CHUNK + 1], ALU.subtract).then_inc(arg, 1)
                        if old:
                            dve.wait_ge(uv, d.n + 1)
                            if not first:
                                dve.wait_ge(acc, d.n)
                            dve.tensor_tensor_scan(ACC[o][:, :], EX[o][:, 2, :], UV[:, :], 0.0 if first else ACC[b][:, CHUNK - 1:CHUNK],
                                                   ALU.mult, ALU.add).then_inc(acc, 1)
                        if new:
                            dve.tensor_tensor(ARG[b][:, 0, :], L[:, 0, :], MX[:, 1:CHUNK + 1], ALU.subtract).then_inc(arg, 1)
                            dve.tensor_tensor(ARG[b][:, 1, :], L[:, 1, :], MX[:, 1:CHUNK + 1], ALU.subtract).then_inc(arg, 1)

                    def weight_sums(c):
                        dve.wait_ge(tro, c.n + 1)
                        dve.tensor_scalar(DENS[:, :], P_DEN[0:ROWS, 0:TILES * HEADS], 1e-16, None, ALU.add).then_inc(dens, 1)

                    def reciprocals(c):
                        dve.wait_ge(dens, c.n + 1)
                        if c.has_before(2):
                            dve.wait_ge(scaled, c.n - 1)
                        dve.reciprocal(RD[c.slot(2)][:, :], DENS[:, :]).then_inc(rd, 1)

                    def add_rows(c):
                        b = c.slot(4)
                        dve.wait_ge(scaled, c.n + 1)
                        if c.has_before(4):
                            dve.wait_ge(s.scattered[b], 16 * TILES * (c.uses(4) - 1))
                            dve.wait_ge(own_stored[b], 16 * (c.uses(4) - 1))
                        dve.tensor_tensor(s.OUT[b][:, :, :], SCALED[c.slot(2)][:, :].rearrange("p (j f) -> p j f", j=TILES),
                                          s.XD[c.slot(8)][:, :, :],
                                          ALU.add).then_inc(s.x_out, 1)

                    first_indices(dve, s, 2 * TILES)
                    skewed(dve, EDGE_CHUNKS, U, [(0, lambda c: next_index(dve, s, c, 2 * TILES)), (3, lambda c: edge_shift(dve, s, c)),
                                                 (7, weight_sums), (1, lambda c: edge_stats(dve, s, c, 2 * TILES)),
                                                 (7, reciprocals), (1, lambda c: edge_sums(dve, s, c)),
                                                 (7, lambda c: edge_ends(dve, s, c)), (1, lambda c: edge_square(dve, s, c)),
                                                 (1, lambda c: edge_variance(dve, s, c)), (5, attend, 1), (7, add_rows)])

        end_phase()

        with ExitStack() as mctx:
            s = EdgeFront(mctx, "m")
            ring, sem = s.ring, s.sem
            TYPE = ring("TYPE", 4, [128, CHUNK], I32)
            HOT = ring("HOT", 2, [PARTS * ETYPES, CHUNK], BF16)
            HM = ring("HM", 2 * ETYPES, [F, CHUNK])
            MS = ring("MS", 2, [F, CHUNK])
            R = ring("R", 2, [F, CHUNK])
            Z = ring("Z", 2, [F, CHUNK])
            NT = ring("NT", 1, [F, CHUNK])[0]
            NT2 = ring("NT2", 2, [F, CHUNK])
            NN = ring("NN", 2, [F, CHUNK])
            D = ring("D", 2, [F, CHUNK])
            D2 = ring("D2", 2, [F, CHUNK])
            D3 = ring("D3", 2, [F, CHUNK])
            X1 = ring("X1", 4, [ROWS, TILES, F])
            type_landed = [sem(f"type_landed{i}") for i in range(4)]
            x1_landed = [sem(f"x1_landed{i}") for i in range(4)]
            masked, hot, msg_used, msg, msum, gates, r_ready, z_ready, nt, nt2, nn, diff, zdiff, summed, tro = map(
                sem, "masked hot msg_used msg msum gates r_ready z_ready nt nt2 nn diff zdiff summed tro".split())
            P_S, P_D, P_M, P_R, P_Z, P_NI, P_NH, P_O = bank
            with nc.Block() as block:
                @block.sync
                def _(sp):
                    def load_own(c):
                        b = c.slot(4)
                        if c.has_before(4):
                            sp.wait_ge(s.norm, c.n - 3)
                            pass_on(sp, s.sp_passed)
                        sp.dma_start(s.XD[b][:, :, :], chunk_rows(x1_edges, c)).then_inc(s.own_landed[b], 16)

                    def load_types(c):
                        b = c.slot(4)
                        if c.has_before(4):
                            sp.wait_ge(masked, ETYPES * (c.n - 3))
                            sp.wait_ge(hot, c.n - 3)
                            pass_on(sp, s.sp_passed)
                        sp.dma_start(TYPE[b][:, :], e_type[bass.ds(c.n * CHUNK, CHUNK)].partition_broadcast(128)).then_inc(type_landed[b], 16)

                    def load_x1(c):
                        b = c.slot(4)
                        if c.has_before(4):
                            sp.wait_ge(s.x_out, c.n - 3)
                            pass_on(sp, s.sp_passed)
                        sp.dma_start(X1[b][:, :, :], chunk_rows(x1_edges, c)).then_inc(x1_landed[b], 16)

                    skewed(sp, EDGE_CHUNKS, U, [(0, load_own), (3, load_types), (4, lambda c: load_keep_cut(sp, s, c, (msum,))), (8, load_x1)])

                @block.gpsimd
                def _(pool):
                    def h_minus_n(c):
                        b = c.slot(2)
                        pool.wait_ge(nn, c.n + 1)
                        pool.tensor_tensor(D[b][:, :], s.H[c.slot(len(s.H))][:, 1, :], NN[b][:, :], ALU.subtract).then_inc(diff, 1)
                        pool.wait_ge(diff, c.n + 1)
                        if c.has_before(2):
                            pool.wait_ge(summed, c.n - 1)
                        pool.tensor_tensor(D2[b][:, :], Z[b][:, :], D[b][:, :], ALU.mult).then_inc(zdiff, 1)

                    skewed(pool, EDGE_CHUNKS, U, [(8, h_minus_n), (11, lambda c: scatter(pool, s, c, out)),
                                                  (0, lambda c: gather(pool, s, c, x1_table, TILES)),
                                                  (2, lambda c: edge_rstd(pool, s, c))])
                    wait_scatters(pool, s)

                @block.tensor
                def _(pe):
                    def messages(c):
                        if c.has_before(1):
                            pe.wait_ge(msum, c.n)
                        for t in range(ETYPES):
                            pe.wait_ge(masked, ETYPES * c.n + t + 1)
                            pe.matmul(P_M[:, 0:CHUNK], msgW_sb[:, t, :], HM[ETYPES * c.slot(2) + t][:, :], start=(t == 0), stop=False).then_inc(msg_used, 1)
                        pe.wait_ge(hot, c.n + 1)
                        pe.matmul(P_M[:, 0:CHUNK], msgb_parts[:, :], HOT[c.slot(2)][:, :], start=False, stop=True).then_inc(msg, 1)

                    def gate_mm(c):
                        b = c.slot(8)
                        if c.has_before(1):
                            pe.wait_ge(r_ready, c.n)
                            pe.wait_ge(z_ready, c.n)
                            pe.wait_ge(nt, c.n)
                        pe.wait_ge(s.relu, c.n + 1)
                        for g, P in enumerate((P_R, P_Z)):
                            pe.matmul(P[:, 0:CHUNK], whh_T[:, g, :], s.H[b][:, 1, :], start=True, stop=False)
                        pe.matmul(P_NH[:, 0:CHUNK], whh_T[:, 2, :], s.H[b][:, 1, :], start=True, stop=True)
                        if c.has_before(1):
                            pe.wait_ge(nt2, c.n)
                        pe.wait_ge(msum, c.n + 1)
                        for g, P in enumerate((P_R, P_Z)):
                            pe.matmul(P[:, 0:CHUNK], wih_T[:, g, :], MS[c.slot(2)][:, :], start=False, stop=True)
                        pe.matmul(P_NI[:, 0:CHUNK], wih_T[:, 2, :], MS[c.slot(2)][:, :], start=True, stop=True).then_inc(gates, 1)

                    def tr_out(c):
                        pe.wait_ge(summed, c.n + 1)
                        if c.has_before(1):
                            pe.wait_ge(s.x_out, c.n)
                        for j in range(TILES):
                            i = pe.transpose(P_O[0:ROWS, j * F:(j + 1) * F], D3[c.slot(2)][:, j * ROWS:(j + 1) * ROWS], ident[:, :])
                        i.then_inc(tro, 1)

                    skewed(pe, EDGE_CHUNKS, U, [(10, tr_out), (7, gate_mm), (6, messages), (4, lambda c: edge_transposes(pe, s, c, (P_S, P_D)))])

                @block.scalar
                def _(act):
                    def sigmoids(c):
                        b = c.slot(2)
                        act.wait_ge(gates, c.n + 1)
                        if c.has_before(2):
                            act.wait_ge(nt, c.n - 1)
                            act.wait_ge(zdiff, c.n - 1)
                        act.activation(R[b][:, :], P_R[:, 0:CHUNK], ACT.Sigmoid, bias=bsum[:, 0:1]).then_inc(r_ready, 1)
                        act.activation(Z[b][:, :], P_Z[:, 0:CHUNK], ACT.Sigmoid, bias=bsum[:, 1:2]).then_inc(z_ready, 1)

                    def tanh(c):
                        b = c.slot(2)
                        act.wait_ge(nt2, c.n + 1)
                        if c.has_before(2):
                            act.wait_ge(summed, c.n - 1)
                            act.wait_ge(diff, c.n - 1)
                        act.activation(NN[b][:, :], NT2[b][:, :], ACT.Tanh, bias=bih[:, 2:3]).then_inc(nn, 1)

                    skewed(act, EDGE_CHUNKS, U, [(4, lambda c: edge_norm(act, s, c)), (7, sigmoids), (7, tanh),
                                                 (4, lambda c: edge_relu(act, s, c, (P_S, P_D), (diff, msg)))])

                @block.vector
                def _(dve):
                    def mask(c):
                        b = c.slot(2)
                        k = c.slot(4)
                        dve.wait_ge(type_landed[k], 16 * c.uses(4))
                        if c.has_before(2):
                            dve.wait_ge(msg, c.n - 1)
                        dve.tensor_scalar(HOT[b][:, :], TYPE[k][0:PARTS * ETYPES, :], type_id[:, 0:1], None, ALU.is_equal).then_inc(hot, 1)
                        dve.wait_ge(s.relu, c.n + 1)
                        for t in range(ETYPES):
                            if c.has_before(2):
                                dve.wait_ge(msg_used, ETYPES * (c.n - 2) + t + 1)
                            dve.scalar_tensor_tensor(HM[ETYPES * b + t][:, :], TYPE[k][:, :], float(t), s.H[c.slot(len(s.H))][:, 0, :],
                                                     ALU.is_equal, ALU.mult).then_inc(masked, 1)

                    def total(c):
                        b = c.slot(2)
                        first = c.known() and c.n == 0
                        dve.wait_ge(msg, c.n + 1)
                        dve.wait_ge(s.kc_landed[c.slot(4)], 16 * c.uses(4))
                        if not first:
                            dve.wait_ge(msum, c.n)
                        if c.has_before(2):
                            dve.wait_ge(gates, c.n - 1)
                        dve.tensor_tensor_scan(MS[b][:, :], s.KC[c.slot(4)][:, 0, :], P_M[:, 0:CHUNK], 0.0 if first else MS[1 - b][:, CHUNK - 1:CHUNK],
                                               ALU.mult, ALU.add).then_inc(msum, 1)

                    def candidate(c):
                        b = c.slot(2)
                        dve.wait_ge(gates, c.n + 1)
                        dve.wait_ge(r_ready, c.n + 1)
                        dve.scalar_tensor_tensor(NT[:, :], P_NH[:, 0:CHUNK], bhh[:, 2:3], R[b][:, :], ALU.add, ALU.mult).then_inc(nt, 1)
                        dve.wait_ge(nt, c.n + 1)
                        if c.has_before(2):
                            dve.wait_ge(nn, c.n - 1)
                        dve.tensor_tensor(NT2[b][:, :], P_NI[:, 0:CHUNK], NT[:, :], ALU.add).then_inc(nt2, 1)

                    def mix(c):
                        b = c.slot(2)
                        dve.wait_ge(zdiff, c.n + 1)
                        if c.has_before(2):
                            dve.wait_ge(tro, c.n - 1)
                        dve.tensor_tensor(D3[b][:, :], D2[b][:, :], NN[b][:, :], ALU.add).then_inc(summed, 1)

                    def add_rows(c):
                        b = c.slot(4)
                        dve.wait_ge(tro, c.n + 1)
                        dve.wait_ge(x1_landed[b], 16 * c.uses(4))
                        if c.has_before(4):
                            dve.wait_ge(s.scattered[b], 16 * TILES * (c.uses(4) - 1))
                        dve.tensor_tensor(s.OUT[b][:, :, :], P_O[0:ROWS, :].rearrange("p (j f) -> p j f", j=TILES),
                                          X1[b][:, :, :], ALU.add).then_inc(s.x_out, 1)

                    first_indices(dve, s, TILES)
                    skewed(dve, EDGE_CHUNKS, U, [(0, lambda c: next_index(dve, s, c, TILES)), (4, lambda c: edge_shift(dve, s, c)),
                                                 (2, lambda c: edge_stats(dve, s, c, TILES)), (10, lambda c: edge_ends(dve, s, c)),
                                                 (2, lambda c: edge_sums(dve, s, c)), (10, add_rows),
                                                 (2, lambda c: edge_square(dve, s, c)), (5, mask),
                                                 (2, lambda c: edge_variance(dve, s, c)), (7, candidate), (9, mix), (6, total)])


_INS = ['x', 'src', 'dst', 'edge_type_8', 'L0_gnn_W', 'L0_gnn_att_src', 'L0_gnn_att_dst', 'L0_gnn_bias',
        'L1_gnn_message_W', 'L1_gnn_message_b', 'L1_gnn_gru_w_ih', 'L1_gnn_gru_w_hh', 'L1_gnn_gru_b_ih', 'L1_gnn_gru_b_hh']


def kernel(**inputs):
    import numpy as _np
    import concourse.bacc as _bacc
    from concourse import mybir as _mybir
    from concourse.bass_utils import run_bass_kernel_spmd as _run

    nc = _bacc.Bacc("TRN2", target_bir_lowering=False, num_devices=1)
    arrays, args = {}, []
    for name in _INS:
        a = _np.ascontiguousarray(inputs[name])
        arrays[f"in_{name}"] = a
        args.append(nc.dram_tensor(f"in_{name}", a.shape, _mybir.dt.from_np(a.dtype), kind="ExternalInput").ap())
    args.append(nc.dram_tensor("out_0", inputs['x'].shape, _mybir.dt.float32, kind="ExternalOutput").ap())
    build(nc, *args)
    r = _run(nc, [arrays], core_ids=[0])
    return r.results[0]["out_0"]
```
